# Optimizing a Trainium2 kernel written in Bass

```python
import numpy as np
import jax
import jax.numpy as jnp

def _softmax(x, axis=-1):
    return jax.nn.softmax(x, axis=axis)

def _gelu(x):
    return jax.nn.gelu(x, approximate=True)

def _silu(x):
    return jax.nn.silu(x)

def _sigmoid(x):
    return jax.nn.sigmoid(x)

def _layernorm(x, axis=-1, eps=1e-05):
    m = jnp.mean(x, axis=axis, keepdims=True)
    v = jnp.var(x, axis=axis, keepdims=True)
    return (x - m) / jnp.sqrt(v + eps)

def _scatter_add(tgt, idx, src, axis=0):
    return tgt.at[idx].add(src)

def _segment_sum(src, seg, n):
    return jax.ops.segment_sum(src, seg, n)
kernel_name = 'mk_decoder_postln_d1_seqx_r8_ddc8bf'

def setup_inputs(seed: int=0):
    np.random.seed(seed)
    _w = jnp.asarray

    def _rec_inputs():
        import jax
        import jax.numpy as jnp
        _rk = jax.random.key(seed)
        x = -0.0002928 + 1 * jax.random.normal(jax.random.fold_in(_rk, 1), (4, 512, 128), jnp.float32)
        _lenS = 512 - jax.random.randint(jax.random.fold_in(_rk, 7), (4,), 0, max(1, 512 // 4) + 1, jnp.int32)
        _lenS2 = 77 - jax.random.randint(jax.random.fold_in(_rk, 8), (4,), 0, max(1, 77 // 4) + 1, jnp.int32)
        _ctx_1024P = jax.random.normal(jax.random.fold_in(_rk, 11), (4, 16, 128), jnp.float32)
        _ctx_1024c = jax.random.dirichlet(jax.random.fold_in(_rk, 511), 0.3 * jnp.ones((16,), jnp.float32), (4, 77))
        _ctx_1024t = jnp.einsum('bsk,bkd->bsd', _ctx_1024c, _ctx_1024P)
        _ctx_1024t = _ctx_1024t * jax.lax.rsqrt(jnp.mean(jnp.square(_ctx_1024t)) + 1e-12) * 0.953939
        ctx_1024 = -1.39393e-06 + 0.999914 * (_ctx_1024t + 0.3 * jax.random.normal(jax.random.fold_in(_rk, 611), (4, 77, 128), jnp.float32))
        return (x, ctx_1024)
    x, ctx_1024 = _rec_inputs()

    def _L0_attn_setup():
        import jax, jax.numpy as jnp
        import numpy as np
        import math
        B, S, DIM, HEADS = (2, 256, 128, 16)

        def _alibi_slopes(n_heads):

            def pow2_slopes(n):
                start = 2 ** (-2 ** (-(math.log2(n) - 3)))
                return [start * start ** i for i in range(n)]
            if math.log2(n_heads).is_integer():
                slopes = pow2_slopes(n_heads)
            else:
                closest = 2 ** math.floor(math.log2(n_heads))
                slopes = pow2_slopes(closest)
                slopes += pow2_slopes(2 * closest)[0::2][:n_heads - closest]
            return np.asarray(slopes, dtype=np.float32).reshape(n_heads, 1, 1)
        key = jax.random.key(seed)
        k1, k2, k3 = jax.random.split(key, 3)
        x = jax.random.normal(k1, (B, S, DIM), dtype=jnp.float32)
        W_qkv = jax.random.normal(k2, (3 * DIM, DIM), dtype=jnp.float32) * 0.02
        W_o = jax.random.normal(k3, (DIM, DIM), dtype=jnp.float32) * 0.02
        return {'x': x, 'W_qkv': W_qkv, 'W_o': W_o}
    _L0_attn_all = _L0_attn_setup()
    _L0_attn_in = {k: v for k, v in _L0_attn_all.items() if k in ('W_qkv', 'W_o')}
    del _L0_attn_all

    def _L0_xattn_setup():
        import jax, jax.numpy as jnp
        import numpy as np
        D_MODEL = 128
        NUM_HEADS = 16
        D_K = D_MODEL // NUM_HEADS

        def _split_heads(x, B):
            return x.reshape(B, -1, NUM_HEADS, D_K).transpose(0, 2, 1, 3)
        key = jax.random.key(seed)
        ks = jax.random.split(key, 11)
        B, S = (2, 256)
        s = 1.0 / np.sqrt(D_MODEL)
        inp = {'Q': jax.random.normal(ks[0], (B, S, D_MODEL), jnp.float32), 'K': jax.random.normal(ks[1], (B, S, D_MODEL), jnp.float32), 'V': jax.random.normal(ks[2], (B, S, D_MODEL), jnp.float32), 'Wq': jax.random.normal(ks[3], (D_MODEL, D_MODEL), jnp.float32) * s, 'bq': jnp.zeros((D_MODEL,), jnp.float32), 'Wk': jax.random.normal(ks[4], (D_MODEL, D_MODEL), jnp.float32) * s, 'bk': jnp.zeros((D_MODEL,), jnp.float32), 'Wv': jax.random.normal(ks[5], (D_MODEL, D_MODEL), jnp.float32) * s, 'bv': jnp.zeros((D_MODEL,), jnp.float32), 'Wo': jax.random.normal(ks[6], (D_MODEL, D_MODEL), jnp.float32) * s, 'bo': jnp.zeros((D_MODEL,), jnp.float32)}
        return inp
    _L0_xattn_all = _L0_xattn_setup()
    _L0_xattn_in = {k: v for k, v in _L0_xattn_all.items() if k in ('Wq', 'bq', 'Wk', 'bk', 'Wv', 'bv', 'Wo', 'bo')}
    del _L0_xattn_all

    def _L0_ffn_setup():
        import jax, jax.numpy as jnp
        import numpy as np
        E = 8
        TOP_K = 2
        B, S, D = (2, 512, 128)
        H = 512
        CAPACITY = 256

        def _moe(x, Wg, W1, b1, W2, b2):
            b, s, d = x.shape
            xf = x.reshape(b * s, d)
            logits = xf.astype(jnp.float32) @ Wg.astype(jnp.float32)
            probs = jax.nn.softmax(logits, axis=-1)
            vals, idx = jax.lax.top_k(probs, TOP_K)
            w = vals / (jnp.sum(vals, axis=-1, keepdims=True) + 1e-09)
            counts = jnp.zeros((E,), dtype=jnp.int32)
            combine = jnp.zeros((b * s, E), dtype=jnp.float32)
            for k in range(TOP_K):
                oh = jax.nn.one_hot(idx[:, k], E, dtype=jnp.int32)
                pos = jnp.cumsum(oh, axis=0) - 1 + counts[None, :]
                keep = (oh == 1) & (pos < CAPACITY)
                counts = counts + jnp.sum(keep.astype(jnp.int32), axis=0)
                combine = combine + w[:, k][:, None] * keep.astype(jnp.float32)
            out = jnp.zeros_like(xf)
            for e in range(E):
                h = jax.nn.gelu(xf @ W1[e] + b1[e])
                ye = h @ W2[e] + b2[e]
                out = out + combine[:, e][:, None].astype(xf.dtype) * ye
            return out.reshape(b, s, d)
        key = jax.random.key(seed)
        k0, k1, k2, k3 = jax.random.split(key, 4)
        return {'x': jax.random.normal(k0, (B, S, D), dtype=jnp.float32), 'Wg': jax.random.normal(k1, (D, E), dtype=jnp.float32) * 0.02, 'W1': jax.random.normal(k2, (E, D, H), dtype=jnp.float32) * 0.02, 'b1': jnp.zeros((E, H), dtype=jnp.float32), 'W2': jax.random.normal(k3, (E, H, D), dtype=jnp.float32) * 0.02, 'b2': jnp.zeros((E, D), dtype=jnp.float32)}
    _L0_ffn_all = _L0_ffn_setup()
    _L0_ffn_in = {k: v for k, v in _L0_ffn_all.items() if k in ('Wg', 'W1', 'b1', 'W2', 'b2')}
    del _L0_ffn_all
    return {'x': x, 'ctx_1024': ctx_1024, 'L0_attn_W_qkv': _L0_attn_in['W_qkv'], 'L0_attn_W_o': _L0_attn_in['W_o'], 'L0_xattn_Wq': _L0_xattn_in['Wq'], 'L0_xattn_bq': _L0_xattn_in['bq'], 'L0_xattn_Wk': _L0_xattn_in['Wk'], 'L0_xattn_bk': _L0_xattn_in['bk'], 'L0_xattn_Wv': _L0_xattn_in['Wv'], 'L0_xattn_bv': _L0_xattn_in['bv'], 'L0_xattn_Wo': _L0_xattn_in['Wo'], 'L0_xattn_bo': _L0_xattn_in['bo'], 'L0_ffn_Wg': _L0_ffn_in['Wg'], 'L0_ffn_W1': _L0_ffn_in['W1'], 'L0_ffn_b1': _L0_ffn_in['b1'], 'L0_ffn_W2': _L0_ffn_in['W2'], 'L0_ffn_b2': _L0_ffn_in['b2']}

def reference(x, ctx_1024, L0_attn_W_qkv, L0_attn_W_o, L0_xattn_Wq, L0_xattn_bq, L0_xattn_Wk, L0_xattn_bk, L0_xattn_Wv, L0_xattn_bv, L0_xattn_Wo, L0_xattn_bo, L0_ffn_Wg, L0_ffn_W1, L0_ffn_b1, L0_ffn_W2, L0_ffn_b2):
    import jax
    import jax.numpy as jnp

    def _L0_attn_ref(x, W_qkv, W_o):
        import jax, jax.numpy as jnp
        import numpy as np
        import math
        B, S, DIM, HEADS = (2, 256, 128, 16)

        def _alibi_slopes(n_heads):

            def pow2_slopes(n):
                start = 2 ** (-2 ** (-(math.log2(n) - 3)))
                return [start * start ** i for i in range(n)]
            if math.log2(n_heads).is_integer():
                slopes = pow2_slopes(n_heads)
            else:
                closest = 2 ** math.floor(math.log2(n_heads))
                slopes = pow2_slopes(closest)
                slopes += pow2_slopes(2 * closest)[0::2][:n_heads - closest]
            return np.asarray(slopes, dtype=np.float32).reshape(n_heads, 1, 1)
        b, s, d = x.shape
        h = HEADS
        hd = d // h
        scale = hd ** (-0.5)
        qkv = x @ W_qkv.T
        q, k, v = jnp.split(qkv, 3, axis=-1)
        q = q.reshape(b, s, h, hd).transpose(0, 2, 1, 3)
        k = k.reshape(b, s, h, hd).transpose(0, 2, 1, 3)
        v = v.reshape(b, s, h, hd).transpose(0, 2, 1, 3)
        scores = jnp.einsum('bhqd,bhkd->bhqk', q, k) * scale
        pos = jnp.arange(s)
        rel = (pos[None, :] - pos[:, None]).astype(scores.dtype)
        slopes = jnp.asarray(_alibi_slopes(h))
        scores = scores - slopes * rel
        causal_mask = pos[None, :] > pos[:, None]
        scores = jnp.where(causal_mask, jnp.finfo(scores.dtype).min, scores)
        weights = jax.nn.softmax(scores, axis=-1)
        out = jnp.einsum('bhqk,bhkd->bhqd', weights, v)
        out = out.transpose(0, 2, 1, 3).reshape(b, s, d)
        return out @ W_o.T

    def _L0_xattn_ref(Q, K, V, Wq, bq, Wk, bk, Wv, bv, Wo, bo):
        import jax, jax.numpy as jnp
        import numpy as np
        D_MODEL = 128
        NUM_HEADS = 16
        D_K = D_MODEL // NUM_HEADS

        def _split_heads(x, B):
            return x.reshape(B, -1, NUM_HEADS, D_K).transpose(0, 2, 1, 3)
        B, S, _ = Q.shape
        q = _split_heads(Q @ Wq.T + bq, B)
        k = _split_heads(K @ Wk.T + bk, B)
        v = _split_heads(V @ Wv.T + bv, B)
        scale = 1.0 / jnp.sqrt(jnp.asarray(D_K, q.dtype))
        scores = jnp.einsum('bhqd,bhkd->bhqk', q, k) * scale
        attn = jax.nn.softmax(scores, axis=-1)
        ctx = jnp.einsum('bhqk,bhkd->bhqd', attn, v)
        ctx = ctx.transpose(0, 2, 1, 3).reshape(B, S, D_MODEL)
        out = ctx @ Wo.T + bo
        return out

    def _L0_ffn_ref(x, Wg, W1, b1, W2, b2):
        import jax, jax.numpy as jnp
        import numpy as np
        E = 8
        TOP_K = 2
        B, S, D = (2, 512, 128)
        H = 512
        CAPACITY = 256

        def _moe(x, Wg, W1, b1, W2, b2):
            b, s, d = x.shape
            xf = x.reshape(b * s, d)
            logits = xf.astype(jnp.float32) @ Wg.astype(jnp.float32)
            probs = jax.nn.softmax(logits, axis=-1)
            vals, idx = jax.lax.top_k(probs, TOP_K)
            w = vals / (jnp.sum(vals, axis=-1, keepdims=True) + 1e-09)
            counts = jnp.zeros((E,), dtype=jnp.int32)
            combine = jnp.zeros((b * s, E), dtype=jnp.float32)
            for k in range(TOP_K):
                oh = jax.nn.one_hot(idx[:, k], E, dtype=jnp.int32)
                pos = jnp.cumsum(oh, axis=0) - 1 + counts[None, :]
                keep = (oh == 1) & (pos < CAPACITY)
                counts = counts + jnp.sum(keep.astype(jnp.int32), axis=0)
                combine = combine + w[:, k][:, None] * keep.astype(jnp.float32)
            out = jnp.zeros_like(xf)
            for e in range(E):
                h = jax.nn.gelu(xf @ W1[e] + b1[e])
                ye = h @ W2[e] + b2[e]
                out = out + combine[:, e][:, None].astype(xf.dtype) * ye
            return out.reshape(b, s, d)
        return _moe(x, Wg, W1, b1, W2, b2)
    x = _layernorm(x + _L0_attn_ref(x, L0_attn_W_qkv, L0_attn_W_o), axis=-1)
    x = _layernorm(x + _L0_xattn_ref(x, ctx_1024, ctx_1024, L0_xattn_Wq, L0_xattn_bq, L0_xattn_Wk, L0_xattn_bk, L0_xattn_Wv, L0_xattn_bv, L0_xattn_Wo, L0_xattn_bo), axis=-1)
    x = _layernorm(x + _L0_ffn_ref(x, L0_ffn_Wg, L0_ffn_W1, L0_ffn_b1, L0_ffn_W2, L0_ffn_b2), axis=-1)
    return x

_drawn_inputs = setup_inputs


def setup_inputs(seed=0):
    import zlib

    import numpy as np

    out = dict(_drawn_inputs(seed))
    spreads = {'L0_xattn_bq': (0.0, 0.301),
     'L0_xattn_bk': (0.0, 0.8),
     'L0_xattn_bv': (0.0, 0.1),
     'L0_xattn_bo': (0.0, 0.1),
     'L0_ffn_b1': (0.0, 0.64),
     'L0_ffn_b2': (0.0, 0.1)}
    factors = {'L0_attn_W_qkv': 3.269, 'L0_attn_W_o': 3.617}
    for name, (base, spread) in spreads.items():
        noise = np.random.default_rng([zlib.crc32(name.encode()), seed]).standard_normal(out[name].shape)
        drawn = base * np.exp(spread * noise) if base else spread * noise
        out[name] = jnp.asarray(drawn.astype(out[name].dtype))
    for name, factor in factors.items():
        out[name] = (out[name] * factor).astype(out[name].dtype)
    return out
```

```python
from contextlib import ExitStack
import math

import numpy as np

import concourse.bass as bass
from concourse import mybir

ALU = mybir.AluOpType
ACT = mybir.ActivationFunctionType
X_AXIS = mybir.AxisListType.X
F32 = mybir.dt.float32
BF16 = mybir.dt.bfloat16
U32 = mybir.dt.uint32

P = 128
B, S, D = 4, 512, 128
H, HD = 16, 8
C = 77
NT = S // P
G = 4
NG = H // G
E, HID, CAP = 8, 512, 256
NC = HID // P
SCALE = HD ** -0.5
EPS = 1e-5
MASKED = -1e30
DROPPED = 8192.0
ROW = D + 2

Q_PARTS = (0, 0, 0, 1, 1, 2)
K_PARTS = (0, 1, 2, 0, 1, 0)
NR = HD * len(Q_PARTS)
ALIBI_ROW = NR
MAX_ROW = 96
SCORE_ROWS = 96

UNITS = {"s": 10, "x": 4}
PAIRS = {"s": 5, "x": 2}

PHASES = [
    ([("s", g) for g in range(NG)],
     {4: ["s_ot", "s_oproj", "s_x1t", "s_xq"]}),
    ([("s", 0), ("s", 1), ("x", 0), ("s", 2), ("x", 1), ("s", 3), ("x", 2), ("x", 3)],
     {6: ["s_ot"], 7: ["s_oproj"],
      8: ["x_ot", "s_x1t", "x_oproj", "s_xq", "x_x2t", "x_logit", "x_count"]}),
    ([("x", g) for g in range(NG)],
     {4: ["x_ot", "x_oproj", "x_x2t", "x_logit", "x_count"]}),
]


class Plan:

    def __init__(self):
        self.at, self.total = [], []
        for groups, after in PHASES:
            at, n = {}, {"unit": 0, "pair": 0, "out": 0, "misc": 0}

            def put(buffer, name, count=1):
                at[buffer, name] = n[buffer]
                n[buffer] += count

            for j in range(-1, len(groups) + 1):
                if j + 1 < len(groups):
                    put("unit", groups[j + 1], UNITS[groups[j + 1][0]])
                if 0 <= j < len(groups):
                    put("pair", groups[j], PAIRS[groups[j][0]])
                if j >= 1:
                    put("out", groups[j - 1])
                if j >= 1:
                    put("misc", ("out",) + groups[j - 1])
                if j + 1 < len(groups):
                    put("misc", ("max",) + groups[j + 1])
                for name in after.get(j, []):
                    put("misc", name)
            self.at.append(at)
            self.total.append(n)

    def before(self, phase, b, buffer, name, more=0):
        n = [t[buffer] for t in self.total]
        here = self.at[phase][buffer, name] + more
        if phase == 0:
            return here
        if phase == 1:
            return b * n[1] + (n[0] - n[1] + here)
        return n[0] + (B - 1) * n[1] + here

    def half(self, phase, buffer, name, more=0):
        assert all(t[buffer] % 2 == 0 for t in self.total)
        return (self.at[phase][buffer, name] + more) % 2


def decoder(nc, a, out):
    plan = Plan()
    with ExitStack() as ctx:
        def sb(name, shape, dt=F32):
            return ctx.enter_context(nc.sbuf_tensor(name, shape, dt))

        def sem(name):
            return ctx.enter_context(nc.semaphore(name))

        def dram(name, shape, dt=F32):
            return nc.dram_tensor(name, shape, dt, kind="Internal").ap()

        q_d = dram("q_stack_d", (B, H, NR, S), BF16)
        k_d = dram("k_stack_d", (B, H, NR, S), BF16)
        v_d = dram("v_d", (B, P, NT * D))
        xq_d = dram("xq_stack_d", (H, NR, S), BF16)
        xk_d = dram("xk_stack_d", (H, NR, B * C), BF16)
        vx_d = dram("vx_d", (B, C, H * 32))
        x2_d = dram("x2_d", (B * S, D))
        slots_d = dram("slots_d", (E * CAP, ROW))
        y_d = dram("y_d", (2 * B * S, D))

        ident = sb("ident", [P, P])
        identb = sb("identb", [P, P], BF16)
        causal = sb("causal", [P, P], BF16)
        before_t = sb("before_t", [P, P], BF16)
        ones = sb("ones", [P, P], BF16)
        e_const = sb("e_const", [P, 3, NT, E])
        w_qkv = sb("w_qkv", [P, 3, D])
        w_o = sb("w_o", [P, D])
        wx = sb("wx", [P, 4, D])
        w_gate = sb("w_gate", [P, E])
        b_col = sb("b_col", [P, 2])
        bq_s = sb("bq_s", [P, 1])
        bv_row = sb("bv_row", [P, D])
        bo_row = sb("bo_row", [P, D])

        stack_q = {"s": sb("stack_q", [P, H, S], BF16), "x": sb("stack_xq", [P, H, S], BF16)}
        stack_k = {"s": sb("stack_k", [P, H, S], BF16), "x": sb("stack_xk", [P, H, P], BF16)}
        probs = {"s": sb("probs", [P, 2, 5, 2 * S]), "x": sb("probs_x", [P, 2, 2, 2 * S])}
        v_s = sb("v_s", [P, NT, H, 32])
        v_x = sb("v_x", [P, H, 32])
        v_tok = sb("v_tok", [P, NT, D])
        negmax = sb("negmax", [P, 2, G, NT])
        nm_parts = sb("nm_parts", [P, 2, 3, G * NT], BF16)
        nm_rows = sb("nm_rows", [3 * G * NT, 2, P], BF16)
        u_sb = sb("u_sb", [P, 2, S])
        rsum = sb("rsum", [P, 2, NT, G])
        o_tok = {k: sb(f"o_tok_{k}", [P, NT, D]) for k in "sx"}
        o_t = {k: sb(f"o_t_{k}", [P, S]) for k in "sx"}

        ctx_t = sb("ctx_t", [P, B * C])
        zeros = sb("zeros", [P, D])
        first_used = sb("first_used", [P, E])
        xq = sb("xq", [P, S])
        xq_parts = sb("xq_parts", [P, 3, S], BF16)

        early = probs["s"][:].rearrange("p a b c -> p (a b c)")
        x_t = early[:, 0:2048]
        qk = early[:, 2048:4096].rearrange("p (i w s) -> p i w s", i=2, w=2)
        qk_parts = early[:, 4096:7168].bitcast(BF16).rearrange("p (i c w s) -> p i c w s", i=2, c=3, w=2)
        v_stage = early[:, 7168:8192].rearrange("p (i n) -> p i n", i=2)
        xk = early[:, 8192:8192 + B * C]
        xk_parts = early[:, 8512:8512 + 3 * B * C // 2].bitcast(BF16).rearrange("p (c n) -> p c n", c=3)
        vx_all = probs["x"][0:C].rearrange("p a b c -> p (a b c)")[:, 0:B * H * 32].rearrange("p (b h n) -> p b h n", b=B, h=H)

        x_tok = sb("x_tok", [P, NT, D])
        r = {k: sb(f"r_{k}", [P, NT, D]) for k in "sx"}
        stats = {k: sb(f"stats_{k}", [P, NT, 6]) for k in "sx"}
        mv = {k: sb(f"mv_{k}", [P, NT, 2]) for k in "sx"}
        var_eps = {k: sb(f"var_eps_{k}", [P, NT]) for k in "sx"}
        rstd = {k: sb(f"rstd_{k}", [P, NT]) for k in "sx"}
        minus_half = sb("minus_half", [P, NT])
        x1 = sb("x1", [P, NT, D])
        x1_bias = sb("x1_bias", [P, NT, D])
        x1_t = sb("x1_t", [P, S])
        x2_t = sb("x2_t", [P, S])

        pay = sb("pay", [P, 2, NT, ROW])
        logit = sb("logit", [P, NT, E])
        prob = sb("prob", [P, NT, E])
        stat4 = sb("stat4", [P, 8, NT])
        pick = sb("pick", [P, NT, E])
        hot = sb("hot", [P, 2, NT, E])
        hotb = sb("hotb", [P, 2, NT, E], BF16)
        tile_base = sb("tile_base", [P, 2, NT + 1, E])
        pos = sb("pos", [P, 2, NT, E])
        used = sb("used", [P, 2, NT, E])
        slotf = sb("slotf", [P, 2, NT])
        slot = sb("slot", [P, 2, NT], U32)
        row_id = sb("row_id", [P, 2, NT])
        empty = sb("empty", [P, ROW])

        xs = sb("xs", [P, 2, 2, ROW])
        w1 = sb("w1", [P, 2, HID + NC])
        w2 = sb("w2", [P, 2, HID + D])
        yrow = sb("yrow", [P, 2, 2], U32)
        flat = probs["s"][:].rearrange("p a b c -> p (a b c)")
        h_t = flat[:, 0:2 * NC * CAP].rearrange("p (i c s) -> p i c s", i=2, c=NC)
        xs_t = flat[:, 2048:2560].rearrange("p (i s) -> p i s", i=2)
        yb = flat[:, 2560:3072].rearrange("p (i t d) -> p i t d", i=2, t=2)
        ys = flat[:, 3072:3584].rearrange("p (i t d) -> p i t d", i=2, t=2)
        fin = flat[:, 4096:10240].rearrange("p (b k t d) -> p b k t d", b=B, k=3, t=NT)

        p_unit = [ctx.enter_context(nc.psum_tensor(f"p_unit{i}", [P, S], F32)) for i in range(2)]
        p_pair = [ctx.enter_context(nc.psum_tensor(f"p_pair{i}", [P, 2 * S], F32)) for i in range(2)]
        p_out = ctx.enter_context(nc.psum_tensor("p_out", [P, S], F32))
        p_misc = ctx.enter_context(nc.psum_tensor("p_misc", [P, S], F32))

        consts_in = sem("consts_in")
        filled = sem("filled")
        xt_in = [sem(f"xt_in{b}") for b in range(B)]
        proj_filled = sem("proj_filled")
        proj_read = sem("proj_read")
        split_step = sem("split_step")
        parts_out = [sem(f"parts_out{b}") for b in range(B)]
        ctx_filled, ctx_read = sem("ctx_filled"), sem("ctx_read")
        ctx_split = sem("ctx_split")
        ctx_out = sem("ctx_out")
        stack_in = {k: [sem(f"stack_in_{k}{g}") for g in range(NG)] for k in "sx"}
        xkv_in = sem("xkv_in")
        tok_in = sem("tok_in")
        vtok_in = sem("vtok_in")
        v_put = sem("v_put")
        unit_filled, unit_read = sem("unit_filled"), sem("unit_read")
        pair_filled, pair_read = sem("pair_filled"), sem("pair_read")
        masked = sem("masked")
        pv_done = {k: sem(f"pv_done_{k}") for k in "sx"}
        out_read = sem("out_read")
        misc_filled, misc_read = sem("misc_filled"), sem("misc_read")
        nm_step = {k: sem(f"nm_step_{k}") for k in "sx"}
        max_in = {k: [sem(f"max_in_{k}{g}") for g in range(NG)] for k in "sx"}
        norm_step = {k: sem(f"norm_step_{k}") for k in "sx"}
        ln_step = {k: sem(f"ln_step_{k}") for k in "sx"}
        ln_pow = {k: sem(f"ln_pow_{k}") for k in "sx"}
        ln_done = {k: sem(f"ln_done_{k}") for k in "sx"}
        bias_added = sem("bias_added")
        xq_split = sem("xq_split")
        xq_out = sem("xq_out")
        route_step = sem("route_step")
        route_exp = sem("route_exp")
        pay_copied = sem("pay_copied")
        x2_out = sem("x2_out")
        sent = [sem("sent_first"), sem("sent_second")]
        slots_in = [sem(f"slots_in{i}") for i in range(2)]
        we_in = [sem(f"we_in{i}") for i in range(2)]
        xs_filled, xs_read = sem("xs_filled"), sem("xs_read")
        h_filled, h_done = sem("h_filled"), sem("h_done")
        y_filled, y_read = sem("y_filled"), sem("y_read")
        y_step = sem("y_step")
        y_sent = [sem(f"y_sent{i}") for i in range(2)]
        fin_in = [sem(f"fin_in{b}") for b in range(B)]
        fin_step, fin_pow = sem("fin_step"), sem("fin_pow")
        fin_ready, fin_out = sem("fin_ready"), sem("fin_out")
        held = sem("held")
        bq_ready = sem("bq_ready")
        pool_fill, stack_zero, zeros_set = sem("pool_fill"), sem("stack_zero"), sem("zeros_set")
        rows_in = sem("rows_in")

        block = ctx.enter_context(nc.Block())

        SPLITS = 4
        LN_STEPS = 3
        HOT_STEP = 16
        ROUTE_STEPS = 31
        MASKS = PAIRS["s"]
        ALL_FILLED = 10
        CONSTS = ((w_qkv[:], a["w_qkv_t"]), (wx[:], a["wx_t"]), (ctx_t[:], a["ctx_t"]), (b_col[:], a["b_col"]),
                  (bv_row[:], a["bv"].partition_broadcast(P)), (bo_row[:], a["bo"].partition_broadcast(P)),
                  (identb[:], a["c_identb"]), (causal[:], a["c_causal"]), (ident[:], a["c_ident"]),
                  (w_o[:], a["w_o_t"]), (w_gate[:], a["w_gate"]), (before_t[:], a["c_before"]),
                  (e_const[:], a["c_expert"]), (row_id[:], a["c_row"]), (empty[:], a["c_empty"].partition_broadcast(P)))

        def pair_parts(kind, u):
            if kind == "x":
                return [(2 * u + i, 0, i * S) for i in range(2)]
            if u < 2:
                return [(2 * u + i, 0, i * S) for i in range(2)]
            if u < 4:
                return [(2 * (u - 2) + i, t, i * S + at) for i in range(2) for t, at in ((3, 0), (1, P))]
            return [(i, 2, i * 2 * P) for i in range(4)]

        def prob_place(i, t):
            for u in range(PAIRS["s"]):
                for head, tile, at in pair_parts("s", u):
                    if (head, tile) == (i, t):
                        return u, at

        def hold(engine, sem, value):
            engine.wait_ge(sem, value)
            if not isinstance(value, int):
                engine.sem_inc(held, 1)

        def load_stacks(sp, g, b):
            for stack, src in ((stack_q["s"], q_d), (stack_k["s"], k_d)):
                sp.dma_start(stack[0:NR, G * g:G * g + G, :],
                             src[b, G * g:G * g + G].rearrange("h r s -> r h s")).then_inc(stack_in["s"][g], 16)

        def split(engine, E, src, parts, sem, base):
            E.tensor_copy(parts[0], src).then_inc(sem, 1)
            hold(engine, sem, base + 1)
            E.tensor_tensor(src, src, parts[0], ALU.subtract).then_inc(sem, 1)
            hold(engine, sem, base + 2)
            E.tensor_copy(parts[1], src).then_inc(sem, 1)
            hold(engine, sem, base + 3)
            E.tensor_tensor(parts[2], src, parts[1], ALU.subtract).then_inc(sem, 1)

        def phases(engine, body):
            body(0, 0, 0, None)
            with engine.Fori(1, B) as b:
                body(1, b, b, b - 1)
            body(2, None, None, B - 1)

        def steps(phase):
            groups, after = PHASES[phase]
            for j in range(-1, len(groups) + 1):
                yield (j, groups[j + 1] if j + 1 < len(groups) else None,
                       groups[j] if 0 <= j < len(groups) else None,
                       groups[j - 1] if j >= 1 else None, after.get(j, []))

        def side(phase, group):
            return PHASES[phase][0].index(group) % 2

        @block.sync
        def _(sp):
            for b in range(B):
                sp.dma_start(x_t[:, b * S:(b + 1) * S], a["x_t"][:, b * S:(b + 1) * S]).then_inc(xt_in[b], 16)
                if b == 0:
                    for dst, src in CONSTS:
                        sp.dma_start(dst, src).then_inc(consts_in, 16)
            for b in range(B):
                i = b % 2
                hold(sp, split_step, SPLITS * (b + 1))
                for n in range(6):
                    for which, parts, dst in ((0, Q_PARTS, q_d), (1, K_PARTS, k_d)):
                        sp.dma_start(dst[b, :, HD * n:HD * (n + 1), :],
                                     qk_parts[:, i, parts[n], which, :]).then_inc(parts_out[b], 16)
                hold(sp, proj_read, 3 * (b + 1))
                sp.dma_start(v_d[b], v_stage[:, i, :]).then_inc(parts_out[b], 16)
                if b == 0:
                    hold(sp, filled, ALL_FILLED)
                    sp.dma_start(stack_q["s"][ALIBI_ROW:ALIBI_ROW + 3], a["c_ones"]).then_inc(rows_in, 16)
                    sp.dma_start(stack_k["s"][ALIBI_ROW:ALIBI_ROW + 3], a["c_alibi"]).then_inc(rows_in, 16)
                    sp.dma_start(x_tok[:], a["x"][0:S, :].rearrange("(t p) d -> p t d", p=P)).then_inc(tok_in, 16)
                    hold(sp, parts_out[0], 16 * 13)
                    sp.dma_start(v_tok[:].rearrange("p t d -> p (t d)"), v_d[0]).then_inc(vtok_in, 16)
                    for g in range(NG):
                        load_stacks(sp, g, 0)
            hold(sp, ctx_split, SPLITS)
            for n in range(6):
                sp.dma_start(xk_d[:, HD * n:HD * (n + 1), :], xk_parts[:, K_PARTS[n], :]).then_inc(ctx_out, 16)
            hold(sp, ctx_read, 1 + B)
            sp.dma_start(vx_d.rearrange("b c n -> c b n"), vx_all.rearrange("c b h n -> c b (h n)")).then_inc(ctx_out, 16)
            hold(sp, ctx_out, 16 * 7)
            for b in range(1, B):
                hold(sp, parts_out[b], 16 * 13)

            def body(phase, it, b, bx):
                for j, grp_max, grp_exp, grp_out, after in steps(phase):
                    if grp_max:
                        kind, g = grp_max
                        hold(sp, misc_read, plan.before(phase, it, "misc", ("max", kind, g), 1))
                        sp.dma_start(stack_q[kind][MAX_ROW:MAX_ROW + 3, G * g:G * g + G, :].rearrange("c h (t q) -> c (h t) q", q=P),
                                     nm_rows[:, side(phase, grp_max), :]).then_inc(max_in[kind][g], 16)
                    if grp_exp and grp_exp[0] == "s":
                        g = grp_exp[1]
                        hold(sp, pair_read, plan.before(phase, it, "pair", grp_exp, PAIRS["s"]))
                        load_stacks(sp, g, (b + 1) % B)
                        if g == NG - 1:
                            hold(sp, v_put, NG * (b + 1))
                            sp.dma_start(v_tok[:].rearrange("p t d -> p (t d)"), v_d[(b + 1) % B]).then_inc(vtok_in, 16)
                    for name in after:
                        if name == "s_oproj":
                            hold(sp, misc_read, plan.before(phase, it, "misc", name, 1))
                            sp.dma_start(x_tok[:], a["x"][bass.ds(((b + 1) % B) * S, S), :].rearrange("(t p) d -> p t d", p=P)).then_inc(tok_in, 16)
                        if name == "s_xq":
                            hold(sp, xq_split, SPLITS * (b + 1))
                            for n in range(6):
                                sp.dma_start(xq_d[:, HD * n:HD * (n + 1), :], xq_parts[:, Q_PARTS[n], :]).then_inc(xq_out, 16)
                            if phase:
                                hold(sp, pair_read, plan.before(phase, it, "pair", ("x", NG - 1), PAIRS["x"]))
                                hold(sp, pv_done["x"], NG * b)
                            sp.dma_start(stack_k["x"][0:NR, :, 0:C],
                                         xk_d[:, :, bass.ds(b * C, C)].rearrange("h r c -> r h c")).then_inc(xkv_in, 16)
                            sp.dma_start(v_x[0:C].rearrange("c h n -> c (h n)"), vx_d[b]).then_inc(xkv_in, 16)
                            hold(sp, xq_out, 16 * 6 * (b + 1))
                            for g in range(NG):
                                sp.dma_start(stack_q["x"][0:NR, G * g:G * g + G, :],
                                             xq_d[G * g:G * g + G].rearrange("h r s -> r h s")).then_inc(stack_in["x"][g], 16)
                        if name == "x_oproj":
                            hold(sp, ln_done["x"], bx + 1)
                            sp.dma_start(x2_d[bass.ds(bx * S, S), :].rearrange("(t p) d -> p t d", p=P),
                                         pay[:, 0, :, 0:D]).then_inc(x2_out, 16)

            phases(sp, body)

            for e in range(E):
                i = e % 2
                if e >= 2:
                    hold(sp, y_step, 2 * (e - 1))
                sp.dma_start(w1[:, i, :], a["w1"][e]).then_inc(we_in[i], 16)
                sp.dma_start(w2[:, i, :], a["w2"][e]).then_inc(we_in[i], 16)
                if e == 0:
                    hold(sp, sent[0], 16 * (NT * B + 1))
                    hold(sp, sent[1], 16 * (NT * B + 1))
                sp.dma_start(xs[:, i, :, :], slots_d[e * CAP:(e + 1) * CAP, :].rearrange("(t p) c -> p t c", p=P)).then_inc(slots_in[i], 16)
            hold(sp, x2_out, 16 * B)
            for i in range(2):
                hold(sp, y_sent[i], 16 * E)
            for b in range(B):
                rows = lambda t, k: t[(k * B + b) * S:(k * B + b + 1) * S, :].rearrange("(t p) d -> p t d", p=P)
                sp.dma_start(fin[:, b, 0], rows(x2_d, 0)).then_inc(fin_in[b], 16)
                sp.dma_start(fin[:, b, 1], rows(y_d, 0)).then_inc(fin_in[b], 16)
                sp.dma_start(fin[:, b, 2], rows(y_d, 1)).then_inc(fin_in[b], 16)
            for b in range(B):
                hold(sp, fin_ready, b + 1)
                sp.dma_start(out[b * S:(b + 1) * S, :].rearrange("(t p) d -> p t d", p=P), fin[:, b, 1]).then_inc(fin_out, 16)
            hold(sp, fin_out, 16 * B)

        @block.tensor
        def _(pe):
            def mm(dst, lhs, rhs, start=True, stop=True):
                return nc.tensor.matmul(dst, lhs, rhs, start=start, stop=stop)

            pe.wait_ge(consts_in, 16 * len(CONSTS))
            for b in range(B):
                i = b % 2
                pe.wait_ge(xt_in[b], 16)
                xb = x_t[:, b * S:(b + 1) * S]
                if b >= 2:
                    pe.wait_ge(proj_read, 3 * (b - 1))
                mm(p_pair[i][:, 0:S], w_qkv[:, 0, :], xb)
                mm(p_pair[i][:, S:2 * S], w_qkv[:, 1, :], xb).then_inc(proj_filled, 1)
                for t in range(NT):
                    last = mm(p_unit[i][:, t * D:(t + 1) * D], xb[:, t * P:(t + 1) * P], w_qkv[:, 2, :])
                last.then_inc(proj_filled, 1)
            mm(p_misc[:, 0:B * C], wx[:, 1, :], ctx_t[:]).then_inc(ctx_filled, 1)
            for b in range(B):
                last = mm(p_out[0:C, b * D:(b + 1) * D], ctx_t[:, b * C:(b + 1) * C], wx[:, 2, :])
            last.then_inc(ctx_filled, 1)
            pe.wait_ge(proj_read, 3 * B)
            pe.wait_ge(ctx_read, 1 + B)
            pe.wait_ge(filled, ALL_FILLED)
            pe.wait_ge(rows_in, 32)
            for b in range(B):
                pe.wait_ge(parts_out[b], 16 * 13)
            pe.wait_ge(ctx_out, 16 * 7)

            def unit(phase, it, group, u):
                kind, g = group
                n = plan.before(phase, it, "unit", group, u)
                if not (phase == 0 and n < 2):
                    pe.wait_ge(unit_read, n - 1)
                bank = p_unit[plan.half(phase, "unit", group, u)]
                sq, sk = stack_q[kind], stack_k[kind]
                if kind == "x":
                    for i in range(G):
                        last = mm(bank[:, i * C:(i + 1) * C], sq[0:SCORE_ROWS, G * g + i, u * P:(u + 1) * P],
                                  sk[0:SCORE_ROWS, G * g + i, 0:C])
                else:
                    if u < 4:
                        parts = [(u, 3, 0)]
                    elif u < 8:
                        parts = [(u - 4, 2, 0), (u - 4, 0, 3 * P)]
                    else:
                        parts = [(2 * (u - 8), 1, 0), (2 * (u - 8) + 1, 1, 2 * P)]
                    for i, t, at in parts:
                        keys = (t + 1) * P
                        mm(bank[:, at:at + keys], sq[0:SCORE_ROWS, G * g + i, t * P:(t + 1) * P],
                           sk[0:SCORE_ROWS, G * g + i, 0:keys], stop=False)
                        last = mm(bank[:, at + t * P:at + keys], identb[:], causal[:], start=False)
                last.then_inc(unit_filled, 1)

            def pair(phase, it, group, u):
                kind, g = group
                n = plan.before(phase, it, "pair", group, u)
                if not (phase == 0 and n < 2):
                    pe.wait_ge(pair_read, n - 1)
                bank = p_pair[plan.half(phase, "pair", group, u)]
                sq, sk = stack_q[kind], stack_k[kind]
                for i, t, at in pair_parts(kind, u):
                    h = G * g + i
                    last = mm(bank[:, at:at + (S - t * P)], sk[:, h, t * P:(t + 1) * P], sq[:, h, t * P:S])
                last.then_inc(pair_filled, 1)

            def values(phase, it, kind, g, b, piece):
                pr = probs[kind][:, g % 2]
                if kind == "x":
                    for i in range(G):
                        last = mm(p_out[32 * i:32 * i + 32, :], v_x[:, G * g + i, :],
                                  pr[:, i // 2, (i % 2) * S:(i % 2 + 1) * S])
                    last.then_inc(pv_done[kind], 1)
                    return
                t = (0, 1, 3, 2)[piece]
                for i in range(G):
                    u, at = prob_place(i, t)
                    last = mm(p_out[32 * i:32 * i + 32, t * P:S], v_s[:, t, G * g + i, :],
                              pr[:, u, at:at + S - t * P], start=(piece == 0), stop=(piece == 3))
                if piece == 3:
                    last.then_inc(pv_done[kind], 1)

            def misc_free(phase, it, name):
                n = plan.before(phase, it, "misc", name)
                if not (phase == 0 and n == 0):
                    pe.wait_ge(misc_read, n)

            def body(phase, it, b, bx):
                batch = {"s": b, "x": bx}
                for j, grp_max, grp_exp, grp_out, after in steps(phase):
                    units = UNITS[grp_max[0]] if grp_max else 0
                    pairs = PAIRS[grp_exp[0]] if grp_exp else 0
                    pieces = (4 if grp_out[0] == "s" else 1) if grp_out else 0
                    if grp_max:
                        kind, g = grp_max
                        need = batch[kind] + 1
                        pe.wait_ge(stack_in[kind][g], (32 if kind == "s" else 16) * need)
                        if kind == "x":
                            pe.wait_ge(xkv_in, 32 * need)
                    if grp_exp:
                        pe.wait_ge(max_in[grp_exp[0]][grp_exp[1]], 16 * (batch[grp_exp[0]] + 1))
                    n = max(units, pairs, pieces)
                    done = [0, 0, 0]
                    for k in range(1, n + 1):
                        while done[1] < -(-pairs * k // n):
                            pair(phase, it, grp_exp, done[1])
                            done[1] += 1
                        while done[0] < -(-units * k // n):
                            unit(phase, it, grp_max, done[0])
                            done[0] += 1
                        while done[2] < -(-pieces * k // n):
                            kind, g = grp_out
                            if done[2] == 0:
                                if kind == "s":
                                    pe.wait_ge(masked, MASKS * (NG * b + g + 1))
                                    pe.wait_ge(v_put, NG * b + g + 1)
                                else:
                                    pe.wait_ge(pair_read, plan.before(phase, it, "pair", grp_out, PAIRS["x"]))
                                m = plan.before(phase, it, "out", grp_out)
                                if not (phase == 0 and m == 0):
                                    pe.wait_ge(out_read, m)
                            values(phase, it, kind, g, b, done[2])
                            done[2] += 1
                    if grp_out:
                        name = ("out",) + grp_out
                        misc_free(phase, it, name)
                        pe.wait_ge(out_read, plan.before(phase, it, "out", grp_out, 1))
                        for t in range(NT):
                            last = nc.tensor.transpose(p_misc[:, t * P:(t + 1) * P], u_sb[:, side(phase, grp_out), t * P:(t + 1) * P], ident[:])
                        last.then_inc(misc_filled, 1)
                    if grp_max:
                        kind, g = grp_max
                        name = ("max",) + grp_max
                        misc_free(phase, it, name)
                        hold(pe, nm_step[kind], SPLITS * (NG * batch[kind] + g + 1))
                        nc.tensor.transpose(p_misc[0:3 * G * NT, 0:P // 2].bitcast(BF16),
                                            nm_parts[:, side(phase, grp_max), :, :].rearrange("p c n -> p (c n)"),
                                            identb[:]).then_inc(misc_filled, 1)
                    for name in after:
                        misc_free(phase, it, name)
                        kind = name[0]
                        if name in ("s_ot", "x_ot"):
                            for t in range(NT):
                                last = nc.tensor.transpose(p_misc[:, t * P:(t + 1) * P], o_tok[kind][:, t, :], ident[:])
                        if name in ("s_oproj", "x_oproj"):
                            for t in range(NT):
                                last = mm(p_misc[:, t * D:(t + 1) * D], o_t[kind][:, t * P:(t + 1) * P],
                                          w_o[:] if kind == "s" else wx[:, 3, :])
                        if name == "s_x1t":
                            pe.wait_ge(ln_done["s"], b + 1)
                            for t in range(NT):
                                last = nc.tensor.transpose(p_misc[:, t * P:(t + 1) * P], x1[:, t, :], ident[:])
                        if name == "s_xq":
                            last = mm(p_misc[:], wx[:, 0, :], x1_t[:])
                        if name == "x_x2t":
                            pe.wait_ge(ln_done["x"], bx + 1)
                            for t in range(NT):
                                last = nc.tensor.transpose(p_misc[:, t * P:(t + 1) * P], pay[:, 0, t, 0:D], ident[:])
                        if name == "x_logit":
                            for t in range(NT):
                                last = mm(p_misc[:, t * E:(t + 1) * E], x2_t[:, t * P:(t + 1) * P], w_gate[:])
                        if name == "x_count":
                            pe.wait_ge(route_step, ROUTE_STEPS * bx + HOT_STEP)
                            chosen = hotb[:].rearrange("p k t e -> p (k t e)")
                            mm(p_misc[:, 0:2 * NT * E], before_t[:], chosen)
                            last = mm(p_misc[:, 2 * NT * E:4 * NT * E], ones[:], chosen)
                        last.then_inc(misc_filled, 1)

            phases(pe, body)

            def hidden(e):
                i = e % 2
                pe.wait_ge(slots_in[i], 16 * (e // 2 + 1))
                if e >= 2:
                    pe.wait_ge(xs_read, e - 1)
                for t in range(2):
                    last = nc.tensor.transpose(p_unit[i][:, t * P:(t + 1) * P], xs[:, i, t, 0:D], ident[:])
                last.then_inc(xs_filled, 1)
                pe.wait_ge(xs_read, e + 1)
                pe.wait_ge(we_in[i], 32 * (e // 2 + 1))
                if e >= 2:
                    pe.wait_ge(h_done, NC * (e - 1))
                for c in range(NC):
                    mm(p_pair[i][:, c * CAP:(c + 1) * CAP], w1[:, i, c * P:(c + 1) * P], xs_t[:, i, :]).then_inc(h_filled, 1)

            def result(e):
                i = e % 2
                bank = (p_out, p_misc)[i]
                pe.wait_ge(h_done, NC * (e + 1))
                if e >= 2:
                    pe.wait_ge(y_step, 2 * (e - 2) + 1)
                for t in range(2):
                    for c in range(NC):
                        last = mm(bank[:, t * D:(t + 1) * D], h_t[:, i, c, t * P:(t + 1) * P], w2[:, i, c * D:(c + 1) * D],
                                  start=(c == 0), stop=(c == NC - 1))
                last.then_inc(y_filled, 1)

            pe.wait_ge(misc_read, plan.before(2, None, "misc", "x_count", 1))
            hidden(0)
            for e in range(E):
                if e + 1 < E:
                    hidden(e + 1)
                result(e)

        @block.scalar
        def _(act):
            act.wait_ge(consts_in, 16 * len(CONSTS))
            nc.scalar.mul(bq_s[:], b_col[:, 0:1], SCALE).then_inc(bq_ready, 1)
            for b in range(B):
                i = b % 2
                act.wait_ge(proj_filled, 2 * b + 1)
                if b >= 2:
                    act.wait_ge(split_step, SPLITS * (b - 1))
                nc.scalar.mul(qk[:, i, 0, :], p_pair[i][:, 0:S], SCALE).then_inc(proj_read, 1)
                nc.scalar.copy(qk[:, i, 1, :], p_pair[i][:, S:2 * S]).then_inc(proj_read, 1)
                act.wait_ge(proj_filled, 2 * b + 2)
                if b >= 2:
                    act.wait_ge(parts_out[b - 2], 16 * 13)
                nc.scalar.copy(v_stage[:, i, :], p_unit[i][:]).then_inc(proj_read, 1)
            act.wait_ge(ctx_filled, 1)
            act.wait_ge(bq_ready, 1)
            nc.scalar.activation(xk, p_misc[:, 0:B * C], ACT.Identity, bias=b_col[:, 1:2]).then_inc(ctx_read, 1)

            def body(phase, it, b, bx):
                batch = {"s": b, "x": bx}
                for j, grp_max, grp_exp, grp_out, after in steps(phase):
                    if grp_exp:
                        kind, g = grp_exp
                        for u in range(PAIRS[kind]):
                            act.wait_ge(pair_filled, plan.before(phase, it, "pair", grp_exp, u + 1))
                            nc.scalar.activation(probs[kind][:, g % 2, u, :], p_pair[plan.half(phase, "pair", grp_exp, u)][:],
                                                 ACT.Exp).then_inc(pair_read, 1)
                    if grp_out:
                        kind, g = grp_out
                        act.wait_ge(pv_done[kind], NG * batch[kind] + g + 1)
                        nc.scalar.copy(u_sb[:, side(phase, grp_out), :], p_out[:]).then_inc(out_read, 1)
                    if grp_max:
                        act.wait_ge(misc_filled, plan.before(phase, it, "misc", ("max",) + grp_max, 1))
                        nc.scalar.copy(nm_rows[:, side(phase, grp_max), :],
                                       p_misc[0:3 * G * NT, 0:P // 2].bitcast(BF16)).then_inc(misc_read, 1)
                    for name in after:
                        src = p_misc[:]
                        if name in ("s_ot", "x_ot", "s_x1t", "x_x2t"):
                            dst = {"s_ot": o_t["s"], "x_ot": o_t["x"], "s_x1t": x1_t, "x_x2t": x2_t}[name]
                            act.wait_ge(misc_filled, plan.before(phase, it, "misc", name, 1))
                            nc.scalar.copy(dst[:], src).then_inc(misc_read, 1)
                        if name == "s_xq":
                            act.wait_ge(misc_filled, plan.before(phase, it, "misc", name, 1))
                            if phase:
                                act.wait_ge(xq_split, SPLITS * b)
                            nc.scalar.activation(xq[:], src, ACT.Identity, bias=bq_s[:], scale=SCALE).then_inc(misc_read, 1)
                        if name == "x_logit":
                            act.wait_ge(misc_read, plan.before(phase, it, "misc", name, 1))
                            nc.scalar.activation(prob[:], logit[:], ACT.Exp).then_inc(route_exp, 1)

            phases(act, body)

            for e in range(E):
                i = e % 2
                act.wait_ge(we_in[i], 32 * (e // 2 + 1))
                if e >= 2:
                    act.wait_ge(y_filled, e - 1)
                for c in range(NC):
                    act.wait_ge(h_filled, NC * e + 2 * (c // 2) + 2)
                    nc.scalar.activation(h_t[:, i, c, :], p_pair[i][:, c * CAP:(c + 1) * CAP], ACT.Gelu_apprx_tanh,
                                         bias=w1[:, i, HID + c:HID + c + 1]).then_inc(h_done, 1)

        @block.vector
        def _(dve):
            nc.vector.memset(zeros[:], 0.0).then_inc(zeros_set, 1)
            nc.vector.memset(stack_k["s"][:], 0.0).then_inc(stack_zero, 1)
            nc.vector.memset(stack_q["s"][:], 0.0).then_inc(filled, 1)
            dve.wait_ge(stack_zero, 1)
            nc.vector.memset(stack_k["s"][MAX_ROW:MAX_ROW + 3], 1.0).then_inc(filled, 1)
            nc.vector.memset(stack_k["x"][:], 0.0).then_inc(stack_zero, 1)
            dve.wait_ge(stack_zero, 2)
            nc.vector.memset(stack_k["x"][MAX_ROW:MAX_ROW + 3, :, 0:C], 1.0).then_inc(filled, 1)
            nc.vector.memset(ones[:], 1.0).then_inc(filled, 1)
            for b in range(B):
                i = b % 2
                dve.wait_ge(proj_read, 3 * b + 2)
                if b >= 2:
                    dve.wait_ge(parts_out[b - 2], 16 * 13)
                split(dve, nc.vector, qk[:, i], [qk_parts[:, i, c] for c in range(3)], split_step, SPLITS * b)
            dve.wait_ge(ctx_read, 1)
            split(dve, nc.vector, xk, [xk_parts[:, c, :] for c in range(3)], ctx_split, 0)
            dve.wait_ge(ctx_filled, 2)
            dve.wait_ge(filled, ALL_FILLED)
            for b in range(B):
                nc.vector.tensor_tensor(vx_all[:, b, :, 0:HD], p_out[0:C, b * D:(b + 1) * D].rearrange("c (h d) -> c h d", d=HD),
                                        bv_row[0:C].rearrange("c (h d) -> c h d", d=HD), ALU.add).then_inc(ctx_read, 1)

            def norm(kind, b, put):
                step, base = ln_step[kind], LN_STEPS * b
                for t in range(NT):
                    last = nc.vector.bn_stats(stats[kind][:, t, :], r[kind][:, t, :])
                last.then_inc(step, 1)
                hold(dve, step, base + 1)
                for t in range(NT):
                    last = nc.vector.bn_aggr(mv[kind][:, t, :], stats[kind][:, t, :])
                last.then_inc(step, 1)
                dve.wait_ge(step, base + 2)
                nc.vector.tensor_scalar(var_eps[kind][:], mv[kind][:, :, 1], EPS, None, ALU.add).then_inc(step, 1)
                dve.wait_ge(ln_pow[kind], b + 1)
                for t in range(NT):
                    last = nc.vector.tensor_scalar(put(t), r[kind][:, t, :], mv[kind][:, t, 0:1], rstd[kind][:, t:t + 1],
                                                   ALU.subtract, ALU.mult)
                last.then_inc(ln_done[kind], 1)

            def weigh(e):
                i = e % 2
                dve.wait_ge(y_filled, e + 1)
                if e >= 2:
                    dve.wait_ge(y_sent[i], 32 * (e // 2))
                nc.vector.tensor_copy(yrow[:, i, :], xs[:, i, :, D + 1])
                nc.vector.tensor_tensor(yb[:, i], (p_out, p_misc)[i][:, 0:2 * D].rearrange("p (t d) -> p t d", t=2),
                                        w2[:, i, HID:HID + D].unsqueeze(1).broadcast_to([P, 2, D]), ALU.add).then_inc(y_step, 1)
                dve.wait_ge(y_step, 2 * e + 1)
                for t in range(2):
                    last = nc.vector.tensor_scalar(ys[:, i, t, :], yb[:, i, t, :], xs[:, i, t, D:D + 1], None, ALU.mult)
                last.then_inc(y_step, 1)

            def route(phase, it, bx):
                k = [0]

                def step(ins):
                    k[0] += 1
                    ins.then_inc(route_step, 1)
                    dve.wait_ge(route_step, ROUTE_STEPS * bx + k[0])

                def per_token(t):
                    return t.unsqueeze(2).broadcast_to([P, NT, E])

                V = nc.vector
                dve.wait_ge(misc_filled, plan.before(phase, it, "misc", "x_logit", 1))
                lg = p_misc[:, 0:NT * E].rearrange("p (t e) -> p t e", e=E)
                step(V.tensor_reduce(stat4[:, 0, :], lg, X_AXIS, ALU.max, negate=True))
                V.tensor_tensor(logit[:], lg, per_token(stat4[:, 0, :]), ALU.add).then_inc(misc_read, 1)
                dve.wait_ge(route_exp, bx + 1)
                step(V.tensor_reduce(stat4[:, 1, :], prob[:], X_AXIS, ALU.add))
                step(V.reciprocal(stat4[:, 2, :], stat4[:, 1, :]))
                step(V.tensor_tensor(prob[:], prob[:], per_token(stat4[:, 2, :]), ALU.mult))
                for c in range(2):
                    step(V.tensor_reduce(stat4[:, 3 + c, :], prob[:], X_AXIS, ALU.max))
                    step(V.tensor_tensor(pick[:], prob[:], per_token(stat4[:, 3 + c, :]), ALU.is_equal))
                    step(V.tensor_tensor(pick[:], pick[:], e_const[:, 0], ALU.mult))
                    step(V.tensor_reduce(stat4[:, 5, :], pick[:], X_AXIS, ALU.max))
                    step(V.tensor_tensor(hot[:, c], pick[:], per_token(stat4[:, 5, :]), ALU.is_equal))
                    if c == 0:
                        step(V.scalar_tensor_tensor(prob[:], hot[:, 0], -2.0, prob[:], ALU.mult, ALU.add))
                step(V.tensor_copy(hotb[:], hot[:]))
                assert k[0] == HOT_STEP
                step(V.tensor_tensor(stat4[:, 6, :], stat4[:, 3, :], stat4[:, 4, :], ALU.add))
                step(V.tensor_scalar(stat4[:, 6, :], stat4[:, 6, :], 1e-9, None, ALU.add))
                step(V.reciprocal(stat4[:, 7, :], stat4[:, 6, :]))
                for c in range(2):
                    V.tensor_tensor(pay[:, c, :, D], stat4[:, 3 + c, :], stat4[:, 7, :], ALU.mult)
                    V.tensor_copy(pay[:, c, :, D + 1], row_id[:, c, :])
                dve.wait_ge(misc_filled, plan.before(phase, it, "misc", "x_count", 1))
                cum = p_misc[:, 0:2 * NT * E].rearrange("p (k t e) -> p k t e", k=2, t=NT)
                tot = p_misc[:, 2 * NT * E:4 * NT * E].rearrange("p (k t e) -> p k t e", k=2, t=NT)
                for t in range(NT):
                    step(V.tensor_tensor(tile_base[:, :, t + 1, :], tot[:, :, t, :], tile_base[:, :, t, :], ALU.add))
                V.tensor_tensor(pos[:], cum, tile_base[:, :, 0:NT, :], ALU.add).then_inc(misc_read, 1)
                step(V.tensor_scalar(first_used[:], tile_base[:, 0, NT, :], float(CAP), None, ALU.min))
                dve.wait_ge(misc_read, plan.before(phase, it, "misc", "x_count", 1))
                V.tensor_scalar(used[:, 0], pos[:, 0], float(CAP), DROPPED, ALU.is_ge, ALU.mult)
                step(V.tensor_tensor(used[:, 1], pos[:, 1], first_used[:].unsqueeze(1).broadcast_to([P, NT, E]), ALU.add))
                V.tensor_tensor(used[:, 0], used[:, 0], pos[:, 0], ALU.add)
                step(V.tensor_scalar(used[:, 1], used[:, 1], float(CAP), DROPPED, ALU.is_ge, ALU.mult))
                step(V.tensor_tensor(used[:, 1], used[:, 1], pos[:, 1], ALU.subtract))
                step(V.tensor_tensor(used[:], used[:], e_const[:, 1:3], ALU.add))
                step(V.tensor_tensor(used[:], used[:], hot[:], ALU.mult))
                step(V.tensor_reduce(slotf[:], used[:], X_AXIS, ALU.add))
                V.tensor_copy(tile_base[:, :, 0, :], tile_base[:, :, NT, :])
                V.tensor_scalar(row_id[:], row_id[:], float(S), None, ALU.add)
                step(V.tensor_copy(slot[:], slotf[:]))
                assert k[0] == ROUTE_STEPS, k[0]

            def body(phase, it, b, bx):
                batch = {"s": b, "x": bx}
                for j, grp_max, grp_exp, grp_out, after in steps(phase):
                    if grp_max:
                        kind, g = grp_max
                        nm = negmax[:, side(phase, grp_max)]
                        for u in range(UNITS[kind]):
                            dve.wait_ge(unit_filled, plan.before(phase, it, "unit", grp_max, u + 1))
                            bank = p_unit[plan.half(phase, "unit", grp_max, u)]
                            if kind == "x":
                                last = nc.vector.tensor_reduce(nm[:, :, u], bank[:, 0:G * C].rearrange("p (i c) -> p i c", c=C), X_AXIS, ALU.max, negate=True)
                            elif u < 4:
                                last = nc.vector.tensor_reduce(nm[:, u, 3:4], bank[:], X_AXIS, ALU.max, negate=True)
                            elif u < 8:
                                nc.vector.tensor_reduce(nm[:, u - 4, 2:3], bank[:, 0:3 * P], X_AXIS, ALU.max, negate=True)
                                last = nc.vector.tensor_reduce(nm[:, u - 4, 0:1], bank[:, 3 * P:], X_AXIS, ALU.max, negate=True)
                            else:
                                last = nc.vector.tensor_reduce(nm[:, 2 * (u - 8):2 * (u - 8) + 2, 1], bank[:].rearrange("p (i c) -> p i c", i=2), X_AXIS, ALU.max, negate=True)
                            last.then_inc(unit_read, 1)
                    if grp_out:
                        kind, g = grp_out
                        i = side(phase, grp_out)
                        dve.wait_ge(misc_filled, plan.before(phase, it, "misc", ("out",) + grp_out, 1))
                        u = p_misc[:].rearrange("p (t i n) -> p t i n", t=NT, i=G)
                        nc.vector.reciprocal(rsum[:, i], u[:, :, :, HD]).then_inc(norm_step[kind], 1)
                        dve.wait_ge(norm_step[kind], NG * batch[kind] + g + 1)
                        nc.vector.tensor_tensor(o_tok[kind][:, :, G * HD * g:G * HD * (g + 1)].rearrange("p t (i d) -> p t i d", i=G),
                                                u[:, :, :, 0:HD], rsum[:, i].unsqueeze(3).broadcast_to([P, NT, G, HD]),
                                                ALU.mult).then_inc(misc_read, 1)
                    for name in after:
                        if name in ("s_oproj", "x_oproj"):
                            kind = name[0]
                            dve.wait_ge(misc_filled, plan.before(phase, it, "misc", name, 1))
                            if kind == "s":
                                dve.wait_ge(tok_in, 16 * (b + 1))
                            else:
                                dve.wait_ge(bias_added, bx + 1)
                            nc.vector.tensor_tensor(r[kind][:].rearrange("p t d -> p (t d)"), p_misc[:],
                                                    (x_tok if kind == "s" else x1_bias)[:].rearrange("p t d -> p (t d)"),
                                                    ALU.add).then_inc(misc_read, 1)
                            dve.wait_ge(misc_read, plan.before(phase, it, "misc", name, 1))
                            if kind == "s":
                                norm("s", b, lambda t: x1[:, t, :])
                            else:
                                dve.wait_ge(sent[0], 16 * NT * bx + 16)
                                dve.wait_ge(sent[1], 16 * NT * bx + 16)
                                norm("x", bx, lambda t: pay[:, 0, t, 0:D])
                        if name == "x_count":
                            route(phase, it, bx)

            phases(dve, body)

            for e in range(E):
                i = e % 2
                dve.wait_ge(xs_filled, e + 1)
                nc.vector.tensor_copy(xs_t[:, i, :], p_unit[i][:, 0:CAP]).then_inc(xs_read, 1)
                if e >= 1:
                    weigh(e - 1)
            weigh(E - 1)

            for b in range(B):
                tokens, first, second = (fin[:, b, k] for k in range(3))
                base = 5 * b
                dve.wait_ge(fin_in[b], 48)
                nc.vector.tensor_tensor(first, first, second, ALU.add).then_inc(fin_step, 1)
                dve.wait_ge(fin_step, base + 1)
                nc.vector.tensor_tensor(tokens, tokens, first, ALU.add).then_inc(fin_step, 1)
                dve.wait_ge(fin_step, base + 2)
                for t in range(NT):
                    last = nc.vector.bn_stats(stats["s"][:, t, :], tokens[:, t, :])
                last.then_inc(fin_step, 1)
                dve.wait_ge(fin_step, base + 3)
                for t in range(NT):
                    last = nc.vector.bn_aggr(mv["s"][:, t, :], stats["s"][:, t, :])
                last.then_inc(fin_step, 1)
                dve.wait_ge(fin_step, base + 4)
                nc.vector.tensor_scalar(var_eps["s"][:], mv["s"][:, :, 1], EPS, None, ALU.add).then_inc(fin_step, 1)
                dve.wait_ge(fin_pow, b + 1)
                for t in range(NT):
                    last = nc.vector.tensor_scalar(first[:, t, :], tokens[:, t, :], mv["s"][:, t, 0:1], rstd["s"][:, t:t + 1],
                                                   ALU.subtract, ALU.mult)
                last.then_inc(fin_ready, 1)

        @block.gpsimd
        def _(pool):
            g_ = nc.gpsimd
            g_.memset(minus_half[:], -0.5).then_inc(filled, 1)
            g_.memset(tile_base[:], 0.0).then_inc(filled, 1)
            g_.memset(v_s[:], 0.0).then_inc(pool_fill, 1)
            g_.memset(v_x[:], 0.0).then_inc(filled, 1)
            g_.memset(vx_all, 0.0).then_inc(pool_fill, 1)
            g_.memset(stack_q["x"][:], 0.0).then_inc(filled, 1)
            hold(pool, pool_fill, 2)
            g_.memset(v_s[:, :, :, HD], 1.0).then_inc(filled, 1)
            g_.memset(vx_all[:, :, :, HD], 1.0).then_inc(filled, 1)
            hold(pool, consts_in, 16 * len(CONSTS))
            pool.dma_start(slots_d.rearrange("(t p) c -> p t c", p=P),
                         empty[:].unsqueeze(1).broadcast_to([P, E * CAP // P, ROW])).then_inc(sent[0], 16)
            hold(pool, zeros_set, 1)
            pool.dma_start(y_d.rearrange("(t p) c -> p t c", p=P),
                         zeros[:].unsqueeze(1).broadcast_to([P, 2 * B * S // P, D])).then_inc(sent[1], 16)

            def root(kind, n, ready, ready_at, done):
                hold(pool, ready, ready_at)
                g_.tensor_tensor(rstd[kind][:], var_eps[kind][:], minus_half[:], ALU.pow).then_inc(done, 1)

            def body(phase, it, b, bx):
                batch = {"s": b, "x": bx}
                for j, grp_max, grp_exp, grp_out, after in steps(phase):
                    if grp_exp and grp_exp[0] == "s":
                        g = grp_exp[1]
                        if g == 0:
                            hold(pool, vtok_in, 16 * (b + 1))
                        if phase:
                            hold(pool, pv_done["s"], NG * (b - 1) + g + 1)
                        for t in range(NT):
                            last = g_.tensor_copy(v_s[:, t, G * g:G * g + G, 0:HD],
                                                  v_tok[:, t, G * HD * g:G * HD * (g + 1)].rearrange("p (i d) -> p i d", i=G))
                        last.then_inc(v_put, 1)
                        for u in range(PAIRS["s"]):
                            hold(pool, pair_read, plan.before(phase, it, "pair", grp_exp, u + 1))
                            pr = probs["s"][:, g % 2, u, :]
                            if u < 2:
                                view, pattern = pr.rearrange("p (i n) -> p i n", i=2)[:, :, 0:P], [[0, 2], [1, P]]
                            elif u < 4:
                                view, pattern = pr.rearrange("p (i n) -> p i n", i=2)[:, :, 0:2 * P], [[0, 2], [0, 2], [1, P]]
                            else:
                                view, pattern = pr.rearrange("p (i n) -> p i n", i=4)[:, :, 0:P], [[0, 4], [1, P]]
                            g_.affine_select(out=view, in_=view, compare_op=ALU.is_ge, fill=0.0, base=0,
                                             pattern=pattern, channel_multiplier=-1).then_inc(masked, 1)
                    if grp_max:
                        kind, g = grp_max
                        i = side(phase, grp_max)
                        hold(pool, unit_read, plan.before(phase, it, "unit", grp_max, UNITS[kind]))
                        split(pool, g_, negmax[:, i].rearrange("p i t -> p (i t)"), [nm_parts[:, i, c, :] for c in range(3)],
                              nm_step[kind], SPLITS * (NG * batch[kind] + g))
                    for name in after:
                        if name == "s_oproj":
                            root("s", b, ln_step["s"], LN_STEPS * (b + 1), ln_pow["s"])
                        if name == "s_xq":
                            if phase:
                                hold(pool, misc_read, plan.before(phase, it, "misc", "x_oproj", 1))
                                hold(pool, xq_out, 16 * 6 * b)
                            hold(pool, ln_done["s"], b + 1)
                            g_.tensor_tensor(x1_bias[:], x1[:], bo_row[:].unsqueeze(1).broadcast_to([P, NT, D]), ALU.add).then_inc(bias_added, 1)
                            hold(pool, misc_read, plan.before(phase, it, "misc", name, 1))
                            split(pool, g_, xq[:], [xq_parts[:, c, :] for c in range(3)], xq_split, SPLITS * b)
                        if name == "x_oproj":
                            root("x", bx, ln_step["x"], LN_STEPS * (bx + 1), ln_pow["x"])
                            hold(pool, ln_done["x"], bx + 1)
                            g_.tensor_copy(pay[:, 1, :, 0:D], pay[:, 0, :, 0:D]).then_inc(pay_copied, 1)
                        if name == "x_count":
                            hold(pool, pay_copied, bx + 1)
                            hold(pool, route_step, ROUTE_STEPS * (bx + 1))
                            hold(pool, x2_out, 16 * (bx + 1))
                            for k in (1, 0):
                                hold(pool, sent[1 - k], 16 * NT * (bx + k - k) + (16 if k == 1 else 16 + 16 * NT))
                                for t in range(NT):
                                    g_.indirect_dma_start(slots_d, bass.IndirectOffsetOnAxis(ap=slot[:, k, t:t + 1], axis=0),
                                                          pay[:, k, t, :], None, bounds_check=E * CAP - 1,
                                                          oob_is_err=False).then_inc(sent[k], 16)

            phases(pool, body)

            for e in range(E):
                i = e % 2
                hold(pool, y_step, 2 * (e + 1))
                for t in range(2):
                    g_.indirect_dma_start(y_d, bass.IndirectOffsetOnAxis(ap=yrow[:, i, t:t + 1], axis=0),
                                          ys[:, i, t, :], None, bounds_check=2 * B * S - 1,
                                          oob_is_err=False).then_inc(y_sent[i], 16)
            for b in range(B):
                root("s", b, fin_step, 5 * (b + 1), fin_pow)


_OUT = "out"


def _constants():
    def bf16_bits(v):
        return (np.ascontiguousarray(v, np.float32).view(np.uint32) >> 16).astype(np.uint16)

    ident = np.eye(P, dtype=np.float32)
    row = np.arange(P)
    start = 2.0 ** (-2.0 ** (-(math.log2(H) - 3)))
    slopes = np.asarray([start * start ** i for i in range(H)], np.float32)
    alibi = -(slopes[:, None] * np.arange(S, dtype=np.float32)[None, :])
    parts = []
    rest = alibi
    for _ in range(3):
        parts.append(bf16_bits(rest))
        rest = rest - (parts[-1].astype(np.uint32) << 16).view(np.float32)
    expert = np.arange(E, dtype=np.float32)
    consts = np.stack([E - expert, expert * CAP, expert * CAP + CAP - 1])
    ids = (np.arange(2)[None, :, None] * B * S + np.arange(NT)[None, None, :] * P + row[:, None, None])
    empty = np.zeros((1, ROW), np.float32)
    empty[0, D + 1] = DROPPED
    return {
        "c_ident": ident, "c_identb": bf16_bits(ident),
        "c_causal": bf16_bits(np.where(row[None, :] > row[:, None], MASKED, 0.0)),
        "c_before": bf16_bits(row[:, None] < row[None, :]),
        "c_expert": np.broadcast_to(consts[None, :, None, :], (P, 3, NT, E)).astype(np.float32).copy(),
        "c_row": ids.astype(np.float32), "c_empty": empty,
        "c_alibi": np.stack(parts), "c_ones": bf16_bits(np.ones((3, H, S))),
    }


def kernel(**inputs):
    import concourse.bacc as _bacc
    from concourse.bass_utils import run_bass_kernel_spmd as _run

    x = {k: np.asarray(v) for k, v in inputs.items()}
    tokens = x["x"].reshape(B * S, D)
    arrays = {
        "x": tokens, "x_t": tokens.T, "ctx_t": x["ctx_1024"].reshape(B * C, D).T,
        "w_qkv_t": x["L0_attn_W_qkv"].reshape(3, D, D).transpose(2, 0, 1),
        "w_o_t": x["L0_attn_W_o"].T,
        "wx_t": np.stack([x[f"L0_xattn_W{n}"].T for n in "qkvo"], axis=1),
        "b_col": np.stack([x["L0_xattn_bq"], x["L0_xattn_bk"]], axis=1),
        "bv": x["L0_xattn_bv"].reshape(1, D), "bo": x["L0_xattn_bo"].reshape(1, D),
        "w_gate": x["L0_ffn_Wg"],
        "w1": np.concatenate([x["L0_ffn_W1"], x["L0_ffn_b1"].reshape(E, NC, P).transpose(0, 2, 1)], axis=2),
        "w2": np.concatenate([x["L0_ffn_W2"].reshape(E, NC, P, D).transpose(0, 2, 1, 3).reshape(E, P, HID),
                              np.broadcast_to(x["L0_ffn_b2"][:, None, :], (E, P, D))], axis=2),
    }
    arrays.update(_constants())
    arrays = {k: np.ascontiguousarray(v) for k, v in arrays.items()}
    nc = _bacc.Bacc("TRN2", target_bir_lowering=False, num_devices=1)
    aps = {k: nc.dram_tensor(f"in_{k}", v.shape, mybir.dt.from_np(v.dtype), kind="ExternalInput").ap() for k, v in arrays.items()}
    aps.update({k: ap.bitcast(BF16) for k, ap in aps.items() if arrays[k].dtype == np.uint16})
    out = nc.dram_tensor("out", (B * S, D), F32, kind="ExternalOutput").ap()
    decoder(nc, aps, out)
    r = _run(nc, [{f"in_{k}": v for k, v in arrays.items()}], core_ids=[0])
    return r.results[0]["out"].reshape(B, S, D)
```

```python
from contextlib import ExitStack
import math

import numpy as np

import concourse.bass as bass
from concourse import mybir

ALU = mybir.AluOpType
ACT = mybir.ActivationFunctionType
X_AXIS = mybir.AxisListType.X
F32 = mybir.dt.float32
BF16 = mybir.dt.bfloat16
U32 = mybir.dt.uint32

P = 128
B, S, D = 4, 512, 128
H, HD = 16, 8
C = 77
NT = S // P
G = 4
NG = H // G
E, HID, CAP = 8, 512, 256
NC = HID // P
SCALE = HD ** -0.5
EPS = 1e-5
MASKED = -1e30
DROPPED = 8192.0
ROW = D + 2

Q_PARTS = (0, 0, 0, 1, 1, 2)
K_PARTS = (0, 1, 2, 0, 1, 0)
NR = HD * len(Q_PARTS)
ALIBI_ROW = NR
MAX_ROW = 96
SCORE_ROWS = 96

UNITS = {"s": 10, "x": 4}
PAIRS = {"s": 5, "x": 2}
VALUES = {"s": 4, "x": 1}

def _s(g, b):
    return ("s", g, b)


def _x(g, b):
    return ("x", g, b)


def _residual(kind, b, *steps):
    return dict(zip(((kind + "_ot", b), (kind + "_oproj", b), ("root", kind, b), ("norm", kind, b)), steps))


OPENING = dict(
    steps=[(None, [_s(0, 0)]), (None, [_s(1, 0)]),
           (_s(0, 0), [_s(2, 0)]), (_s(1, 0), [_s(3, 0)]), (_s(2, 0), [_s(0, 1)]), (_s(3, 0), [_s(1, 1)]),
           (_s(0, 1), [_s(2, 1)]), (_s(1, 1), [_s(3, 1)]), (_s(2, 1), []), (_s(3, 1), [_x(0, 0), _x(1, 0)])],
    rest={
        **{("load_s", g, 1): (3 + g, 0.05) for g in range(NG)}, ("load_v", 1): (6, 0.1),
        ("clear", 0): (1, 0.95),
        ("q_proj", 2): (3, 0.4), ("k_proj", 2): (3, 0.5), ("v_proj", 2): (3, 0.6), ("qk_split", 2): (4, 0.5), ("qk_store", 2): (5, 0.3),
        ("q_proj", 3): (5, 0.4), ("k_proj", 3): (5, 0.5), ("v_proj", 3): (5, 0.6), ("qk_split", 3): (6, 0.5), ("qk_store", 3): (7, 0.3),
        **_residual("s", 0, (7, 0.5), (8, 0.1), (8, 0.3), (8, 0.5)),
        ("s_x1t", 0): (8, 0.9), ("s_xq", 0): (9, 0.1), ("xq_split", 0): (9, 0.15), ("xq_store", 0): (9, 0.6), ("load_x", 0): (9, 0.7),
        ("bias", 0): (9, 0.9), ("max",) + _x(0, 0): (9, 1.1),
    })
LOOP = dict(
    before=[_s(2, 1), _s(3, 1)],
    steps=[(_x(0, 0), [_x(2, 0), _x(3, 0)]), (_x(1, 0), [_s(0, 2)]), (_x(2, 0), [_s(1, 2)]), (_x(3, 0), [_s(2, 2)]),
           (_s(0, 2), [_s(3, 2)]), (_s(1, 2), []), (_s(2, 2), [_x(0, 1)]), (_s(3, 2), [_x(1, 1)])],
    rest={
        ("max",) + _x(1, 0): (0, 0.25),
        **{("load_s", g, 2): (0, 0.1) for g in range(NG)}, ("load_v", 2): (0, 0.12),
        **_residual("s", 1, (1, 0.5), (2, 0.1), (2, 0.3), (2, 0.5)),
        ("s_x1t", 1): (2, 0.95), ("s_xq", 1): (3, 0.3), ("xq_split", 1): (3, 0.4), ("xq_store", 1): (3, 0.9), ("load_x", 1): (5, 0.3),
        **_residual("x", 0, (5, 0.5), (6, 0.1), (6, 0.3), (6, 0.45)),
        ("pay", 0): (6, 0.5), ("bias", 1): (6, 0.55), ("x_x2t", 0): (6, 0.8),
        ("x_logit", 0): (7, 0.1), ("gate_exp", 0): (7, 0.2), ("pick", 0): (7, 0.4), ("x_count", 0): (7, 0.85), ("send", 0): (7, 1.1),
    })
CLOSING = dict(
    before=[_s(2, 1), _s(3, 1)],
    steps=[(_x(0, 0), [_x(2, 0), _x(3, 0)]), (_x(1, 0), []), (_x(2, 0), []), (_x(3, 0), []), (None, []),
           (None, [_x(0, 1), _x(1, 1)]), (_x(0, 1), [_x(2, 1)]), (_x(1, 1), [_x(3, 1)]), (_x(2, 1), []), (_x(3, 1), []),
           (None, []), (None, [])],
    rest={
        ("max",) + _x(1, 0): (0, 0.25),
        **_residual("s", 1, (1, 0.5), (2, 0.1), (2, 0.3), (2, 0.5)),
        ("s_x1t", 1): (3, 0.2), ("s_xq", 1): (3, 0.3), ("xq_split", 1): (3, 0.4), ("xq_store", 1): (4, 0.5), ("load_x", 1): (4, 0.9),
        **_residual("x", 0, (5, 0.2), (5, 0.25), (5, 0.3), (5, 0.35)),
        ("pay", 0): (5, 0.4), ("bias", 1): (5, 0.4), ("max",) + _x(0, 1): (5, 1.1),
        ("x_x2t", 0): (6, 0.8),
        ("x_logit", 0): (7, 0.4), ("gate_exp", 0): (7, 0.5), ("pick", 0): (7, 0.6), ("x_count", 0): (8, 0.5), ("send", 0): (8, 0.9),
        **_residual("x", 1, (11, 0.2), (11, 0.25), (11, 0.3), (11, 0.35)),
        ("pay", 1): (11, 0.4), ("x_x2t", 1): (11, 0.4),
        ("x_logit", 1): (11, 0.5), ("gate_exp", 1): (11, 0.6), ("pick", 1): (11, 0.7), ("x_count", 1): (11, 0.8), ("send", 1): (11, 0.9),
    })
PHASES = (OPENING, LOOP, CLOSING)
MISC = ("out", "max", "q_proj", "k_proj", "v_proj", "s_ot", "s_oproj", "s_x1t", "s_xq",
        "x_ot", "x_oproj", "x_x2t", "x_logit", "x_count")


def _events(phase):
    steps, rest, before = phase["steps"], phase["rest"], phase.get("before", [None, None])
    exps = before + [exp for exp, _ in steps]
    events = []
    for j, (exp, maxes) in enumerate(steps):
        items = [(place, 3, what) for what, (step, place) in rest.items() if step == j]
        last, older = exps[j + 1], exps[j]
        if exp:
            n = PAIRS[exp[0]]
            items += [(u / n if j or phase is OPENING else 0.9 + u / n / 100, 0, ("pair", exp, u)) for u in range(n)]
        units = [("unit", group, u) for group in maxes for u in range(UNITS[group[0]])]
        items += [((k + 1) / len(units), 1, unit) for k, unit in enumerate(units)]
        items += [(1.01, 1, ("split",) + group) for group in maxes]
        if last:
            pieces = VALUES[last[0]]
            items += [((p + 0.6) / pieces, 2, ("values", last, p)) for p in range(pieces)]
            items.append((1.02, 2, ("take",) + last))
        if older:
            items.append((0.12, 2, ("out",) + older))
        if j:
            items += [(0.25, 2, ("max",) + group) for group in steps[j - 1][1] if ("max",) + group not in rest]
        events += [what for _, _, what in sorted(items, key=lambda i: i[:2])]
    return events


EVENTS = [_events(phase) for phase in PHASES]


class Plan:

    def __init__(self):
        self.at, self.total = [], []
        for events in EVENTS:
            at, n = {}, {"unit": 0, "pair": 0, "misc": 0, "values": 0, "turn": 0}
            for what in events:
                buffer = "misc" if what[0] in MISC else what[0]
                if buffer in n and not (buffer == "values" and what[2]):
                    at[what] = n[buffer]
                    n[buffer] += 1
                if what[0] == "out":
                    at["turn", what] = n["turn"]
                    n["turn"] += 1
            self.at.append(at)
            self.total.append(n)

    def before(self, phase, it, what, more=0):
        buffer = "misc" if what[0] in MISC else what[0]
        n = [t[buffer] for t in self.total]
        here = self.at[phase][what] + more
        return (here, it * n[1] + (n[0] + here) if phase == 1 else None, n[0] + (B - 2) * n[1] + here)[phase]

    def turn(self, phase, it, what):
        return self.before(phase, it, ("turn", what))

    def half(self, phase, what):
        assert all(t[what[0]] % 2 == 0 for t in self.total)
        return self.at[phase][what] % 2

    def batch(self, phase, it, b):
        return (b, it + b if phase == 1 else None, B - 2 + b)[phase]


def decoder(nc, a, out):
    plan = Plan()
    with ExitStack() as ctx:
        def sb(name, shape, dt=F32):
            return ctx.enter_context(nc.sbuf_tensor(name, shape, dt))

        def sem(name):
            return ctx.enter_context(nc.semaphore(name))

        def dram(name, shape, dt=F32):
            return nc.dram_tensor(name, shape, dt, kind="Internal").ap()

        q_d = dram("q_stack_d", (B, H, NR, S), BF16)
        k_d = dram("k_stack_d", (B, H, NR, S), BF16)
        v_d = dram("v_d", (B, P, NT * D))
        xq_d = dram("xq_stack_d", (H, NR, S), BF16)
        xk_d = dram("xk_stack_d", (H, NR, B * C), BF16)
        vx_d = dram("vx_d", (B, C, H * 32))
        x2_d = dram("x2_d", (B * S, D))
        slots_d = dram("slots_d", (E * CAP, ROW))
        y_d = dram("y_d", (2 * B * S, D))

        ident = sb("ident", [P, P])
        identb = sb("identb", [P, P], BF16)
        causal = sb("causal", [P, P], BF16)
        before_t = sb("before_t", [P, P], BF16)
        ones = sb("ones", [P, P], BF16)
        e_const = sb("e_const", [P, 3, NT, E])
        w_qkv = sb("w_qkv", [P, 3, D])
        w_o = sb("w_o", [P, D])
        wx = sb("wx", [P, 4, D])
        w_gate = sb("w_gate", [P, E])
        b_col = sb("b_col", [P, 2])
        bq_s = sb("bq_s", [P, 1])
        bv_row = sb("bv_row", [P, D])
        bo_row = sb("bo_row", [P, D])

        stack_q = {"s": sb("stack_q", [P, H, S], BF16), "x": sb("stack_xq", [P, H, S], BF16)}
        stack_k = {"s": sb("stack_k", [P, H, S], BF16), "x": sb("stack_xk", [P, H, P], BF16)}
        probs = {"s": sb("probs", [P, 2, 5, 2 * S]), "x": sb("probs_x", [P, 2, 2, 2 * S])}
        v_s = sb("v_s", [P, NT, H, 32])
        v_x = sb("v_x", [P, H, 32])
        v_tok = sb("v_tok", [P, NT, D])
        negmax = sb("negmax", [P, NG, G, NT])
        nm_parts = sb("nm_parts", [P, NG, 3, G * NT], BF16)
        nm_rows = sb("nm_rows", [3 * G * NT, NG, P], BF16)
        u_sb = sb("u_sb", [P, 2, S])
        rsum = sb("rsum", [P, 2, NT, G])
        o_tok = {k: sb(f"o_tok_{k}", [P, NT, D]) for k in "sx"}
        o_t = {k: sb(f"o_t_{k}", [P, S]) for k in "sx"}

        ctx_t = sb("ctx_t", [P, B * C])
        zeros = sb("zeros", [P, D])
        first_used = sb("first_used", [P, E])
        xq = sb("xq", [P, S])
        xq_parts = sb("xq_parts", [P, 3, S], BF16)

        qk = sb("qk", [P, 2, S])
        qk_parts = sb("qk_parts", [P, 3, 2, S], BF16)
        v_stage = sb("v_stage", [P, NT * D])

        early = probs["s"][:, 1].rearrange("p b c -> p (b c)")
        qk_first = early[:, 0:1024].rearrange("p (w s) -> p w s", w=2)
        parts_first = early[:, 1024:2560].bitcast(BF16).rearrange("p (c w s) -> p c w s", c=3, w=2)
        xk = early[:, 2560:2560 + B * C]
        xk_parts = early[:, 3072:3072 + 3 * B * C // 2].bitcast(BF16).rearrange("p (c n) -> p c n", c=3)
        early_x = probs["x"][:].rearrange("p a b c -> p (a b c)")
        x_t = early_x[:, 0:B * S]
        vx_all = early_x[0:C, B * S:B * S + B * H * 32].rearrange("p (b h n) -> p b h n", b=B, h=H)

        x_tok = sb("x_tok", [P, NT, D])
        r = {k: sb(f"r_{k}", [P, NT, D]) for k in "sx"}
        stats = {k: sb(f"stats_{k}", [P, NT, 6]) for k in "sx"}
        mv = {k: sb(f"mv_{k}", [P, NT, 2]) for k in "sx"}
        var_eps = {k: sb(f"var_eps_{k}", [P, NT]) for k in "sx"}
        rstd = {k: sb(f"rstd_{k}", [P, NT]) for k in "sx"}
        minus_half = sb("minus_half", [P, NT])
        x1 = sb("x1", [P, NT, D])
        x1_bias = sb("x1_bias", [P, NT, D])
        x1_t = sb("x1_t", [P, S])
        x2_t = sb("x2_t", [P, S])

        pay = sb("pay", [P, 2, NT, ROW])
        logit = sb("logit", [P, NT, E])
        prob = sb("prob", [P, NT, E])
        stat4 = sb("stat4", [P, 8, NT])
        pick = sb("pick", [P, NT, E])
        hot = sb("hot", [P, 2, NT, E])
        hotb = sb("hotb", [P, 2, NT, E], BF16)
        tile_base = sb("tile_base", [P, 2, NT + 1, E])
        pos = sb("pos", [P, 2, NT, E])
        used = sb("used", [P, 2, NT, E])
        slotf = sb("slotf", [P, 2, NT])
        slot = sb("slot", [P, 2, NT], U32)
        row_id = sb("row_id", [P, 2, NT])
        empty = sb("empty", [P, ROW])

        xs = sb("xs", [P, 2, 2, ROW])
        w1 = sb("w1", [P, 2, HID + NC])
        w2 = sb("w2", [P, 2, HID + D])
        yrow = sb("yrow", [P, 2, 2], U32)
        flat = probs["s"][:].rearrange("p a b c -> p (a b c)")
        h_t = flat[:, 0:2 * NC * CAP].rearrange("p (i c s) -> p i c s", i=2, c=NC)
        xs_t = flat[:, 2048:2560].rearrange("p (i s) -> p i s", i=2)
        yb = flat[:, 2560:3072].rearrange("p (i t d) -> p i t d", i=2, t=2)
        ys = flat[:, 3072:3584].rearrange("p (i t d) -> p i t d", i=2, t=2)
        fin = flat[:, 4096:10240].rearrange("p (b k t d) -> p b k t d", b=B, k=3, t=NT)

        p_unit = [ctx.enter_context(nc.psum_tensor(f"p_unit{i}", [P, S], F32)) for i in range(2)]
        p_pair = [ctx.enter_context(nc.psum_tensor(f"p_pair{i}", [P, 2 * S], F32)) for i in range(2)]
        p_out = ctx.enter_context(nc.psum_tensor("p_out", [P, S], F32))
        p_misc = ctx.enter_context(nc.psum_tensor("p_misc", [P, S], F32))

        consts_in = sem("consts_in")
        filled = sem("filled")
        xt_in = [sem(f"xt_in{b}") for b in range(B)]
        w_in = sem("w_in")
        proj_filled = sem("proj_filled")
        q_read, k_read, v_read = sem("q_read"), sem("k_read"), sem("v_read")
        first_split = sem("first_split")
        high_done = sem("high_done")
        qk_split = sem("qk_split")
        parts_out = [sem(f"parts_out{b}") for b in range(B)]
        ctx_filled, ctx_read = sem("ctx_filled"), sem("ctx_read")
        ctx_split = sem("ctx_split")
        ctx_out = sem("ctx_out")
        stack_in = {k: [sem(f"stack_in_{k}{g}") for g in range(NG)] for k in "sx"}
        xkv_in = sem("xkv_in")
        tok_in = sem("tok_in")
        vtok_in = sem("vtok_in")
        v_put = sem("v_put")
        unit_filled, unit_read = sem("unit_filled"), sem("unit_read")
        pair_filled, pair_read = sem("pair_filled"), sem("pair_read")
        masked = sem("masked")
        pv_done = {k: sem(f"pv_done_{k}") for k in "sx"}
        out_read = sem("out_read")
        misc_filled, misc_read = sem("misc_filled"), sem("misc_read")
        nm_step = {k: sem(f"nm_step_{k}") for k in "sx"}
        max_in = {k: [sem(f"max_in_{k}{g}") for g in range(NG)] for k in "sx"}
        norm_step = {k: sem(f"norm_step_{k}") for k in "sx"}
        ln_step = {k: sem(f"ln_step_{k}") for k in "sx"}
        ln_pow = {k: sem(f"ln_pow_{k}") for k in "sx"}
        ln_done = {k: sem(f"ln_done_{k}") for k in "sx"}
        bias_added = sem("bias_added")
        xq_split = sem("xq_split")
        xq_out = sem("xq_out")
        route_step = sem("route_step")
        route_exp = sem("route_exp")
        pay_copied = sem("pay_copied")
        x2_out = sem("x2_out")
        sent = [sem("sent_first"), sem("sent_second")]
        slots_in = [sem(f"slots_in{i}") for i in range(2)]
        we_in = [sem(f"we_in{i}") for i in range(2)]
        xs_filled, xs_read = sem("xs_filled"), sem("xs_read")
        h_filled, h_done = sem("h_filled"), sem("h_done")
        y_filled, y_read = sem("y_filled"), sem("y_read")
        y_step = sem("y_step")
        y_sent = [sem(f"y_sent{i}") for i in range(2)]
        fin_in = [sem(f"fin_in{b}") for b in range(B)]
        fin_step, fin_pow = sem("fin_step"), sem("fin_pow")
        fin_ready, fin_out = sem("fin_ready"), sem("fin_out")
        held = sem("held")
        bq_ready = sem("bq_ready")
        pool_fill, stack_zero, zeros_set = sem("pool_fill"), sem("stack_zero"), sem("zeros_set")
        vx_ready, x_ready, small_ready = sem("vx_ready"), sem("x_ready"), sem("small_ready")
        rows_in = sem("rows_in")

        block = ctx.enter_context(nc.Block())

        SPLITS = 4
        LN_STEPS = 3
        HOT_STEP = 16
        PICK_STEP = 19
        ROUTE_STEPS = 31
        MASKS = PAIRS["s"]
        ALL_FILLED = 3
        CONSTS = ((wx[:], a["wx_t"]), (ctx_t[:], a["ctx_t"]), (b_col[:], a["b_col"]),
                  (bv_row[:], a["bv"].partition_broadcast(P)), (bo_row[:], a["bo"].partition_broadcast(P)),
                  (identb[:], a["c_identb"]), (causal[:], a["c_causal"]), (ident[:], a["c_ident"]),
                  (w_o[:], a["w_o_t"]), (w_gate[:], a["w_gate"]), (before_t[:], a["c_before"]),
                  (e_const[:], a["c_expert"]), (row_id[:], a["c_row"]), (empty[:], a["c_empty"].partition_broadcast(P)))

        def pair_parts(kind, u):
            if kind == "x":
                return [(2 * u + i, 0, i * S) for i in range(2)]
            if u < 2:
                return [(2 * u + i, 0, i * S) for i in range(2)]
            if u < 4:
                return [(2 * (u - 2) + i, t, i * S + at) for i in range(2) for t, at in ((3, 0), (1, P))]
            return [(i, 2, i * 2 * P) for i in range(4)]

        def prob_place(i, t):
            for u in range(PAIRS["s"]):
                for head, tile, at in pair_parts("s", u):
                    if (head, tile) == (i, t):
                        return u, at

        def hold(engine, sem, value):
            engine.wait_ge(sem, value)
            if not isinstance(value, int):
                engine.sem_inc(held, 1)

        def load_stacks(sp, g, b):
            for stack, src in ((stack_q["s"], q_d), (stack_k["s"], k_d)):
                sp.dma_start(stack[0:NR, G * g:G * g + G, :],
                             src[b, G * g:G * g + G].rearrange("h r s -> r h s")).then_inc(stack_in["s"][g], 16)

        def store_parts(sp, b, parts, order):
            for which in order:
                for n in range(6):
                    sp.dma_start((q_d, k_d)[which][b, :, HD * n:HD * (n + 1), :],
                                 parts[:, (Q_PARTS, K_PARTS)[which][n], which, :]).then_inc(parts_out[b], 16)

        def split(engine, E, src, parts, sem, base):
            E.tensor_copy(parts[0], src).then_inc(sem, 1)
            hold(engine, sem, base + 1)
            E.tensor_tensor(src, src, parts[0], ALU.subtract).then_inc(sem, 1)
            hold(engine, sem, base + 2)
            E.tensor_copy(parts[1], src).then_inc(sem, 1)
            hold(engine, sem, base + 3)
            E.tensor_tensor(parts[2], src, parts[1], ALU.subtract).then_inc(sem, 1)

        def phases(engine, body):
            body(0, None)
            with engine.Fori(0, B - 2) as i:
                body(1, i)
            body(2, None)

        @block.sync
        def _(sp):
            for b in range(B):
                sp.dma_start(x_t[:, b * S:(b + 1) * S], a["x_t"][:, b * S:(b + 1) * S]).then_inc(xt_in[b], 16)
                if b == 0:
                    sp.dma_start(w_qkv[:], a["w_qkv_t"]).then_inc(w_in, 16)
            for dst, src in CONSTS:
                sp.dma_start(dst, src).then_inc(consts_in, 16)
            hold(sp, filled, ALL_FILLED)
            sp.dma_start(stack_q["s"][ALIBI_ROW:ALIBI_ROW + 3], a["c_ones"]).then_inc(rows_in, 16)
            sp.dma_start(stack_k["s"][ALIBI_ROW:ALIBI_ROW + 3], a["c_alibi"]).then_inc(rows_in, 16)
            for which in range(2):
                hold(sp, first_split, SPLITS * (which + 1))
                store_parts(sp, 0, parts_first, [which])
            hold(sp, parts_out[0], 16 * 12)
            for g in range(NG):
                load_stacks(sp, g, 0)
            hold(sp, qk_split, 3)
            store_parts(sp, 1, qk_parts, range(2))
            hold(sp, v_read, 2)
            sp.dma_start(v_d[1], v_stage[:]).then_inc(parts_out[1], 16)
            sp.dma_start(x_tok[:], a["x"][0:S, :].rearrange("(t p) d -> p t d", p=P)).then_inc(tok_in, 16)
            hold(sp, ctx_split, SPLITS)
            for n in range(6):
                sp.dma_start(xk_d[:, HD * n:HD * (n + 1), :], xk_parts[:, K_PARTS[n], :]).then_inc(ctx_out, 16)
            hold(sp, ctx_read, 1 + B)
            sp.dma_start(vx_d.rearrange("b c n -> c b n"), vx_all.rearrange("c b h n -> c b (h n)")).then_inc(ctx_out, 16)

            def body(phase, it):
                at = lambda what, more=0: plan.before(phase, it, what, more)
                for what in EVENTS[phase]:
                    name, b = what[0], plan.batch(phase, it, what[-1] if isinstance(what[-1], int) else 0)
                    if name == "max":
                        kind, g = what[1:3]
                        hold(sp, misc_read, at(what, 1))
                        sp.dma_start(stack_q[kind][MAX_ROW:MAX_ROW + 3, G * g:G * g + G, :].rearrange("c h (t q) -> c (h t) q", q=P),
                                     nm_rows[:, g, :]).then_inc(max_in[kind][g], 16)
                    if name == "load_s":
                        g = what[1]
                        if phase == 0:
                            if g == 0:
                                hold(sp, parts_out[1], 16 * 13)
                            hold(sp, pair_read, at(("pair", _s(g, 0), PAIRS["s"] - 1), 1))
                        elif g == 0:
                            hold(sp, pair_read, at(("pair", _x(0, 0), 0)))
                            for done in parts_out[2:]:
                                hold(sp, done, 16 * 13)
                        load_stacks(sp, g, b)
                    if name == "load_v":
                        hold(sp, v_put, NG * b)
                        sp.dma_start(v_tok[:].rearrange("p t d -> p (t d)"), v_d[b]).then_inc(vtok_in, 16)
                    if name == "qk_store":
                        hold(sp, qk_split, 3 * b)
                        store_parts(sp, b, qk_parts, range(2))
                        hold(sp, misc_read, at(("v_proj", what[1]), 1))
                        sp.dma_start(v_d[b], v_stage[:]).then_inc(parts_out[b], 16)
                    if name == "s_oproj" and phase < 2:
                        hold(sp, misc_read, at(what, 1))
                        sp.dma_start(x_tok[:], a["x"][bass.ds((b + 1) * S, S), :].rearrange("(t p) d -> p t d", p=P)).then_inc(tok_in, 16)
                    if name == "xq_store":
                        hold(sp, xq_split, SPLITS * (b + 1))
                        for n in range(6):
                            sp.dma_start(xq_d[:, HD * n:HD * (n + 1), :], xq_parts[:, Q_PARTS[n], :]).then_inc(xq_out, 16)
                    if name == "load_x":
                        if phase == 0:
                            hold(sp, ctx_out, 16 * 7)
                            hold(sp, x_ready, 3)
                        else:
                            hold(sp, pv_done["x"], NG * b)
                        sp.dma_start(stack_k["x"][0:NR, :, 0:C],
                                     xk_d[:, :, bass.ds(b * C, C)].rearrange("h r c -> r h c")).then_inc(xkv_in, 16)
                        sp.dma_start(v_x[0:C].rearrange("c h n -> c (h n)"), vx_d[b]).then_inc(xkv_in, 16)
                        hold(sp, xq_out, 16 * 6 * (b + 1))
                        for g in range(NG):
                            sp.dma_start(stack_q["x"][0:NR, G * g:G * g + G, :],
                                         xq_d[G * g:G * g + G].rearrange("h r s -> r h s")).then_inc(stack_in["x"][g], 16)
                    if name == "pay":
                        hold(sp, ln_done["x"], b + 1)
                        sp.dma_start(x2_d[bass.ds(b * S, S), :].rearrange("(t p) d -> p t d", p=P),
                                     pay[:, 0, :, 0:D]).then_inc(x2_out, 16)

            phases(sp, body)

            for e in range(E):
                i = e % 2
                if e >= 2:
                    hold(sp, y_step, 2 * (e - 1))
                sp.dma_start(w1[:, i, :], a["w1"][e]).then_inc(we_in[i], 16)
                sp.dma_start(w2[:, i, :], a["w2"][e]).then_inc(we_in[i], 16)
                if e == 0:
                    hold(sp, sent[0], 16 * (NT * B + 1))
                    hold(sp, sent[1], 16 * (NT * B + 1))
                sp.dma_start(xs[:, i, :, :], slots_d[e * CAP:(e + 1) * CAP, :].rearrange("(t p) c -> p t c", p=P)).then_inc(slots_in[i], 16)
            hold(sp, x2_out, 16 * B)
            for i in range(2):
                hold(sp, y_sent[i], 16 * E)
            for b in range(B):
                rows = lambda t, k: t[(k * B + b) * S:(k * B + b + 1) * S, :].rearrange("(t p) d -> p t d", p=P)
                sp.dma_start(fin[:, b, 0], rows(x2_d, 0)).then_inc(fin_in[b], 16)
                sp.dma_start(fin[:, b, 1], rows(y_d, 0)).then_inc(fin_in[b], 16)
                sp.dma_start(fin[:, b, 2], rows(y_d, 1)).then_inc(fin_in[b], 16)
            for b in range(B):
                hold(sp, fin_ready, b + 1)
                sp.dma_start(out[b * S:(b + 1) * S, :].rearrange("(t p) d -> p t d", p=P), fin[:, b, 1]).then_inc(fin_out, 16)
            hold(sp, fin_out, 16 * B)

        @block.tensor
        def _(pe):
            def mm(dst, lhs, rhs, start=True, stop=True):
                return nc.tensor.matmul(dst, lhs, rhs, start=start, stop=stop)

            pe.wait_ge(w_in, 16)
            for b in range(2):
                pe.wait_ge(xt_in[b], 16)
                xb = x_t[:, b * S:(b + 1) * S]
                for which in range(2):
                    mm(p_pair[b][:, which * S:(which + 1) * S], w_qkv[:, which, :], xb).then_inc(proj_filled, 1)
                for t in range(NT):
                    last = mm(p_unit[b][:, t * D:(t + 1) * D], xb[:, t * P:(t + 1) * P], w_qkv[:, 2, :])
                last.then_inc(proj_filled, 1)
            pe.wait_ge(consts_in, 16 * len(CONSTS))
            mm(p_misc[:, 0:B * C], wx[:, 1, :], ctx_t[:]).then_inc(ctx_filled, 1)
            for b in range(B):
                last = mm(p_out[0:C, b * D:(b + 1) * D], ctx_t[:, b * C:(b + 1) * C], wx[:, 2, :])
            last.then_inc(ctx_filled, 1)
            pe.wait_ge(q_read, 2)
            pe.wait_ge(k_read, 2)
            pe.wait_ge(v_read, 2)
            pe.wait_ge(ctx_read, 1 + B)
            pe.wait_ge(filled, ALL_FILLED)
            pe.wait_ge(rows_in, 32)

            def unit(phase, it, what):
                _, (kind, g, rel), u = what
                n = plan.before(phase, it, what)
                if u == 0:
                    need = plan.batch(phase, it, rel) + 1
                    pe.wait_ge(stack_in[kind][g], (32 if kind == "s" else 16) * need)
                    if kind == "x":
                        pe.wait_ge(xkv_in, 32 * need)
                if not (phase == 0 and n < 2):
                    pe.wait_ge(unit_read, n - 1)
                bank = p_unit[plan.half(phase, what)]
                sq, sk = stack_q[kind], stack_k[kind]
                if kind == "x":
                    for i in range(G):
                        last = mm(bank[:, i * C:(i + 1) * C], sq[0:SCORE_ROWS, G * g + i, u * P:(u + 1) * P],
                                  sk[0:SCORE_ROWS, G * g + i, 0:C])
                else:
                    if u < 4:
                        parts = [(u, 3, 0)]
                    elif u < 8:
                        parts = [(u - 4, 2, 0), (u - 4, 0, 3 * P)]
                    else:
                        parts = [(2 * (u - 8), 1, 0), (2 * (u - 8) + 1, 1, 2 * P)]
                    for i, t, at in parts:
                        keys = (t + 1) * P
                        mm(bank[:, at:at + keys], sq[0:SCORE_ROWS, G * g + i, t * P:(t + 1) * P],
                           sk[0:SCORE_ROWS, G * g + i, 0:keys], stop=False)
                        last = mm(bank[:, at + t * P:at + keys], identb[:], causal[:], start=False)
                last.then_inc(unit_filled, 1)

            def pair(phase, it, what):
                _, (kind, g, rel), u = what
                n = plan.before(phase, it, what)
                if u == 0:
                    pe.wait_ge(max_in[kind][g], 16 * (plan.batch(phase, it, rel) + 1))
                if not (phase == 0 and n < 2):
                    pe.wait_ge(pair_read, n - 1)
                bank = p_pair[plan.half(phase, what)]
                sq, sk = stack_q[kind], stack_k[kind]
                for i, t, at in pair_parts(kind, u):
                    h = G * g + i
                    last = mm(bank[:, at:at + (S - t * P)], sk[:, h, t * P:(t + 1) * P], sq[:, h, t * P:S])
                last.then_inc(pair_filled, 1)

            def values(phase, it, what):
                _, (kind, g, rel), piece = what
                done = NG * plan.batch(phase, it, rel) + g
                if piece == 0:
                    if kind == "s":
                        pe.wait_ge(v_put, done + 1)
                    n = plan.before(phase, it, what)
                    if not (phase == 0 and n == 0):
                        pe.wait_ge(out_read, n)
                pr = probs[kind][:, g % 2]
                if kind == "x":
                    pe.wait_ge(pair_read, plan.before(phase, it, ("pair", what[1], PAIRS["x"] - 1), 1))
                    for i in range(G):
                        last = mm(p_out[32 * i:32 * i + 32, :], v_x[:, G * g + i, :],
                                  pr[:, i // 2, (i % 2) * S:(i % 2 + 1) * S])
                    last.then_inc(pv_done[kind], 1)
                    return
                t, pairs = ((0, 2), (1, 4), (3, 4), (2, 5))[piece]
                pe.wait_ge(masked, PAIRS["s"] * done + pairs)
                for i in range(G):
                    u, at = prob_place(i, t)
                    last = mm(p_out[32 * i:32 * i + 32, t * P:S], v_s[:, t, G * g + i, :],
                              pr[:, u, at:at + S - t * P], start=(piece == 0), stop=(piece == 3))
                if piece == 3:
                    last.then_inc(pv_done[kind], 1)

            def body(phase, it):
                for what in EVENTS[phase]:
                    name = what[0]
                    if name in ("unit", "pair", "values"):
                        {"unit": unit, "pair": pair, "values": values}[name](phase, it, what)
                    if name not in MISC:
                        continue
                    b = plan.batch(phase, it, what[-1])
                    n = plan.before(phase, it, what)
                    if not (phase == 0 and n == 0):
                        pe.wait_ge(misc_read, n)
                    if name == "out":
                        kind, g = what[1:3]
                        pe.wait_ge(out_read, plan.turn(phase, it, what) + 1)
                        for t in range(NT):
                            last = nc.tensor.transpose(p_misc[:, t * P:(t + 1) * P], u_sb[:, g % 2, t * P:(t + 1) * P], ident[:])
                    if name == "max":
                        kind, g = what[1:3]
                        hold(pe, nm_step[kind], SPLITS * (NG * b + g + 1))
                        last = nc.tensor.transpose(p_misc[0:3 * G * NT, 0:P // 2].bitcast(BF16),
                                                   nm_parts[:, g, :, :].rearrange("p c n -> p (c n)"), identb[:])
                    if name in ("q_proj", "k_proj"):
                        if name == "q_proj":
                            pe.wait_ge(xt_in[b], 16)
                        last = mm(p_misc[:], w_qkv[:, int(name == "k_proj"), :], x_t[:, b * S:(b + 1) * S])
                    if name == "v_proj":
                        for t in range(NT):
                            last = mm(p_misc[:, t * D:(t + 1) * D], x_t[:, b * S + t * P:b * S + (t + 1) * P], w_qkv[:, 2, :])
                    kind = name[0]
                    if name in ("s_ot", "x_ot"):
                        for t in range(NT):
                            last = nc.tensor.transpose(p_misc[:, t * P:(t + 1) * P], o_tok[kind][:, t, :], ident[:])
                    if name in ("s_oproj", "x_oproj"):
                        for t in range(NT):
                            last = mm(p_misc[:, t * D:(t + 1) * D], o_t[kind][:, t * P:(t + 1) * P],
                                      w_o[:] if kind == "s" else wx[:, 3, :])
                    if name == "s_x1t":
                        pe.wait_ge(ln_done["s"], b + 1)
                        for t in range(NT):
                            last = nc.tensor.transpose(p_misc[:, t * P:(t + 1) * P], x1[:, t, :], ident[:])
                    if name == "s_xq":
                        last = mm(p_misc[:], wx[:, 0, :], x1_t[:])
                    if name == "x_x2t":
                        pe.wait_ge(ln_done["x"], b + 1)
                        for t in range(NT):
                            last = nc.tensor.transpose(p_misc[:, t * P:(t + 1) * P], pay[:, 0, t, 0:D], ident[:])
                    if name == "x_logit":
                        for t in range(NT):
                            last = mm(p_misc[:, t * E:(t + 1) * E], x2_t[:, t * P:(t + 1) * P], w_gate[:])
                    if name == "x_count":
                        pe.wait_ge(route_step, ROUTE_STEPS * b + HOT_STEP)
                        chosen = hotb[:].rearrange("p k t e -> p (k t e)")
                        mm(p_misc[:, 0:2 * NT * E], before_t[:], chosen)
                        last = mm(p_misc[:, 2 * NT * E:4 * NT * E], ones[:], chosen)
                    last.then_inc(misc_filled, 1)

            phases(pe, body)

            def hidden(e):
                i = e % 2
                pe.wait_ge(slots_in[i], 16 * (e // 2 + 1))
                if e >= 2:
                    pe.wait_ge(xs_read, e - 1)
                for t in range(2):
                    last = nc.tensor.transpose(p_unit[i][:, t * P:(t + 1) * P], xs[:, i, t, 0:D], ident[:])
                last.then_inc(xs_filled, 1)
                pe.wait_ge(xs_read, e + 1)
                pe.wait_ge(we_in[i], 32 * (e // 2 + 1))
                if e >= 2:
                    pe.wait_ge(h_done, NC * (e - 1))
                for c in range(NC):
                    mm(p_pair[i][:, c * CAP:(c + 1) * CAP], w1[:, i, c * P:(c + 1) * P], xs_t[:, i, :]).then_inc(h_filled, 1)

            def result(e):
                i = e % 2
                bank = (p_out, p_misc)[i]
                pe.wait_ge(h_done, NC * (e + 1))
                if e >= 2:
                    pe.wait_ge(y_step, 2 * (e - 2) + 1)
                for t in range(2):
                    for c in range(NC):
                        last = mm(bank[:, t * D:(t + 1) * D], h_t[:, i, c, t * P:(t + 1) * P], w2[:, i, c * D:(c + 1) * D],
                                  start=(c == 0), stop=(c == NC - 1))
                last.then_inc(y_filled, 1)

            pe.wait_ge(misc_read, plan.before(2, None, ("x_count", 1), 1))
            hidden(0)
            for e in range(E):
                if e + 1 < E:
                    hidden(e + 1)
                result(e)

        @block.scalar
        def _(act):
            for b in range(2):
                act.wait_ge(proj_filled, 3 * b + 1)
                nc.scalar.mul((qk_first if b == 0 else qk)[:, 0, :], p_pair[b][:, 0:S], SCALE).then_inc(q_read, 1)
                act.wait_ge(proj_filled, 3 * b + 2)
                nc.scalar.copy((qk_first if b == 0 else qk)[:, 1, :], p_pair[b][:, S:2 * S]).then_inc(k_read, 1)
                if b:
                    act.wait_ge(q_read, 2)
                    act.wait_ge(k_read, 2)
                    nc.scalar.copy(qk_parts[:, 0], qk[:]).then_inc(high_done, 1)
                act.wait_ge(proj_filled, 3 * b + 3)
                nc.scalar.copy(v_tok[:].rearrange("p t d -> p (t d)") if b == 0 else v_stage[:], p_unit[b][:]).then_inc(v_read, 1)
            act.wait_ge(consts_in, 16 * len(CONSTS))
            nc.scalar.mul(bq_s[:], b_col[:, 0:1], SCALE).then_inc(bq_ready, 1)
            act.wait_ge(ctx_filled, 1)
            act.wait_ge(bq_ready, 1)
            nc.scalar.activation(xk, p_misc[:, 0:B * C], ACT.Identity, bias=b_col[:, 1:2]).then_inc(ctx_read, 1)
            act.wait_ge(parts_out[0], 16 * 12)

            def body(phase, it):
                for what in EVENTS[phase]:
                    name = what[0]
                    if name == "pair":
                        kind, g, _ = what[1]
                        if phase == 0 and what == ("pair", _s(1, 0), 0):
                            act.wait_ge(ctx_out, 16 * 7)
                        act.wait_ge(pair_filled, plan.before(phase, it, what, 1))
                        nc.scalar.activation(probs[kind][:, g % 2, what[2], :], p_pair[plan.half(phase, what)][:],
                                             ACT.Exp).then_inc(pair_read, 1)
                        continue
                    b = plan.batch(phase, it, what[-1])
                    if name == "take":
                        kind, g = what[1:3]
                        act.wait_ge(pv_done[kind], NG * b + g + 1)
                        nc.scalar.copy(u_sb[:, g % 2, :], p_out[:]).then_inc(out_read, 1)
                    if name == "max":
                        act.wait_ge(misc_filled, plan.before(phase, it, what, 1))
                        nc.scalar.copy(nm_rows[:, what[2], :], p_misc[0:3 * G * NT, 0:P // 2].bitcast(BF16)).then_inc(misc_read, 1)
                    if name in ("q_proj", "k_proj"):
                        which = int(name == "k_proj")
                        act.wait_ge(misc_filled, plan.before(phase, it, what, 1))
                        if which == 0:
                            act.wait_ge(qk_split, 3 * (b - 1))
                            act.wait_ge(parts_out[b - 1], 16 * 13)
                            nc.scalar.mul(qk[:, 0, :], p_misc[:], SCALE).then_inc(q_read, 1)
                        else:
                            nc.scalar.copy(qk[:, 1, :], p_misc[:]).then_inc(k_read, 1)
                        act.wait_ge((q_read, k_read)[which], b + 1)
                        nc.scalar.copy(qk_parts[:, 0, which, :], qk[:, which, :]).then_inc(misc_read, 1)
                    if name == "v_proj":
                        act.wait_ge(misc_filled, plan.before(phase, it, what, 1))
                        nc.scalar.copy(v_stage[:], p_misc[:]).then_inc(misc_read, 1)
                    if name in ("s_ot", "x_ot", "s_x1t", "x_x2t"):
                        dst = {"s_ot": o_t["s"], "x_ot": o_t["x"], "s_x1t": x1_t, "x_x2t": x2_t}[name]
                        act.wait_ge(misc_filled, plan.before(phase, it, what, 1))
                        nc.scalar.copy(dst[:], p_misc[:]).then_inc(misc_read, 1)
                    if name == "s_xq":
                        act.wait_ge(misc_filled, plan.before(phase, it, what, 1))
                        if phase:
                            act.wait_ge(xq_split, SPLITS * b)
                        nc.scalar.activation(xq[:], p_misc[:], ACT.Identity, bias=bq_s[:], scale=SCALE).then_inc(misc_read, 1)
                    if name == "gate_exp":
                        act.wait_ge(misc_read, plan.before(phase, it, ("x_logit",) + what[1:], 1))
                        nc.scalar.activation(prob[:], logit[:], ACT.Exp).then_inc(route_exp, 1)

            phases(act, body)

            for e in range(E):
                i = e % 2
                act.wait_ge(we_in[i], 32 * (e // 2 + 1))
                if e >= 2:
                    act.wait_ge(y_filled, e - 1)
                for c in range(NC):
                    act.wait_ge(h_filled, NC * e + 2 * (c // 2) + 2)
                    nc.scalar.activation(h_t[:, i, c, :], p_pair[i][:, c * CAP:(c + 1) * CAP], ACT.Gelu_apprx_tanh,
                                         bias=w1[:, i, HID + c:HID + c + 1]).then_inc(h_done, 1)

        @block.vector
        def _(dve):
            nc.vector.memset(ones[:], 1.0).then_inc(filled, 1)
            nc.vector.memset(stack_k["s"][:].bitcast(F32), 0.0).then_inc(stack_zero, 1)
            dve.wait_ge(stack_zero, 1)
            nc.vector.memset(stack_k["s"][MAX_ROW:MAX_ROW + 3], 1.0).then_inc(filled, 1)
            for which in range(2):
                dve.wait_ge((q_read, k_read)[which], 1)
                split(dve, nc.vector, qk_first[:, which], [parts_first[:, c, which] for c in range(3)], first_split, SPLITS * which)
            nc.vector.memset(zeros[:], 0.0).then_inc(zeros_set, 1)
            dve.wait_ge(ctx_read, 1)
            split(dve, nc.vector, xk, [xk_parts[:, c, :] for c in range(3)], ctx_split, 0)
            dve.wait_ge(ctx_filled, 2)
            dve.wait_ge(vx_ready, 1)
            dve.wait_ge(consts_in, 16 * len(CONSTS))
            for b in range(B):
                nc.vector.tensor_tensor(vx_all[:, b, :, 0:HD], p_out[0:C, b * D:(b + 1) * D].rearrange("c (h d) -> c h d", d=HD),
                                        bv_row[0:C].rearrange("c (h d) -> c h d", d=HD), ALU.add).then_inc(ctx_read, 1)
            nc.vector.memset(stack_k["x"][:].bitcast(F32), 0.0).then_inc(stack_zero, 1)
            dve.wait_ge(stack_zero, 2)
            nc.vector.memset(stack_k["x"][MAX_ROW:MAX_ROW + 3, :, 0:C], 1.0).then_inc(x_ready, 1)

            def spread(kind, b):
                step, base = ln_step[kind], LN_STEPS * b
                for t in range(NT):
                    last = nc.vector.bn_stats(stats[kind][:, t, :], r[kind][:, t, :])
                last.then_inc(step, 1)
                hold(dve, step, base + 1)
                for t in range(NT):
                    last = nc.vector.bn_aggr(mv[kind][:, t, :], stats[kind][:, t, :])
                last.then_inc(step, 1)
                dve.wait_ge(step, base + 2)
                nc.vector.tensor_scalar(var_eps[kind][:], mv[kind][:, :, 1], EPS, None, ALU.add).then_inc(step, 1)

            def norm(kind, b, put):
                dve.wait_ge(ln_pow[kind], b + 1)
                for t in range(NT):
                    last = nc.vector.tensor_scalar(put(t), r[kind][:, t, :], mv[kind][:, t, 0:1], rstd[kind][:, t:t + 1],
                                                   ALU.subtract, ALU.mult)
                last.then_inc(ln_done[kind], 1)

            def weigh(e):
                i = e % 2
                dve.wait_ge(y_filled, e + 1)
                if e >= 2:
                    dve.wait_ge(y_sent[i], 32 * (e // 2))
                nc.vector.tensor_copy(yrow[:, i, :], xs[:, i, :, D + 1])
                nc.vector.tensor_tensor(yb[:, i], (p_out, p_misc)[i][:, 0:2 * D].rearrange("p (t d) -> p t d", t=2),
                                        w2[:, i, HID:HID + D].unsqueeze(1).broadcast_to([P, 2, D]), ALU.add).then_inc(y_step, 1)
                dve.wait_ge(y_step, 2 * e + 1)
                for t in range(2):
                    last = nc.vector.tensor_scalar(ys[:, i, t, :], yb[:, i, t, :], xs[:, i, t, D:D + 1], None, ALU.mult)
                last.then_inc(y_step, 1)

            def route(phase, it, rel, part):
                k = [{"x_logit": 0, "pick": 1, "x_count": PICK_STEP}[part]]
                bx = plan.batch(phase, it, rel)

                def step(ins):
                    k[0] += 1
                    ins.then_inc(route_step, 1)
                    dve.wait_ge(route_step, ROUTE_STEPS * bx + k[0])

                def per_token(t):
                    return t.unsqueeze(2).broadcast_to([P, NT, E])

                V = nc.vector
                if part == "x_logit":
                    dve.wait_ge(misc_filled, plan.before(phase, it, ("x_logit", rel), 1))
                    lg = p_misc[:, 0:NT * E].rearrange("p (t e) -> p t e", e=E)
                    step(V.tensor_reduce(stat4[:, 0, :], lg, X_AXIS, ALU.max, negate=True))
                    V.tensor_tensor(logit[:], lg, per_token(stat4[:, 0, :]), ALU.add).then_inc(misc_read, 1)
                if part == "pick":
                    dve.wait_ge(route_exp, bx + 1)
                    step(V.tensor_reduce(stat4[:, 1, :], prob[:], X_AXIS, ALU.add))
                    step(V.reciprocal(stat4[:, 2, :], stat4[:, 1, :]))
                    step(V.tensor_tensor(prob[:], prob[:], per_token(stat4[:, 2, :]), ALU.mult))
                    for c in range(2):
                        step(V.tensor_reduce(stat4[:, 3 + c, :], prob[:], X_AXIS, ALU.max))
                        step(V.tensor_tensor(pick[:], prob[:], per_token(stat4[:, 3 + c, :]), ALU.is_equal))
                        step(V.tensor_tensor(pick[:], pick[:], e_const[:, 0], ALU.mult))
                        step(V.tensor_reduce(stat4[:, 5, :], pick[:], X_AXIS, ALU.max))
                        step(V.tensor_tensor(hot[:, c], pick[:], per_token(stat4[:, 5, :]), ALU.is_equal))
                        if c == 0:
                            step(V.scalar_tensor_tensor(prob[:], hot[:, 0], -2.0, prob[:], ALU.mult, ALU.add))
                    step(V.tensor_copy(hotb[:], hot[:]))
                    assert k[0] == HOT_STEP
                    step(V.tensor_tensor(stat4[:, 6, :], stat4[:, 3, :], stat4[:, 4, :], ALU.add))
                    step(V.tensor_scalar(stat4[:, 6, :], stat4[:, 6, :], 1e-9, None, ALU.add))
                    step(V.reciprocal(stat4[:, 7, :], stat4[:, 6, :]))
                    for c in range(2):
                        V.tensor_tensor(pay[:, c, :, D], stat4[:, 3 + c, :], stat4[:, 7, :], ALU.mult)
                        V.tensor_copy(pay[:, c, :, D + 1], row_id[:, c, :])
                    assert k[0] == PICK_STEP
                if part == "x_count":
                    dve.wait_ge(misc_filled, plan.before(phase, it, ("x_count", rel), 1))
                    cum = p_misc[:, 0:2 * NT * E].rearrange("p (k t e) -> p k t e", k=2, t=NT)
                    tot = p_misc[:, 2 * NT * E:4 * NT * E].rearrange("p (k t e) -> p k t e", k=2, t=NT)
                    for t in range(NT):
                        step(V.tensor_tensor(tile_base[:, :, t + 1, :], tot[:, :, t, :], tile_base[:, :, t, :], ALU.add))
                    V.tensor_tensor(pos[:], cum, tile_base[:, :, 0:NT, :], ALU.add).then_inc(misc_read, 1)
                    step(V.tensor_scalar(first_used[:], tile_base[:, 0, NT, :], float(CAP), None, ALU.min))
                    dve.wait_ge(misc_read, plan.before(phase, it, ("x_count", rel), 1))
                    V.tensor_scalar(used[:, 0], pos[:, 0], float(CAP), DROPPED, ALU.is_ge, ALU.mult)
                    step(V.tensor_tensor(used[:, 1], pos[:, 1], first_used[:].unsqueeze(1).broadcast_to([P, NT, E]), ALU.add))
                    V.tensor_tensor(used[:, 0], used[:, 0], pos[:, 0], ALU.add)
                    step(V.tensor_scalar(used[:, 1], used[:, 1], float(CAP), DROPPED, ALU.is_ge, ALU.mult))
                    step(V.tensor_tensor(used[:, 1], used[:, 1], pos[:, 1], ALU.subtract))
                    step(V.tensor_tensor(used[:], used[:], e_const[:, 1:3], ALU.add))
                    step(V.tensor_tensor(used[:], used[:], hot[:], ALU.mult))
                    step(V.tensor_reduce(slotf[:], used[:], X_AXIS, ALU.add))
                    V.tensor_copy(tile_base[:, :, 0, :], tile_base[:, :, NT, :])
                    V.tensor_scalar(row_id[:], row_id[:], float(S), None, ALU.add)
                    step(V.tensor_copy(slot[:], slotf[:]))
                    assert k[0] == ROUTE_STEPS, k[0]

            dve.wait_ge(small_ready, 1)

            def body(phase, it):
                for what in EVENTS[phase]:
                    name = what[0]
                    if name == "unit":
                        (kind, g, _), u = what[1:]
                        nm = negmax[:, g]
                        dve.wait_ge(unit_filled, plan.before(phase, it, what, 1))
                        bank = p_unit[plan.half(phase, what)]
                        if kind == "x":
                            last = nc.vector.tensor_reduce(nm[:, :, u], bank[:, 0:G * C].rearrange("p (i c) -> p i c", c=C), X_AXIS, ALU.max, negate=True)
                        elif u < 4:
                            last = nc.vector.tensor_reduce(nm[:, u, 3:4], bank[:], X_AXIS, ALU.max, negate=True)
                        elif u < 8:
                            nc.vector.tensor_reduce(nm[:, u - 4, 2:3], bank[:, 0:3 * P], X_AXIS, ALU.max, negate=True)
                            last = nc.vector.tensor_reduce(nm[:, u - 4, 0:1], bank[:, 3 * P:], X_AXIS, ALU.max, negate=True)
                        else:
                            last = nc.vector.tensor_reduce(nm[:, 2 * (u - 8):2 * (u - 8) + 2, 1], bank[:].rearrange("p (i c) -> p i c", i=2), X_AXIS, ALU.max, negate=True)
                        last.then_inc(unit_read, 1)
                        continue
                    if name in ("pair", "values"):
                        continue
                    b = plan.batch(phase, it, what[-1])
                    if name == "out":
                        kind, g = what[1:3]
                        dve.wait_ge(misc_filled, plan.before(phase, it, what, 1))
                        u = p_misc[:].rearrange("p (t i n) -> p t i n", t=NT, i=G)
                        nc.vector.reciprocal(rsum[:, g % 2], u[:, :, :, HD]).then_inc(norm_step[kind], 1)
                        dve.wait_ge(norm_step[kind], NG * b + g + 1)
                        nc.vector.tensor_tensor(o_tok[kind][:, :, G * HD * g:G * HD * (g + 1)].rearrange("p t (i d) -> p t i d", i=G),
                                                u[:, :, :, 0:HD], rsum[:, g % 2].unsqueeze(3).broadcast_to([P, NT, G, HD]),
                                                ALU.mult).then_inc(misc_read, 1)
                    if name in ("s_oproj", "x_oproj"):
                        kind = name[0]
                        dve.wait_ge(misc_filled, plan.before(phase, it, what, 1))
                        if kind == "s":
                            dve.wait_ge(tok_in, 16 * (b + 1))
                        else:
                            dve.wait_ge(bias_added, b + 1)
                        nc.vector.tensor_tensor(r[kind][:].rearrange("p t d -> p (t d)"), p_misc[:],
                                                (x_tok if kind == "s" else x1_bias)[:].rearrange("p t d -> p (t d)"),
                                                ALU.add).then_inc(misc_read, 1)
                        dve.wait_ge(misc_read, plan.before(phase, it, what, 1))
                        spread(kind, b)
                    if name == "norm":
                        if what[1] == "s":
                            if phase:
                                hold(dve, bias_added, b)
                            norm("s", b, lambda t: x1[:, t, :])
                        else:
                            dve.wait_ge(sent[0], 16 * NT * b + 16)
                            dve.wait_ge(sent[1], 16 * NT * b + 16)
                            norm("x", b, lambda t: pay[:, 0, t, 0:D])
                    if name in ("x_logit", "pick", "x_count"):
                        route(phase, it, what[1], name)

            phases(dve, body)

            for e in range(E):
                i = e % 2
                dve.wait_ge(xs_filled, e + 1)
                nc.vector.tensor_copy(xs_t[:, i, :], p_unit[i][:, 0:CAP]).then_inc(xs_read, 1)
                if e >= 1:
                    weigh(e - 1)
            weigh(E - 1)

            for b in range(B):
                tokens, first, second = (fin[:, b, k] for k in range(3))
                base = 5 * b
                dve.wait_ge(fin_in[b], 48)
                nc.vector.tensor_tensor(first, first, second, ALU.add).then_inc(fin_step, 1)
                dve.wait_ge(fin_step, base + 1)
                nc.vector.tensor_tensor(tokens, tokens, first, ALU.add).then_inc(fin_step, 1)
                dve.wait_ge(fin_step, base + 2)
                for t in range(NT):
                    last = nc.vector.bn_stats(stats["s"][:, t, :], tokens[:, t, :])
                last.then_inc(fin_step, 1)
                dve.wait_ge(fin_step, base + 3)
                for t in range(NT):
                    last = nc.vector.bn_aggr(mv["s"][:, t, :], stats["s"][:, t, :])
                last.then_inc(fin_step, 1)
                dve.wait_ge(fin_step, base + 4)
                nc.vector.tensor_scalar(var_eps["s"][:], mv["s"][:, :, 1], EPS, None, ALU.add).then_inc(fin_step, 1)
                dve.wait_ge(fin_pow, b + 1)
                for t in range(NT):
                    last = nc.vector.tensor_scalar(first[:, t, :], tokens[:, t, :], mv["s"][:, t, 0:1], rstd["s"][:, t:t + 1],
                                                   ALU.subtract, ALU.mult)
                last.then_inc(fin_ready, 1)

        @block.gpsimd
        def _(pool):
            g_ = nc.gpsimd
            g_.memset(stack_q["s"][:].bitcast(F32), 0.0).then_inc(filled, 1)
            g_.memset(minus_half[:], -0.5)
            g_.memset(tile_base[:], 0.0).then_inc(small_ready, 1)
            g_.memset(vx_all, 0.0).then_inc(pool_fill, 1)
            g_.memset(v_s[:], 0.0).then_inc(pool_fill, 1)
            hold(pool, pool_fill, 1)
            g_.memset(vx_all[:, :, :, HD], 1.0).then_inc(vx_ready, 1)
            hold(pool, pool_fill, 2)
            g_.memset(v_s[:, :, :, HD], 1.0)

            def split_rest(b):
                base = 3 * (b - 1)
                g_.tensor_tensor(qk[:], qk[:], qk_parts[:, 0], ALU.subtract).then_inc(qk_split, 1)
                hold(pool, qk_split, base + 1)
                g_.tensor_copy(qk_parts[:, 1], qk[:]).then_inc(qk_split, 1)
                hold(pool, qk_split, base + 2)
                g_.tensor_tensor(qk_parts[:, 2], qk[:], qk_parts[:, 1], ALU.subtract).then_inc(qk_split, 1)

            hold(pool, high_done, 1)
            split_rest(1)
            g_.memset(stack_q["x"][:].bitcast(F32), 0.0).then_inc(x_ready, 1)
            g_.memset(v_x[:], 0.0).then_inc(x_ready, 1)

            def body(phase, it):
                for what in EVENTS[phase]:
                    name = what[0]
                    if name == "pair" and what[1][0] == "s":
                        _, (kind, g, rel), u = what
                        b = plan.batch(phase, it, rel)
                        if u == 0:
                            if phase == 0 and rel == 0:
                                hold(pool, v_read, 1)
                            else:
                                hold(pool, vtok_in, 16 * b)
                                hold(pool, pv_done["s"], NG * (b - 1) + g + 1)
                            for t in range(NT):
                                last = g_.tensor_copy(v_s[:, t, G * g:G * g + G, 0:HD],
                                                      v_tok[:, t, G * HD * g:G * HD * (g + 1)].rearrange("p (i d) -> p i d", i=G))
                            last.then_inc(v_put, 1)
                        hold(pool, pair_read, plan.before(phase, it, what, 1))
                        pr = probs["s"][:, g % 2, u, :]
                        if u < 2:
                            view, pattern = pr.rearrange("p (i n) -> p i n", i=2)[:, :, 0:P], [[0, 2], [1, P]]
                        elif u < 4:
                            view, pattern = pr.rearrange("p (i n) -> p i n", i=2)[:, :, 0:2 * P], [[0, 2], [0, 2], [1, P]]
                        else:
                            view, pattern = pr.rearrange("p (i n) -> p i n", i=4)[:, :, 0:P], [[0, 4], [1, P]]
                        g_.affine_select(out=view, in_=view, compare_op=ALU.is_ge, fill=0.0, base=0,
                                         pattern=pattern, channel_multiplier=-1).then_inc(masked, 1)
                    if name in ("pair", "unit", "values"):
                        continue
                    b = plan.batch(phase, it, what[-1])
                    if name == "split":
                        kind, g = what[1:3]
                        hold(pool, unit_read, plan.before(phase, it, ("unit", what[1:], UNITS[kind] - 1), 1))
                        split(pool, g_, negmax[:, g].rearrange("p i t -> p (i t)"), [nm_parts[:, g, c, :] for c in range(3)],
                              nm_step[kind], SPLITS * (NG * b + g))
                    if name == "clear":
                        hold(pool, consts_in, 16 * len(CONSTS))
                        pool.dma_start(slots_d.rearrange("(t p) c -> p t c", p=P),
                                       empty[:].unsqueeze(1).broadcast_to([P, E * CAP // P, ROW])).then_inc(sent[0], 16)
                        hold(pool, zeros_set, 1)
                        pool.dma_start(y_d.rearrange("(t p) c -> p t c", p=P),
                                       zeros[:].unsqueeze(1).broadcast_to([P, 2 * B * S // P, D])).then_inc(sent[1], 16)
                    if name == "qk_split":
                        hold(pool, misc_read, plan.before(phase, it, ("k_proj", what[1]), 1))
                        split_rest(b)
                    if name == "root":
                        kind = what[1]
                        hold(pool, ln_step[kind], LN_STEPS * (b + 1))
                        g_.tensor_tensor(rstd[kind][:], var_eps[kind][:], minus_half[:], ALU.pow).then_inc(ln_pow[kind], 1)
                    if name == "xq_split":
                        if phase:
                            hold(pool, xq_out, 16 * 6 * b)
                        hold(pool, misc_read, plan.before(phase, it, ("s_xq", what[1]), 1))
                        split(pool, g_, xq[:], [xq_parts[:, c, :] for c in range(3)], xq_split, SPLITS * b)
                    if name == "bias":
                        if phase:
                            hold(pool, misc_read, plan.before(phase, it, ("x_oproj", what[1] - 1), 1))
                        else:
                            hold(pool, consts_in, 16 * len(CONSTS))
                        hold(pool, ln_done["s"], b + 1)
                        g_.tensor_tensor(x1_bias[:], x1[:], bo_row[:].unsqueeze(1).broadcast_to([P, NT, D]), ALU.add).then_inc(bias_added, 1)
                    if name == "pay":
                        hold(pool, ln_done["x"], b + 1)
                        g_.tensor_copy(pay[:, 1, :, 0:D], pay[:, 0, :, 0:D]).then_inc(pay_copied, 1)
                    if name == "send":
                        hold(pool, pay_copied, b + 1)
                        hold(pool, route_step, ROUTE_STEPS * (b + 1))
                        hold(pool, x2_out, 16 * (b + 1))
                        for k in (1, 0):
                            hold(pool, sent[1 - k], 16 * NT * b + (16 if k == 1 else 16 + 16 * NT))
                            for t in range(NT):
                                g_.indirect_dma_start(slots_d, bass.IndirectOffsetOnAxis(ap=slot[:, k, t:t + 1], axis=0),
                                                      pay[:, k, t, :], None, bounds_check=E * CAP - 1,
                                                      oob_is_err=False).then_inc(sent[k], 16)

            phases(pool, body)

            for e in range(E):
                i = e % 2
                hold(pool, y_step, 2 * (e + 1))
                for t in range(2):
                    g_.indirect_dma_start(y_d, bass.IndirectOffsetOnAxis(ap=yrow[:, i, t:t + 1], axis=0),
                                          ys[:, i, t, :], None, bounds_check=2 * B * S - 1,
                                          oob_is_err=False).then_inc(y_sent[i], 16)
            for b in range(B):
                hold(pool, fin_step, 5 * (b + 1))
                g_.tensor_tensor(rstd["s"][:], var_eps["s"][:], minus_half[:], ALU.pow).then_inc(fin_pow, 1)


_OUT = "out"


def _constants():
    def bf16_bits(v):
        return (np.ascontiguousarray(v, np.float32).view(np.uint32) >> 16).astype(np.uint16)

    ident = np.eye(P, dtype=np.float32)
    row = np.arange(P)
    start = 2.0 ** (-2.0 ** (-(math.log2(H) - 3)))
    slopes = np.asarray([start * start ** i for i in range(H)], np.float32)
    alibi = -(slopes[:, None] * np.arange(S, dtype=np.float32)[None, :])
    parts = []
    rest = alibi
    for _ in range(3):
        parts.append(bf16_bits(rest))
        rest = rest - (parts[-1].astype(np.uint32) << 16).view(np.float32)
    expert = np.arange(E, dtype=np.float32)
    consts = np.stack([E - expert, expert * CAP, expert * CAP + CAP - 1])
    ids = (np.arange(2)[None, :, None] * B * S + np.arange(NT)[None, None, :] * P + row[:, None, None])
    empty = np.zeros((1, ROW), np.float32)
    empty[0, D + 1] = DROPPED
    return {
        "c_ident": ident, "c_identb": bf16_bits(ident),
        "c_causal": bf16_bits(np.where(row[None, :] > row[:, None], MASKED, 0.0)),
        "c_before": bf16_bits(row[:, None] < row[None, :]),
        "c_expert": np.broadcast_to(consts[None, :, None, :], (P, 3, NT, E)).astype(np.float32).copy(),
        "c_row": ids.astype(np.float32), "c_empty": empty,
        "c_alibi": np.stack(parts), "c_ones": bf16_bits(np.ones((3, H, S))),
    }


def kernel(**inputs):
    import concourse.bacc as _bacc
    from concourse.bass_utils import run_bass_kernel_spmd as _run

    x = {k: np.asarray(v) for k, v in inputs.items()}
    tokens = x["x"].reshape(B * S, D)
    arrays = {
        "x": tokens, "x_t": tokens.T, "ctx_t": x["ctx_1024"].reshape(B * C, D).T,
        "w_qkv_t": x["L0_attn_W_qkv"].reshape(3, D, D).transpose(2, 0, 1),
        "w_o_t": x["L0_attn_W_o"].T,
        "wx_t": np.stack([x[f"L0_xattn_W{n}"].T for n in "qkvo"], axis=1),
        "b_col": np.stack([x["L0_xattn_bq"], x["L0_xattn_bk"]], axis=1),
        "bv": x["L0_xattn_bv"].reshape(1, D), "bo": x["L0_xattn_bo"].reshape(1, D),
        "w_gate": x["L0_ffn_Wg"],
        "w1": np.concatenate([x["L0_ffn_W1"], x["L0_ffn_b1"].reshape(E, NC, P).transpose(0, 2, 1)], axis=2),
        "w2": np.concatenate([x["L0_ffn_W2"].reshape(E, NC, P, D).transpose(0, 2, 1, 3).reshape(E, P, HID),
                              np.broadcast_to(x["L0_ffn_b2"][:, None, :], (E, P, D))], axis=2),
    }
    arrays.update(_constants())
    arrays = {k: np.ascontiguousarray(v) for k, v in arrays.items()}
    nc = _bacc.Bacc("TRN2", target_bir_lowering=False, num_devices=1)
    aps = {k: nc.dram_tensor(f"in_{k}", v.shape, mybir.dt.from_np(v.dtype), kind="ExternalInput").ap() for k, v in arrays.items()}
    aps.update({k: ap.bitcast(BF16) for k, ap in aps.items() if arrays[k].dtype == np.uint16})
    out = nc.dram_tensor("out", (B * S, D), F32, kind="ExternalOutput").ap()
    decoder(nc, aps, out)
    r = _run(nc, [{f"in_{k}": v for k, v in arrays.items()}], core_ids=[0])
    return r.results[0]["out"].reshape(B, S, D)
```

```python
from contextlib import ExitStack
import math

import numpy as np

import concourse.bass as bass
from concourse import mybir

ALU = mybir.AluOpType
ACT = mybir.ActivationFunctionType
X_AXIS = mybir.AxisListType.X
F32 = mybir.dt.float32
BF16 = mybir.dt.bfloat16
U32 = mybir.dt.uint32

P = 128
B, S, D = 4, 512, 128
H, HD = 16, 8
C = 77
NT = S // P
G = 4
NG = H // G
E, HID, CAP = 8, 512, 256
NC = HID // P
SCALE = HD ** -0.5
EPS = 1e-5
MASKED = -1e30
DROPPED = 8192.0
ROW = D + 2

Q_PARTS = (0, 1, 2, 0, 1, 0)
K_PARTS = (0, 0, 0, 1, 1, 2)
RUNS = ((0, 3), (3, 2), (5, 1))
PRODUCTS = len(Q_PARTS)
NR = HD * PRODUCTS
ALIBI_ROW = NR
MAX_ROW = 96
SCORE_ROWS = 96

UNITS = {"s": 10, "x": 4}
PAIRS = {"s": 5, "x": 2}
VALUES = {"s": 4, "x": 1}

CLEARS = 6


def _s(g, b):
    return ("s", g, b)


def _x(g, b):
    return ("x", g, b)


OPENING = dict(
    exps=[None, None, _s(0, 0), _s(1, 0), _s(2, 0), _s(3, 0),
          _s(0, 1), _s(1, 1), _s(2, 1), _s(3, 1)],
    units={
        _s(0, 0): (0.00, 1.00), _s(1, 0): (1.00, 2.00), _s(2, 0): (1.92, 2.92), _s(3, 0): (3.00, 4.00),
        _s(0, 1): (4.00, 5.00), _s(1, 1): (5.00, 6.00), _s(2, 1): (6.00, 7.00), _s(3, 1): (7.11, 8.06),
        _x(0, 0): (9.80, 9.95), _x(1, 0): (10.00, 10.05),
    },
    at={
        ("max",) + _s(0, 0): 1.27, ("split",) + _s(1, 0): 2.06, ("max",) + _s(1, 0): 2.15, ("clear", 0): 2.97,
        ("pairs",) + _s(1, 0): 3.06, ("load_s", 0, 1): 3.09, ("q_proj", 2): 3.46, ("k_proj", 2): 3.56,
        ("v_proj", 2): 3.67, ("clear", 1): 3.97, ("load_xkv", 0): 4.48, ("load_s", 1, 1): 4.56,
        ("qk_split", 0, 2): 4.81, ("take",) + _s(1, 0): 4.97, ("pairs",) + _s(3, 0): 4.99, ("clear", 2): 5.04,
        ("split",) + _s(0, 1): 5.05, ("qk_split", 1, 2): 5.15, ("max",) + _s(0, 1): 5.22, ("clear", 3): 5.50,
        ("load_s", 2, 1): 5.59, ("qk_store", 2): 5.65, ("clear", 4): 5.97, ("split",) + _s(1, 1): 5.97,
        ("load_s", 3, 1): 6.03, ("load_v", 1): 6.17, ("q_proj", 3): 6.44, ("qk_split", 0, 3): 6.49,
        ("k_proj", 3): 6.55, ("v_proj", 3): 6.58, ("qk_split", 1, 3): 6.99, ("take",) + _s(3, 0): 7.07,
        ("out",) + _s(3, 0): 7.10, ("values",) + _s(0, 1): 7.19, ("s_ot", 0): 7.30, ("s_oproj", 0): 7.40,
        ("root", "s", 0): 7.54, ("norm", "s", 0): 7.64, ("s_x1t", 0): 7.93, ("s_xq", 0): 8.09, ("xq_split", 0): 8.18,
        ("xq_store", 0): 8.29, ("clear", 5): 8.50, ("load_x", 0): 8.64, ("out",) + _s(0, 1): 8.69,
        ("take",) + _s(1, 1): 9.05, ("qk_store", 3): 9.16, ("pairs",) + _s(3, 1): 9.61, ("max",) + _x(0, 0): 10.03,
        ("take",) + _s(2, 1): 10.03, ("bias", 0): 10.39,
    })

LOOP = dict(
    before=[_s(2, 1), _s(3, 1)],
    exps=[_x(0, 0), _x(1, 0), _x(2, 0), _x(3, 0), _s(0, 2), _s(1, 2),
          _s(2, 2), _s(3, 2)],
    units={
        _x(2, 0): (0.00, 0.44), _x(3, 0): (0.50, 1.00), _s(0, 2): (1.00, 2.00), _s(1, 2): (1.92, 2.95),
        _s(2, 2): (3.00, 4.00), _s(3, 2): (4.00, 5.00), _x(0, 1): (6.18, 6.96), _x(1, 1): (6.73, 8.00),
    },
    at={
        ("load_s", 0, 2): -0.50, ("load_v", 2): -0.50, ("load_s", 1, 2): -0.06, ("load_s", 2, 2): 0.24,
        ("load_s", 3, 2): 0.30, ("max",) + _x(1, 0): 0.32, ("split",) + _x(2, 0): 0.41, ("pairs",) + _x(0, 0): 0.90,
        ("take",) + _s(3, 1): 0.96, ("out",) + _s(3, 1): 1.03, ("s_ot", 1): 1.30, ("max",) + _x(3, 0): 1.39,
        ("take",) + _x(0, 0): 1.45, ("split",) + _s(0, 2): 2.07, ("s_oproj", 1): 2.36, ("norm", "s", 1): 2.55,
        ("root", "s", 1): 2.56, ("take",) + _x(1, 0): 2.84, ("pairs",) + _x(3, 0): 2.99, ("xq_store", 1): 3.16,
        ("s_x1t", 1): 3.21, ("max",) + _s(1, 2): 3.35, ("s_xq", 1): 3.36, ("xq_split", 1): 3.51,
        ("take",) + _x(2, 0): 3.87, ("pairs",) + _s(0, 2): 4.00, ("values",) + _x(3, 0): 4.39,
        ("take",) + _x(3, 0): 4.46, ("load_xkv", 1): 4.60, ("split",) + _s(3, 2): 4.71, ("out",) + _x(3, 0): 4.77,
        ("x_ot", 0): 4.99, ("x_oproj", 0): 5.04, ("values",) + _s(0, 2): 5.10, ("load_x", 1): 5.25,
        ("root", "x", 0): 5.29, ("norm", "x", 0): 5.35, ("max",) + _s(3, 2): 5.37, ("pay", 0): 5.39,
        ("x_x2t", 0): 5.60, ("x_logit", 0): 5.83, ("bias", 1): 5.90, ("gate_exp", 0): 5.93, ("pick", 0, 0): 6.03,
        ("pick", 1, 0): 6.05, ("pick", 2, 0): 6.06, ("pick", 3, 0): 6.06, ("pick", 4, 0): 6.08, ("pick", 5, 0): 6.10,
        ("x_count", 0): 6.43, ("place", 0, 0): 6.43, ("place", 1, 0): 6.44, ("send", 0, 0): 6.63,
        ("take",) + _s(1, 2): 6.83, ("split",) + _x(0, 1): 6.99, ("send", 1, 0): 7.05, ("values",) + _s(2, 2): 8.04,
        ("send", 2, 0): 8.30, ("take",) + _s(2, 2): 8.30, ("send", 3, 0): 8.46,
    })

CLOSING = dict(
    before=[_s(2, 1), _s(3, 1)],
    exps=[_x(0, 0), _x(1, 0), _x(2, 0), _x(3, 0), None, None,
          _x(0, 1), _x(1, 1), _x(2, 1), _x(3, 1), None, None],
    units={
        _x(2, 0): (0.00, 0.50), _x(3, 0): (0.50, 1.00), _x(0, 1): (4.42, 4.62), _x(1, 1): (4.64, 4.84),
        _x(2, 1): (4.85, 5.15), _x(3, 1): (5.31, 5.60),
    },
    at={
        ("values",) + _s(3, 1): 0.10, ("max",) + _x(1, 0): 0.39, ("load_expert", 0): 0.60, ("take",) + _s(3, 1): 0.83,
        ("split",) + _x(2, 0): 0.85, ("pairs",) + _x(0, 0): 0.90, ("max",) + _x(2, 0): 0.97,
        ("out",) + _s(3, 1): 1.00, ("s_ot", 1): 1.05, ("split",) + _x(3, 0): 1.06, ("load_expert", 1): 1.60,
        ("root", "s", 1): 2.18, ("s_oproj", 1): 2.21, ("xq_store", 1): 2.40, ("norm", "s", 1): 2.41,
        ("load_expert", 2): 2.59, ("out",) + _x(0, 0): 2.68, ("s_x1t", 1): 2.86, ("s_xq", 1): 3.11,
        ("xq_split", 1): 3.21, ("load_expert", 3): 3.60, ("values",) + _x(3, 0): 4.00, ("take",) + _x(3, 0): 4.10,
        ("load_xkv", 1): 4.10, ("load_x", 1): 4.12, ("out",) + _x(3, 0): 4.25, ("x_ot", 0): 4.30,
        ("x_oproj", 0): 4.40, ("root", "x", 0): 4.45, ("split",) + _x(0, 1): 4.63, ("split",) + _x(1, 1): 4.85,
        ("norm", "x", 0): 4.86, ("bias", 1): 4.88, ("max",) + _x(0, 1): 4.98, ("max",) + _x(1, 1): 5.20,
        ("x_x2t", 0): 5.25, ("max",) + _x(2, 1): 5.74, ("pay", 0): 5.78, ("x_logit", 0): 6.20, ("gate_exp", 0): 6.30,
        ("pick", 0, 0): 6.30, ("pick", 1, 0): 6.50, ("max",) + _x(3, 1): 6.50, ("load_expert", 4): 6.60,
        ("pick", 2, 0): 6.70, ("pick", 3, 0): 7.20, ("pick", 4, 0): 7.40, ("load_expert", 5): 7.60,
        ("pick", 5, 0): 7.70, ("x_count", 0): 8.10, ("place", 0, 0): 8.30, ("place", 1, 0): 8.50,
        ("load_expert", 6): 8.60, ("send", 0, 0): 8.62, ("send", 1, 0): 8.63, ("values",) + _x(1, 1): 8.69,
        ("send", 2, 0): 8.70, ("send", 3, 0): 8.71, ("out",) + _x(1, 1): 9.08, ("load_expert", 7): 9.51,
        ("take",) + _x(2, 1): 9.85, ("take",) + _x(3, 1): 9.90, ("out",) + _x(2, 1): 10.36,
        ("values",) + _x(3, 1): 10.37, ("out",) + _x(3, 1): 11.15, ("x_ot", 1): 11.24, ("x_oproj", 1): 11.29,
        ("root", "x", 1): 11.34, ("norm", "x", 1): 11.36, ("pay", 1): 11.39, ("x_x2t", 1): 11.48,
        ("x_logit", 1): 11.58, ("gate_exp", 1): 11.66, ("pick", 0, 1): 11.68, ("pick", 1, 1): 11.69,
        ("pick", 2, 1): 11.70, ("pick", 3, 1): 11.71, ("pick", 4, 1): 11.72, ("pick", 5, 1): 11.91,
        ("send", 0, 1): 12.19, ("x_count", 1): 12.27, ("send", 1, 1): 12.27, ("place", 0, 1): 12.28,
        ("place", 1, 1): 12.28, ("send", 2, 1): 12.38, ("send", 3, 1): 12.40,
    })

PHASES = (OPENING, LOOP, CLOSING)
MISC = ("out", "max", "q_proj", "k_proj", "v_proj", "s_ot", "s_oproj", "s_x1t", "s_xq",
        "x_ot", "x_oproj", "x_x2t", "x_logit", "x_count")


def _events(phase):
    at = dict(phase["at"])
    items = []
    exps = phase.get("before", [None, None]) + phase["exps"]
    for j, group in enumerate(exps, start=-2):
        if not group:
            continue
        if j >= 0:
            n = PAIRS[group[0]]
            start = at.pop(("pairs",) + group, j)
            items += [(start + (j + 1 - start) * u / n, ("pair", group, u)) for u in range(n)]
        if -1 <= j < len(phase["exps"]) - 1:
            pieces = VALUES[group[0]]
            start = at.pop(("values",) + group, j + 1 + 0.6 / pieces)
            items += [(start + p / pieces, ("values", group, p)) for p in range(pieces)]
            at.setdefault(("take",) + group, j + 1.99)
        if -2 <= j < len(phase["exps"]) - 2:
            at.setdefault(("out",) + group, j + 2.12)
    for group, (first, last) in phase["units"].items():
        n = UNITS[group[0]]
        items += [(first + (last - first) * (k + 0.9) / n, ("unit", group, k)) for k in range(n)]
        at.setdefault(("split",) + group, last - 0.005)
        if last + 0.25 < len(phase["exps"]):
            at.setdefault(("max",) + group, last + 0.25)
    items += [(place, what) for what, place in at.items()]
    events = [what for _, what in sorted(items, key=lambda i: i[0])]
    turn = exps + [group for group in phase["units"] if group not in exps]
    for name in ("pair", "values", "unit"):
        keys = [(turn.index(what[1]), what[2]) for what in events if what[0] == name]
        assert keys == sorted(keys), name
    for name in ("clear", "load_s", "load_expert", "pick", "place", "send"):
        keys = [what[:0:-1] for what in events if what[0] == name]
        assert keys == sorted(keys), name
    keys = [what[1] for what in events if what[0] in ("load_xkv", "load_x")]
    assert keys == sorted(keys) and all(events.index(("load_xkv", b)) < events.index(("load_x", b)) for b in keys)
    for name in ("split", "max", "take", "out"):
        keys = [turn.index(what[1:]) if what[1:] in turn else -1 for what in events if what[0] == name]
        assert keys == sorted(keys), name
    return events


EVENTS = [_events(phase) for phase in PHASES]


class Plan:

    def __init__(self):
        self.at, self.total = [], []
        for events in EVENTS:
            at, n = {}, {("misc", 0): 0, ("misc", 1): 0, "unit": 0, "pair": 0, "misc": 0, "values": 0, "turn": 0}
            for what in events:
                buffer = "misc" if what[0] in MISC else what[0]
                if buffer in n and not (buffer == "values" and what[2]):
                    at[what] = n[buffer]
                    if buffer == "misc":
                        bank = ("misc", n[buffer] % 2)
                        at[bank, what] = n[bank]
                        n[bank] += 1
                    n[buffer] += 1
                if what[0] == "out":
                    at["turn", what] = n["turn"]
                    n["turn"] += 1
            self.at.append(at)
            self.total.append(n)

    def before(self, phase, it, what, more=0):
        buffer = what[0] if isinstance(what[0], tuple) else "misc" if what[0] in MISC else what[0]
        n = [t[buffer] for t in self.total]
        here = self.at[phase][what] + more
        return (here, it * n[1] + (n[0] + here) if phase == 1 else None, n[0] + (B - 2) * n[1] + here)[phase]

    def turn(self, phase, it, what):
        return self.before(phase, it, ("turn", what))

    def bank(self, phase, what):
        return self.at[phase][what] % 2

    def reads(self, phase, it, what, more=0):
        return self.before(phase, it, (("misc", self.bank(phase, what)), what), more)

    def half(self, phase, what):
        assert all(t[what[0]] % 2 == 0 for t in self.total)
        return self.at[phase][what] % 2

    def batch(self, phase, it, b):
        return (b, it + b if phase == 1 else None, B - 2 + b)[phase]


def decoder(nc, a, out):
    plan = Plan()
    with ExitStack() as ctx:
        def sb(name, shape, dt=F32):
            return ctx.enter_context(nc.sbuf_tensor(name, shape, dt))

        def sem(name):
            return ctx.enter_context(nc.semaphore(name))

        def dram(name, shape, dt=F32):
            return nc.dram_tensor(name, shape, dt, kind="Internal").ap()

        q_d = dram("q_stack_d", (B, H, NR, S), BF16)
        k_d = dram("k_stack_d", (B, H, NR, S), BF16)
        v_d = dram("v_d", (B, P, NT * D))
        xq_d = dram("xq_stack_d", (H, NR, S), BF16)
        xk_d = dram("xk_stack_d", (H, NR, B * C), BF16)
        vx_d = dram("vx_d", (B, C, H * 32))
        x2_d = dram("x2_d", (B * S, D))
        slots_d = dram("slots_d", (E * CAP, ROW))
        y_d = dram("y_d", (2 * B * S, D))

        ident = sb("ident", [P, P])
        identb = sb("identb", [P, P], BF16)
        causal = sb("causal", [P, P], BF16)
        before_t = sb("before_t", [P, P], BF16)
        ones = sb("ones", [P, P], BF16)
        e_const = sb("e_const", [P, 3, NT, E])
        w_qkv = sb("w_qkv", [P, 3, D])
        w_o = sb("w_o", [P, D])
        wx = sb("wx", [P, 4, D])
        w_gate = sb("w_gate", [P, E])
        b_col = sb("b_col", [P, 2])
        bq_s = sb("bq_s", [P, 1])
        bv_row = sb("bv_row", [P, D])
        bo_row = sb("bo_row", [P, D])

        stack_q = {"s": sb("stack_q", [P, H, S], BF16), "x": sb("stack_xq", [P, H, S], BF16)}
        stack_k = {"s": sb("stack_k", [P, H, S], BF16), "x": sb("stack_xk", [P, H, P], BF16)}
        probs = {"s": sb("probs", [P, 2, 5, 2 * S]), "x": sb("probs_x", [P, 2, 2, 2 * S])}
        v_s = sb("v_s", [P, NT, H, 32])
        v_x = sb("v_x", [P, H, 32])
        v_tok = sb("v_tok", [P, NT, D])
        negmax = sb("negmax", [P, NG, G, NT])
        nm_parts = sb("nm_parts", [P, NG, 3, G * NT], BF16)
        nm_rows = sb("nm_rows", [3 * G * NT, NG, P], BF16)
        u_sb = sb("u_sb", [P, 2, S])
        rsum = sb("rsum", [P, 2, NT, G])
        o_tok = {k: sb(f"o_tok_{k}", [P, NT, D]) for k in "sx"}
        o_t = {k: sb(f"o_t_{k}", [P, S]) for k in "sx"}

        ctx_t = sb("ctx_t", [P, B * C])
        zeros = sb("zeros", [P, D])
        first_used = sb("first_used", [P, E])
        xq = sb("xq", [P, S])
        xq_parts = sb("xq_parts", [P, 3, S], BF16)

        qk = sb("qk", [P, 2, S])
        qk_parts = sb("qk_parts", [P, 3, 2, S], BF16)
        v_stage = sb("v_stage", [P, NT * D])

        early = probs["s"][:, 1].rearrange("p b c -> p (b c)")
        qk_first = early[:, 0:1024].rearrange("p (w s) -> p w s", w=2)
        parts_first = early[:, 1024:2560].bitcast(BF16).rearrange("p (c w s) -> p c w s", c=3, w=2)
        xk = early[:, 2560:2560 + B * C]
        xk_parts = early[:, 3072:3072 + 3 * B * C // 2].bitcast(BF16).rearrange("p (c n) -> p c n", c=3)
        early_x = probs["x"][:].rearrange("p a b c -> p (a b c)")
        x_t = early_x[:, 0:B * S]
        vx_all = early_x[0:C, B * S:B * S + B * H * 32].rearrange("p (b h n) -> p b h n", b=B, h=H)

        x_tok = sb("x_tok", [P, NT, D])
        r = {k: sb(f"r_{k}", [P, NT, D]) for k in "sx"}
        stats = {k: sb(f"stats_{k}", [P, NT, 6]) for k in "sx"}
        mv = {k: sb(f"mv_{k}", [P, NT, 2]) for k in "sx"}
        var_eps = {k: sb(f"var_eps_{k}", [P, NT]) for k in "sx"}
        rstd = {k: sb(f"rstd_{k}", [P, NT]) for k in "sx"}
        minus_half = sb("minus_half", [P, NT])
        x1 = sb("x1", [P, NT, D])
        x1_bias = sb("x1_bias", [P, NT, D])
        x1_t = sb("x1_t", [P, S])
        x2_t = sb("x2_t", [P, S])

        pay = sb("pay", [P, 2, NT, ROW])
        logit = sb("logit", [P, NT, E])
        prob = sb("prob", [P, NT, E])
        stat4 = sb("stat4", [P, 8, NT])
        pick = sb("pick", [P, NT, E])
        hot = sb("hot", [P, 2, NT, E])
        hotb = sb("hotb", [P, 2, NT, E], BF16)
        tile_base = sb("tile_base", [P, 2, NT + 1, E])
        pos = sb("pos", [P, 2, NT, E])
        used = sb("used", [P, 2, NT, E])
        slotf = sb("slotf", [P, 2, NT])
        slot = sb("slot", [P, 2, NT], U32)
        row_id = sb("row_id", [P, 2, NT])
        empty = sb("empty", [P, ROW])
        fin_stats = sb("fin_stats", [P, B, NT, 6])
        fin_mv = sb("fin_mv", [P, B, NT, 2])
        fin_rstd = sb("fin_rstd", [P, B, NT])
        fin_shift = sb("fin_shift", [P, B, NT])

        w1 = stack_q["s"][:].bitcast(F32).rearrange("p h s -> p (h s)").rearrange("p (e n) -> p e n", e=E)
        w2 = stack_k["s"][:].bitcast(F32).rearrange("p h s -> p (h s)").rearrange("p (e n) -> p e n", e=E)
        b1 = sb("b1", [P, E, NC])
        b2 = sb("b2", [P, E, D])
        yrow = sb("yrow", [P, E, 2], U32)
        flat = probs["s"][:].rearrange("p a b c -> p (a b c)")
        h_t = flat[:, 0:2 * NC * CAP].rearrange("p (i c s) -> p i c s", i=2, c=NC)
        xs = flat[:, 2048:2048 + E * 2 * ROW].rearrange("p (e t c) -> p e t c", e=E, t=2)
        xs_t = flat[:, 4224:4224 + E * CAP].rearrange("p (e s) -> p e s", e=E)
        yb = flat[:, 6272:6272 + 2 * 2 * D].rearrange("p (i t d) -> p i t d", i=2, t=2)
        ys = flat[:, 6784:6784 + E * 2 * D].rearrange("p (e t d) -> p e t d", e=E, t=2)
        free_x = (probs["x"][:].rearrange("p a b c -> p (a b c)"), stack_q["x"][:].bitcast(F32).rearrange("p h s -> p (h s)"))
        fin = [free_x[k // 2][:, B * S * (k % 2):B * S * (k % 2 + 1)].rearrange("p (b t d) -> p b t d", b=B, t=NT) for k in range(4)]

        p_unit = [ctx.enter_context(nc.psum_tensor(f"p_unit{i}", [P, S], F32)) for i in range(2)]
        p_exp = [ctx.enter_context(nc.psum_tensor(f"p_exp{i}", [P, S], F32)) for i in range(3)]
        p_out = ctx.enter_context(nc.psum_tensor("p_out", [P, S], F32))
        p_misc = [ctx.enter_context(nc.psum_tensor(f"p_misc{i}", [P, S], F32)) for i in range(2)]

        w_in, consts_in, later_in = sem("w_in"), sem("consts_in"), sem("later_in")
        rows_in = sem("rows_in")
        filled = sem("filled")
        vx_ready = sem("vx_ready")
        x_ready = sem("x_ready")
        small_ready = sem("small_ready")
        pool_fill = sem("pool_fill")
        zeros_set = sem("zeros_set")
        bq_ready = sem("bq_ready")
        xt_in = [sem(f"xt_in{b}") for b in range(B)]
        proj_filled = sem("proj_filled")
        q_read, k_read, v_read = sem("q_read"), sem("k_read"), sem("v_read")
        first_split = sem("first_split")
        high_done = sem("high_done")
        qk_split = sem("qk_split")
        parts_out = [sem(f"parts_out{b}") for b in range(B)]
        ctx_filled, ctx_read = sem("ctx_filled"), sem("ctx_read")
        ctx_split = sem("ctx_split")
        ctx_out = sem("ctx_out")
        stack_in = {k: [sem(f"stack_in_{k}{g}") for g in range(NG)] for k in "sx"}
        xkv_in = sem("xkv_in")
        tok_in = sem("tok_in")
        vtok_in = sem("vtok_in")
        v_put = sem("v_put")
        unit_filled, unit_read = sem("unit_filled"), sem("unit_read")
        nm_step = {k: sem(f"nm_step_{k}") for k in "sx"}
        max_in = {k: [sem(f"max_in_{k}{g}") for g in range(NG)] for k in "sx"}
        exp_filled, exp_read = sem("exp_filled"), sem("exp_read")
        masked = sem("masked")
        pv_done = {k: sem(f"pv_done_{k}") for k in "sx"}
        out_read = sem("out_read")
        misc_filled = sem("misc_filled")
        misc_read = [sem(f"misc_read{i}") for i in range(2)]
        norm_step = {k: sem(f"norm_step_{k}") for k in "sx"}
        ln_step = {k: sem(f"ln_step_{k}") for k in "sx"}
        ln_pow = {k: sem(f"ln_pow_{k}") for k in "sx"}
        ln_done = {k: sem(f"ln_done_{k}") for k in "sx"}
        bias_added = sem("bias_added")
        xq_read = sem("xq_read")
        xq_split = sem("xq_split")
        xq_out = sem("xq_out")
        route_step, route_exp = sem("route_step"), sem("route_exp")
        pay_copied = sem("pay_copied")
        x2_out, x2_in = sem("x2_out"), sem("x2_in")
        sent = sem("sent")
        slots_in = [sem(f"slots_in{k}") for k in range(NG)]
        we_in = [sem(f"we_in{e}") for e in range(E)]
        xs_filled, xs_read = sem("xs_filled"), sem("xs_read")
        h_filled, h_done = sem("h_filled"), sem("h_done")
        y_filled = sem("y_filled")
        y_step = sem("y_step")
        y_sent = sem("y_sent")
        fin_in = [sem(f"fin_in{b}") for b in range(B)]
        fin_added = sem("fin_added")
        fin_step, fin_pow = sem("fin_step"), sem("fin_pow")
        fin_ready, fin_out = sem("fin_ready"), sem("fin_out")
        held = sem("held")

        block = ctx.enter_context(nc.Block())

        SPLITS = 4
        LN_STEPS = 3
        HOT_STEP = 16
        PICK_STEP = 19
        ROUTE_STEPS = 31
        FIN_STEPS = 4
        ALL_FILLED = 3
        CONSTS = ((wx[:], a["wx_t"]), (ctx_t[:], a["ctx_t"]), (b_col[:], a["b_col"]), (identb[:], a["c_identb"]),
                  (causal[:], a["c_causal"]), (bv_row[:], a["bv"].partition_broadcast(P)))
        LATER_CONSTS = ((ident[:], a["c_ident"]), (w_o[:], a["w_o_t"]), (bo_row[:], a["bo"].partition_broadcast(P)),
                        (w_gate[:], a["w_gate"]), (before_t[:], a["c_before"]), (e_const[:], a["c_expert"]),
                        (row_id[:], a["c_row"]), (empty[:], a["c_empty"].partition_broadcast(P)))

        q_banks = p_exp + p_misc[1:]
        h_banks = (p_exp[0:2], [p_exp[2], p_misc[1]])

        def pair_parts(kind, u):
            if kind == "x":
                return [(2 * u + i, 0, i * S) for i in range(2)]
            if u < 2:
                return [(2 * u + i, 0, i * S) for i in range(2)]
            if u < 4:
                return [(2 * (u - 2) + i, t, i * S + at) for i in range(2) for t, at in ((3, 0), (1, P))]
            return [(i, 2, i * 2 * P) for i in range(4)]

        def prob_place(i, t):
            for u in range(PAIRS["s"]):
                for head, tile, at in pair_parts("s", u):
                    if (head, tile) == (i, t):
                        return u, at

        def hold(engine, sem, value):
            engine.wait_ge(sem, value)
            if not isinstance(value, int):
                engine.sem_inc(held, 1)

        def misc_done(engine, phase, it, what):
            hold(engine, misc_read[plan.bank(phase, what)], plan.reads(phase, it, what, 1))

        def load_stacks(sp, g, b):
            for stack, src in ((stack_q["s"], q_d), (stack_k["s"], k_d)):
                sp.dma_start(stack[0:NR, G * g:G * g + G, :],
                             src[b, G * g:G * g + G].rearrange("h r s -> r h s")).then_inc(stack_in["s"][g], 16)

        def store_runs(sp, which, dst, parts, done):
            rows = dst.rearrange("h (d n) s -> (h d) n s", n=PRODUCTS)
            for k, (first, many) in enumerate(RUNS):
                src = parts[:, 0:many, :] if which == 0 else parts[:, k, :].unsqueeze(1).broadcast_to([P, many, parts.shape[-1]])
                sp.dma_start(rows[:, first:first + many, :], src).then_inc(done, 16)

        def store_parts(sp, b, parts, order):
            for which in order:
                store_runs(sp, which, (q_d, k_d)[which][b], parts[:, :, which, :], parts_out[b])

        def split(engine, E, src, parts, sem, base):
            E.tensor_copy(parts[0], src).then_inc(sem, 1)
            hold(engine, sem, base + 1)
            E.tensor_tensor(src, src, parts[0], ALU.subtract).then_inc(sem, 1)
            hold(engine, sem, base + 2)
            E.tensor_copy(parts[1], src).then_inc(sem, 1)
            hold(engine, sem, base + 3)
            E.tensor_tensor(parts[2], src, parts[1], ALU.subtract).then_inc(sem, 1)

        def phases(engine, body):
            body(0, None)
            with engine.Fori(0, B - 2) as i:
                body(1, i)
            body(2, None)

        @block.sync
        def _(sp):
            for b in range(B):
                sp.dma_start(x_t[:, b * S:(b + 1) * S], a["x_t"][:, b * S:(b + 1) * S]).then_inc(xt_in[b], 16)
                if b == 0:
                    sp.dma_start(w_qkv[:], a["w_qkv_t"]).then_inc(w_in, 16)
            for dst, src in CONSTS[0:4]:
                sp.dma_start(dst, src).then_inc(consts_in, 16)
            hold(sp, filled, ALL_FILLED)
            sp.dma_start(stack_q["s"][ALIBI_ROW:ALIBI_ROW + 3], a["c_ones"]).then_inc(rows_in, 16)
            sp.dma_start(stack_k["s"][ALIBI_ROW:ALIBI_ROW + 3], a["c_alibi"]).then_inc(rows_in, 16)
            sp.dma_start(stack_k["s"][MAX_ROW:MAX_ROW + 3], a["c_ones"]).then_inc(rows_in, 16)
            for dst, src in CONSTS[4:]:
                sp.dma_start(dst, src).then_inc(consts_in, 16)
            for which in range(2):
                hold(sp, first_split, SPLITS * (which + 1))
                store_parts(sp, 0, parts_first, [which])
            hold(sp, parts_out[0], 16 * 2 * len(RUNS))
            for g in range(NG):
                load_stacks(sp, g, 0)
            for dst, src in LATER_CONSTS:
                sp.dma_start(dst, src).then_inc(later_in, 16)
            hold(sp, qk_split, 6)
            store_parts(sp, 1, qk_parts, range(2))
            hold(sp, v_read, 2)
            sp.dma_start(v_d[1], v_stage[:]).then_inc(parts_out[1], 16)
            sp.dma_start(x_tok[:], a["x"][0:S, :].rearrange("(t p) d -> p t d", p=P)).then_inc(tok_in, 16)
            hold(sp, ctx_split, SPLITS)
            store_runs(sp, 1, xk_d, xk_parts, ctx_out)
            hold(sp, ctx_read, 1 + B)
            sp.dma_start(vx_d.rearrange("b c n -> c b n"), vx_all.rearrange("c b h n -> c b (h n)")).then_inc(ctx_out, 16)

            def body(phase, it):
                at = lambda what, more=0: plan.before(phase, it, what, more)
                for what in EVENTS[phase]:
                    name, b = what[0], plan.batch(phase, it, what[-1] if isinstance(what[-1], int) else 0)
                    if name == "max":
                        kind, g = what[1:3]
                        misc_done(sp, phase, it, what)
                        sp.dma_start(stack_q[kind][MAX_ROW:MAX_ROW + 3, G * g:G * g + G, :].rearrange("c h (t q) -> c (h t) q", q=P),
                                     nm_rows[:, g, :]).then_inc(max_in[kind][g], 16)
                    if name == "load_s":
                        g = what[1]
                        if phase == 0:
                            if g == 0:
                                hold(sp, parts_out[1], 16 * (2 * len(RUNS) + 1))
                            hold(sp, exp_read, 2 * at(("pair", _s(g, 0), PAIRS["s"] - 1), 1))
                        elif g == 0:
                            hold(sp, exp_read, 2 * at(("pair", _x(0, 0), 0)))
                            for done in parts_out[2:]:
                                hold(sp, done, 16 * (2 * len(RUNS) + 1))
                        load_stacks(sp, g, b)
                    if name == "load_v":
                        hold(sp, v_put, NG * b)
                        sp.dma_start(v_tok[:].rearrange("p t d -> p (t d)"), v_d[b]).then_inc(vtok_in, 16)
                    if name == "qk_store":
                        hold(sp, qk_split, 6 * b)
                        store_parts(sp, b, qk_parts, range(2))
                        misc_done(sp, phase, it, ("v_proj", what[1]))
                        sp.dma_start(v_d[b], v_stage[:]).then_inc(parts_out[b], 16)
                    if name == "s_oproj" and phase < 2:
                        misc_done(sp, phase, it, what)
                        sp.dma_start(x_tok[:], a["x"][bass.ds((b + 1) * S, S), :].rearrange("(t p) d -> p t d", p=P)).then_inc(tok_in, 16)
                    if name == "xq_store":
                        hold(sp, xq_split, 3 * (b + 1))
                        store_runs(sp, 0, xq_d, xq_parts[:], xq_out)
                    if name == "load_xkv":
                        if phase == 0:
                            hold(sp, ctx_out, 16 * (len(RUNS) + 1))
                            hold(sp, x_ready, 3)
                            sp.dma_start(stack_k["x"][MAX_ROW:MAX_ROW + 3, :, 0:C], a["c_ones"][:, :, 0:C]).then_inc(rows_in, 16)
                        else:
                            hold(sp, pv_done["x"], NG * b)
                        sp.dma_start(stack_k["x"][0:NR, :, 0:C],
                                     xk_d[:, :, bass.ds(b * C, C)].rearrange("h r c -> r h c")).then_inc(xkv_in, 16)
                        sp.dma_start(v_x[0:C].rearrange("c h n -> c (h n)"), vx_d[b]).then_inc(xkv_in, 16)
                    if name == "load_x":
                        hold(sp, xq_out, 16 * len(RUNS) * (b + 1))
                        for g in range(NG):
                            sp.dma_start(stack_q["x"][0:NR, G * g:G * g + G, :],
                                         xq_d[G * g:G * g + G].rearrange("h r s -> r h s")).then_inc(stack_in["x"][g], 16)
                    if name == "load_expert":
                        e = what[1]
                        if e == 0:
                            hold(sp, exp_read, 2 * at(("pair", _x(0, 0), 0)))
                            sp.dma_start(b1[:], a["b1"]).then_inc(we_in[0], 16)
                            sp.dma_start(b2[:], a["b2"].partition_broadcast(P)).then_inc(we_in[0], 16)
                        sp.dma_start(w1[:, e, :], a["w1"][e]).then_inc(we_in[e], 16)
                        sp.dma_start(w2[:, e, :], a["w2"][e]).then_inc(we_in[e], 16)
                    if name == "pay":
                        hold(sp, ln_done["x"], b + 1)
                        sp.dma_start(x2_d[bass.ds(b * S, S), :].rearrange("(t p) d -> p t d", p=P),
                                     pay[:, 0, :, 0:D]).then_inc(x2_out, 16)

            phases(sp, body)

            hold(sp, sent, 16 * CLEARS + 16 * 2 * NT * B)
            for k in range(NG):
                sp.dma_start(xs[:, 2 * k:2 * k + 2].rearrange("p e t c -> p e (t c)"),
                             slots_d[2 * k * CAP:2 * (k + 1) * CAP, :].rearrange("(e p t) c -> p e (t c)", p=P, t=2)).then_inc(slots_in[k], 16)
            rows = lambda t, k, b: t[(k * B + b) * S:(k * B + b + 1) * S, :].rearrange("(p t) d -> p t d", p=P)
            hold(sp, x2_out, 16 * B)
            hold(sp, pv_done["x"], NG * B)
            for b in range(B):
                sp.dma_start(fin[0][:, b], rows(x2_d, 0, b)).then_inc(x2_in, 16)
            hold(sp, y_sent, 32 * E)
            for b in range(B):
                for k in range(2):
                    sp.dma_start(fin[1 + k][:, b], rows(y_d, k, b)).then_inc(fin_in[b], 16)
            for b in range(B):
                hold(sp, fin_ready, b + 1)
                sp.dma_start(rows(out, 0, b), fin[3][:, b]).then_inc(fin_out, 16)
            hold(sp, fin_out, 16 * B)

        @block.tensor
        def _(pe):
            def mm(dst, lhs, rhs, start=True, stop=True):
                return nc.tensor.matmul(dst, lhs, rhs, start=start, stop=stop)

            pe.wait_ge(w_in, 16)
            for b in range(2):
                pe.wait_ge(xt_in[b], 16)
                xb = x_t[:, b * S:(b + 1) * S]
                for which in range(2):
                    mm(q_banks[2 * b + which][:], w_qkv[:, which, :], xb).then_inc(proj_filled, 1)
                for t in range(NT):
                    last = mm(p_unit[b][:, t * D:(t + 1) * D], xb[:, t * P:(t + 1) * P], w_qkv[:, 2, :])
                last.then_inc(proj_filled, 1)
            pe.wait_ge(consts_in, 16 * len(CONSTS))
            mm(p_misc[0][:, 0:B * C], wx[:, 1, :], ctx_t[:]).then_inc(ctx_filled, 1)
            for b in range(B):
                last = mm(p_out[0:C, b * D:(b + 1) * D], ctx_t[:, b * C:(b + 1) * C], wx[:, 2, :])
            last.then_inc(ctx_filled, 1)
            pe.wait_ge(q_read, 2)
            pe.wait_ge(k_read, 2)
            pe.wait_ge(v_read, 2)
            pe.wait_ge(ctx_read, 1 + B)
            pe.wait_ge(filled, ALL_FILLED)
            pe.wait_ge(rows_in, 48)

            def unit(phase, it, what):
                _, (kind, g, rel), u = what
                n = plan.before(phase, it, what)
                if u == 0:
                    need = plan.batch(phase, it, rel) + 1
                    pe.wait_ge(stack_in[kind][g], (32 if kind == "s" else 16) * need)
                    if kind == "x":
                        pe.wait_ge(xkv_in, 32 * need)
                        if phase == 0:
                            pe.wait_ge(rows_in, 64)
                if not (phase == 0 and n < 2):
                    pe.wait_ge(unit_read, n - 1)
                bank = p_unit[plan.half(phase, what)]
                sq, sk = stack_q[kind], stack_k[kind]
                if kind == "x":
                    for i in range(G):
                        last = mm(bank[:, i * C:(i + 1) * C], sq[0:SCORE_ROWS, G * g + i, u * P:(u + 1) * P],
                                  sk[0:SCORE_ROWS, G * g + i, 0:C])
                else:
                    if u < 4:
                        parts = [(u, 3, 0)]
                    elif u < 8:
                        parts = [(u - 4, 2, 0), (u - 4, 0, 3 * P)]
                    else:
                        parts = [(2 * (u - 8), 1, 0), (2 * (u - 8) + 1, 1, 2 * P)]
                    for i, t, at in parts:
                        keys = (t + 1) * P
                        mm(bank[:, at:at + keys], sq[0:SCORE_ROWS, G * g + i, t * P:(t + 1) * P],
                           sk[0:SCORE_ROWS, G * g + i, 0:keys], stop=False)
                        last = mm(bank[:, at + t * P:at + keys], identb[:], causal[:], start=False)
                last.then_inc(unit_filled, 1)

            def pair(phase, it, what):
                _, (kind, g, rel), u = what
                n = plan.before(phase, it, what)
                if u == 0:
                    pe.wait_ge(max_in[kind][g], 16 * (plan.batch(phase, it, rel) + 1))
                sq, sk = stack_q[kind], stack_k[kind]
                for half in range(2):
                    fill = 2 * plan.at[phase][what] + half
                    if fill >= 3:
                        pe.wait_ge(exp_read, 2 * n + half - 2)
                    elif phase:
                        pe.wait_ge(exp_read, 2 * plan.before(phase, it, what, -plan.at[phase][what]))
                    bank = p_exp[fill % 3]
                    for i, t, at in pair_parts(kind, u):
                        if at // S == half:
                            h = G * g + i
                            last = mm(bank[:, at % S:at % S + (S - t * P)], sk[:, h, t * P:(t + 1) * P], sq[:, h, t * P:S])
                    last.then_inc(exp_filled, 1)

            def values(phase, it, what):
                _, (kind, g, rel), piece = what
                done = NG * plan.batch(phase, it, rel) + g
                if piece == 0:
                    if kind == "s":
                        pe.wait_ge(v_put, done + 1)
                    n = plan.before(phase, it, what)
                    if not (phase == 0 and n == 0):
                        pe.wait_ge(out_read, n)
                pr = probs[kind][:, g % 2]
                if kind == "x":
                    pe.wait_ge(exp_read, 2 * plan.before(phase, it, ("pair", what[1], PAIRS["x"] - 1), 1))
                    for i in range(G):
                        last = mm(p_out[32 * i:32 * i + 32, :], v_x[:, G * g + i, :],
                                  pr[:, i // 2, (i % 2) * S:(i % 2 + 1) * S])
                    last.then_inc(pv_done[kind], 1)
                    return
                t, pairs = ((0, 2), (1, 4), (3, 4), (2, 5))[piece]
                pe.wait_ge(masked, PAIRS["s"] * done + pairs)
                for i in range(G):
                    u, at = prob_place(i, t)
                    last = mm(p_out[32 * i:32 * i + 32, t * P:S], v_s[:, t, G * g + i, :],
                              pr[:, u, at:at + S - t * P], start=(piece == 0), stop=(piece == 3))
                if piece == 3:
                    last.then_inc(pv_done[kind], 1)

            def body(phase, it):
                for what in EVENTS[phase]:
                    name = what[0]
                    if name in ("unit", "pair", "values"):
                        {"unit": unit, "pair": pair, "values": values}[name](phase, it, what)
                    if name not in MISC:
                        continue
                    b = plan.batch(phase, it, what[-1])
                    bank = p_misc[plan.bank(phase, what)]
                    if not (phase == 0 and plan.at[phase][what] < 2):
                        pe.wait_ge(misc_read[plan.bank(phase, what)], plan.reads(phase, it, what))
                    source = {"s_ot": ("out", "s", NG - 1, what[-1]), "x_ot": ("out", "x", NG - 1, what[-1]), "s_oproj": ("s_ot", what[-1]),
                              "x_oproj": ("x_ot", what[-1]), "s_xq": ("s_x1t", what[-1]), "x_logit": ("x_x2t", what[-1])}.get(name)
                    if source:
                        pe.wait_ge(misc_read[plan.bank(phase, source)], plan.reads(phase, it, source, 1))
                    if phase == 0 and what == ("out",) + _s(0, 0):
                        pe.wait_ge(later_in, 16 * len(LATER_CONSTS))
                    if name == "out":
                        kind, g = what[1:3]
                        pe.wait_ge(out_read, plan.turn(phase, it, what) + 1)
                        for t in range(NT):
                            last = nc.tensor.transpose(bank[:, t * P:(t + 1) * P], u_sb[:, g % 2, t * P:(t + 1) * P], ident[:])
                    if name == "max":
                        kind, g = what[1:3]
                        hold(pe, nm_step[kind], SPLITS * (NG * b + g + 1))
                        last = nc.tensor.transpose(bank[0:3 * G * NT, 0:P // 2].bitcast(BF16),
                                                   nm_parts[:, g, :, :].rearrange("p c n -> p (c n)"), identb[:])
                    if name in ("q_proj", "k_proj"):
                        if name == "q_proj":
                            pe.wait_ge(xt_in[b], 16)
                        last = mm(bank[:], w_qkv[:, int(name == "k_proj"), :], x_t[:, b * S:(b + 1) * S])
                    if name == "v_proj":
                        for t in range(NT):
                            last = mm(bank[:, t * D:(t + 1) * D], x_t[:, b * S + t * P:b * S + (t + 1) * P], w_qkv[:, 2, :])
                    kind = name[0]
                    if name in ("s_ot", "x_ot"):
                        for t in range(NT):
                            last = nc.tensor.transpose(bank[:, t * P:(t + 1) * P], o_tok[kind][:, t, :], ident[:])
                    if name in ("s_oproj", "x_oproj"):
                        for t in range(NT):
                            last = mm(bank[:, t * D:(t + 1) * D], o_t[kind][:, t * P:(t + 1) * P],
                                      w_o[:] if kind == "s" else wx[:, 3, :])
                    if name == "s_x1t":
                        pe.wait_ge(ln_done["s"], b + 1)
                        for t in range(NT):
                            last = nc.tensor.transpose(bank[:, t * P:(t + 1) * P], x1[:, t, :], ident[:])
                    if name == "s_xq":
                        last = mm(bank[:], wx[:, 0, :], x1_t[:])
                    if name == "x_x2t":
                        pe.wait_ge(ln_done["x"], b + 1)
                        for t in range(NT):
                            last = nc.tensor.transpose(bank[:, t * P:(t + 1) * P], pay[:, 0, t, 0:D], ident[:])
                    if name == "x_logit":
                        for t in range(NT):
                            last = mm(bank[:, t * E:(t + 1) * E], x2_t[:, t * P:(t + 1) * P], w_gate[:])
                    if name == "x_count":
                        pe.wait_ge(route_step, ROUTE_STEPS * b + HOT_STEP)
                        chosen = hotb[:].rearrange("p k t e -> p (k t e)")
                        mm(bank[:, 0:2 * NT * E], before_t[:], chosen)
                        last = mm(bank[:, 2 * NT * E:4 * NT * E], ones[:], chosen)
                    last.then_inc(misc_filled, 1)

            phases(pe, body)

            def tokens(e):
                if e % 2 == 0:
                    pe.wait_ge(slots_in[e // 2], 16)
                if e >= 2:
                    pe.wait_ge(xs_read, e - 1)
                for t in range(2):
                    last = nc.tensor.transpose(p_unit[e % 2][:, t * P:(t + 1) * P], xs[:, e, t, 0:D], ident[:])
                last.then_inc(xs_filled, 1)

            def hidden(e):
                pe.wait_ge(xs_read, e + 1)
                pe.wait_ge(we_in[e], 64 if e == 0 else 32)
                if e >= 2:
                    pe.wait_ge(h_done, NC * (e - 1))
                for c in range(NC):
                    mm(h_banks[e % 2][c // 2][:, c % 2 * CAP:(c % 2 + 1) * CAP], w1[:, e, c * P:(c + 1) * P], xs_t[:, e, :]).then_inc(h_filled, 1)

            def result(e):
                bank = (p_out, p_misc[0])[e % 2]
                pe.wait_ge(h_done, NC * (e + 1))
                if e >= 2:
                    pe.wait_ge(y_step, 2 * (e - 2) + 1)
                for t in range(2):
                    for c in range(NC):
                        last = mm(bank[:, t * D:(t + 1) * D], h_t[:, e % 2, c, t * P:(t + 1) * P], w2[:, e, c * D:(c + 1) * D],
                                  start=(c == 0), stop=(c == NC - 1))
                last.then_inc(y_filled, 1)

            for bank in range(2):
                last_fill = [w for w in EVENTS[2] if w[0] in MISC and plan.bank(2, w) == bank][-1]
                pe.wait_ge(misc_read[bank], plan.reads(2, None, last_fill, 1))
            tokens(0)
            tokens(1)
            hidden(0)
            for e in range(E):
                if e + 2 < E:
                    tokens(e + 2)
                if e + 1 < E:
                    hidden(e + 1)
                result(e)

        @block.scalar
        def _(act):
            for b in range(2):
                act.wait_ge(proj_filled, 3 * b + 1)
                nc.scalar.mul((qk_first if b == 0 else qk)[:, 0, :], q_banks[2 * b][:], SCALE).then_inc(q_read, 1)
                act.wait_ge(proj_filled, 3 * b + 2)
                nc.scalar.copy((qk_first if b == 0 else qk)[:, 1, :], q_banks[2 * b + 1][:]).then_inc(k_read, 1)
                if b:
                    act.wait_ge(q_read, 2)
                    act.wait_ge(k_read, 2)
                    nc.scalar.copy(qk_parts[:, 0], qk[:]).then_inc(high_done, 1)
                act.wait_ge(proj_filled, 3 * b + 3)
                nc.scalar.copy(v_tok[:].rearrange("p t d -> p (t d)") if b == 0 else v_stage[:], p_unit[b][:]).then_inc(v_read, 1)
            act.wait_ge(consts_in, 16 * len(CONSTS))
            nc.scalar.mul(bq_s[:], b_col[:, 0:1], SCALE).then_inc(bq_ready, 1)
            act.wait_ge(ctx_filled, 1)
            act.wait_ge(bq_ready, 1)
            nc.scalar.activation(xk, p_misc[0][:, 0:B * C], ACT.Identity, bias=b_col[:, 1:2]).then_inc(ctx_read, 1)
            act.wait_ge(parts_out[0], 16 * 2 * len(RUNS))

            def body(phase, it):
                for what in EVENTS[phase]:
                    name = what[0]
                    if name == "pair":
                        kind, g, _ = what[1]
                        if phase == 0 and what == ("pair", _s(1, 0), 0):
                            act.wait_ge(ctx_out, 16 * (len(RUNS) + 1))
                        for half in range(2):
                            act.wait_ge(exp_filled, 2 * plan.before(phase, it, what) + half + 1)
                            nc.scalar.activation(probs[kind][:, g % 2, what[2], half * S:(half + 1) * S],
                                                 p_exp[(2 * plan.at[phase][what] + half) % 3][:], ACT.Exp).then_inc(exp_read, 1)
                        continue
                    b = plan.batch(phase, it, what[-1])
                    if name in MISC:
                        bank, done = p_misc[plan.bank(phase, what)], misc_read[plan.bank(phase, what)]
                    if name == "take":
                        kind, g = what[1:3]
                        act.wait_ge(pv_done[kind], NG * b + g + 1)
                        nc.scalar.copy(u_sb[:, g % 2, :], p_out[:]).then_inc(out_read, 1)
                    if name == "max":
                        act.wait_ge(misc_filled, plan.before(phase, it, what, 1))
                        nc.scalar.copy(nm_rows[:, what[2], :], bank[0:3 * G * NT, 0:P // 2].bitcast(BF16)).then_inc(done, 1)
                    if name in ("q_proj", "k_proj"):
                        which = int(name == "k_proj")
                        act.wait_ge(misc_filled, plan.before(phase, it, what, 1))
                        if which == 0:
                            act.wait_ge(qk_split, 6 * (b - 1))
                            act.wait_ge(parts_out[b - 1], 16 * (2 * len(RUNS) + 1))
                            nc.scalar.mul(qk[:, 0, :], bank[:], SCALE).then_inc(q_read, 1)
                        else:
                            nc.scalar.copy(qk[:, 1, :], bank[:]).then_inc(k_read, 1)
                        act.wait_ge((q_read, k_read)[which], b + 1)
                        nc.scalar.copy(qk_parts[:, 0, which, :], qk[:, which, :]).then_inc(done, 1)
                    if name == "v_proj":
                        act.wait_ge(misc_filled, plan.before(phase, it, what, 1))
                        nc.scalar.copy(v_stage[:], bank[:]).then_inc(done, 1)
                    if name in ("s_ot", "x_ot", "s_x1t", "x_x2t"):
                        dst = {"s_ot": o_t["s"], "x_ot": o_t["x"], "s_x1t": x1_t, "x_x2t": x2_t}[name]
                        act.wait_ge(misc_filled, plan.before(phase, it, what, 1))
                        nc.scalar.copy(dst[:], bank[:]).then_inc(done, 1)
                    if name == "s_xq":
                        act.wait_ge(misc_filled, plan.before(phase, it, what, 1))
                        if phase:
                            act.wait_ge(xq_split, 3 * b)
                            act.wait_ge(xq_out, 16 * len(RUNS) * b)
                        nc.scalar.activation(xq[:], bank[:], ACT.Identity, bias=bq_s[:], scale=SCALE).then_inc(xq_read, 1)
                        act.wait_ge(xq_read, b + 1)
                        nc.scalar.copy(xq_parts[:, 0], xq[:]).then_inc(done, 1)
                    if name == "gate_exp":
                        gate = ("x_logit", what[1])
                        act.wait_ge(misc_read[plan.bank(phase, gate)], plan.reads(phase, it, gate, 1))
                        nc.scalar.activation(prob[:], logit[:], ACT.Exp).then_inc(route_exp, 1)

            phases(act, body)

            for e in range(E):
                i = e % 2
                if e == 0:
                    act.wait_ge(we_in[0], 64)
                if e >= 2:
                    act.wait_ge(y_filled, e - 1)
                for c in range(NC):
                    act.wait_ge(h_filled, NC * e + 2 * (c // 2) + 2)
                    nc.scalar.activation(h_t[:, i, c, :], h_banks[i][c // 2][:, c % 2 * CAP:(c % 2 + 1) * CAP], ACT.Gelu_apprx_tanh,
                                         bias=b1[:, e, c:c + 1]).then_inc(h_done, 1)

            for b in range(B):
                act.wait_ge(fin_pow, 2 * (b + 1))
                for t in range(NT):
                    last = nc.scalar.activation(fin[3][:, b, t, :], fin[0][:, b, t, :], ACT.Identity,
                                                bias=fin_shift[:, b, t:t + 1], scale=fin_rstd[:, b, t:t + 1])
                last.then_inc(fin_ready, 1)

        @block.vector
        def _(dve):
            nc.vector.memset(ones[:], 1.0).then_inc(filled, 1)
            nc.vector.memset(stack_k["s"][:].bitcast(F32), 0.0).then_inc(filled, 1)

            def split_rest(b, which):
                src, parts, base = qk[:, which], qk_parts[:, :, which], 6 * (b - 1) + 3 * which
                nc.vector.tensor_tensor(src, src, parts[:, 0], ALU.subtract).then_inc(qk_split, 1)
                dve.wait_ge(qk_split, base + 1)
                nc.vector.tensor_copy(parts[:, 1], src).then_inc(qk_split, 1)
                dve.wait_ge(qk_split, base + 2)
                nc.vector.tensor_tensor(parts[:, 2], src, parts[:, 1], ALU.subtract).then_inc(qk_split, 1)

            for which in range(2):
                dve.wait_ge((q_read, k_read)[which], 1)
                split(dve, nc.vector, qk_first[:, which], [parts_first[:, c, which] for c in range(3)], first_split, SPLITS * which)
            dve.wait_ge(high_done, 1)
            split_rest(1, 0)
            split_rest(1, 1)
            nc.vector.memset(zeros[:], 0.0).then_inc(zeros_set, 1)
            dve.wait_ge(ctx_read, 1)
            split(dve, nc.vector, xk, [xk_parts[:, c, :] for c in range(3)], ctx_split, 0)
            dve.wait_ge(ctx_filled, 2)
            dve.wait_ge(vx_ready, 1)
            dve.wait_ge(consts_in, 16 * len(CONSTS))
            for b in range(B):
                nc.vector.tensor_tensor(vx_all[:, b, :, 0:HD], p_out[0:C, b * D:(b + 1) * D].rearrange("c (h d) -> c h d", d=HD),
                                        bv_row[0:C].rearrange("c (h d) -> c h d", d=HD), ALU.add).then_inc(ctx_read, 1)
            nc.vector.memset(stack_k["x"][:].bitcast(F32), 0.0).then_inc(x_ready, 1)

            def spread(kind, b):
                step, base = ln_step[kind], LN_STEPS * b
                for t in range(NT):
                    last = nc.vector.bn_stats(stats[kind][:, t, :], r[kind][:, t, :])
                last.then_inc(step, 1)
                hold(dve, step, base + 1)
                for t in range(NT):
                    last = nc.vector.bn_aggr(mv[kind][:, t, :], stats[kind][:, t, :])
                last.then_inc(step, 1)
                dve.wait_ge(step, base + 2)
                nc.vector.tensor_scalar(var_eps[kind][:], mv[kind][:, :, 1], EPS, None, ALU.add).then_inc(step, 1)

            def norm(kind, b, put):
                dve.wait_ge(ln_pow[kind], b + 1)
                for t in range(NT):
                    last = nc.vector.tensor_scalar(put(t), r[kind][:, t, :], mv[kind][:, t, 0:1], rstd[kind][:, t:t + 1],
                                                   ALU.subtract, ALU.mult)
                last.then_inc(ln_done[kind], 1)

            def weigh(e):
                i = e % 2
                dve.wait_ge(y_filled, e + 1)
                nc.vector.tensor_tensor(yb[:, i], (p_out, p_misc[0])[i][:, 0:2 * D].rearrange("p (t d) -> p t d", t=2),
                                        b2[:, e, :].unsqueeze(1).broadcast_to([P, 2, D]), ALU.add).then_inc(y_step, 1)
                dve.wait_ge(y_step, 2 * e + 1)
                for t in range(2):
                    last = nc.vector.tensor_scalar(ys[:, e, t, :], yb[:, i, t, :], xs[:, e, t, D:D + 1], None, ALU.mult)
                last.then_inc(y_step, 1)

            def route(phase, it, part, n, rel):
                k = [{"x_logit": [0], "pick": [1, 4, 7, 10, 13, HOT_STEP], "x_count": [PICK_STEP], "place": [PICK_STEP + 4, PICK_STEP + 7]}[part][n]]
                bx = plan.batch(phase, it, rel)

                def ready():
                    dve.wait_ge(route_step, ROUTE_STEPS * bx + k[0])

                def step(ins, last=False):
                    k[0] += 1
                    ins.then_inc(route_step, 1)
                    if not last:
                        ready()

                def per_token(t):
                    return t.unsqueeze(2).broadcast_to([P, NT, E])

                V = nc.vector
                if part in MISC:
                    bank, done = p_misc[plan.bank(phase, (part, rel))], misc_read[plan.bank(phase, (part, rel))]
                    dve.wait_ge(misc_filled, plan.before(phase, it, (part, rel), 1))
                if part != "x_logit":
                    ready()
                choice = int(n >= 3)
                if part == "x_logit":
                    lg = bank[:, 0:NT * E].rearrange("p (t e) -> p t e", e=E)
                    step(V.tensor_reduce(stat4[:, 0, :], lg, X_AXIS, ALU.max, negate=True))
                    V.tensor_tensor(logit[:], lg, per_token(stat4[:, 0, :]), ALU.add).then_inc(done, 1)
                if (part, n) == ("pick", 0):
                    dve.wait_ge(route_exp, bx + 1)
                    step(V.tensor_reduce(stat4[:, 1, :], prob[:], X_AXIS, ALU.add))
                    step(V.reciprocal(stat4[:, 2, :], stat4[:, 1, :]))
                    step(V.tensor_tensor(prob[:], prob[:], per_token(stat4[:, 2, :]), ALU.mult), last=True)
                if part == "pick" and n in (1, 3):
                    step(V.tensor_reduce(stat4[:, 3 + choice, :], prob[:], X_AXIS, ALU.max))
                    step(V.tensor_tensor(pick[:], prob[:], per_token(stat4[:, 3 + choice, :]), ALU.is_equal))
                    step(V.tensor_tensor(pick[:], pick[:], e_const[:, 0], ALU.mult), last=True)
                if part == "pick" and n in (2, 4):
                    step(V.tensor_reduce(stat4[:, 5, :], pick[:], X_AXIS, ALU.max))
                    step(V.tensor_tensor(hot[:, choice], pick[:], per_token(stat4[:, 5, :]), ALU.is_equal))
                    if choice == 0:
                        step(V.scalar_tensor_tensor(prob[:], hot[:, 0], -2.0, prob[:], ALU.mult, ALU.add), last=True)
                    else:
                        step(V.tensor_copy(hotb[:], hot[:]), last=True)
                        assert k[0] == HOT_STEP
                if (part, n) == ("pick", 5):
                    step(V.tensor_tensor(stat4[:, 6, :], stat4[:, 3, :], stat4[:, 4, :], ALU.add))
                    step(V.tensor_scalar(stat4[:, 6, :], stat4[:, 6, :], 1e-9, None, ALU.add))
                    step(V.reciprocal(stat4[:, 7, :], stat4[:, 6, :]))
                    for c in range(2):
                        V.tensor_tensor(pay[:, c, :, D], stat4[:, 3 + c, :], stat4[:, 7, :], ALU.mult)
                        V.tensor_copy(pay[:, c, :, D + 1], row_id[:, c, :])
                    assert k[0] == PICK_STEP
                if part == "x_count":
                    cum = bank[:, 0:2 * NT * E].rearrange("p (k t e) -> p k t e", k=2, t=NT)
                    tot = bank[:, 2 * NT * E:4 * NT * E].rearrange("p (k t e) -> p k t e", k=2, t=NT)
                    for t in range(NT):
                        step(V.tensor_tensor(tile_base[:, :, t + 1, :], tot[:, :, t, :], tile_base[:, :, t, :], ALU.add))
                    V.tensor_tensor(pos[:], cum, tile_base[:, :, 0:NT, :], ALU.add).then_inc(done, 1)
                if (part, n) == ("place", 0):
                    count = ("x_count", rel)
                    dve.wait_ge(misc_read[plan.bank(phase, count)], plan.reads(phase, it, count, 1))
                    step(V.tensor_scalar(first_used[:], tile_base[:, 0, NT, :], float(CAP), None, ALU.min))
                    V.tensor_scalar(used[:, 0], pos[:, 0], float(CAP), DROPPED, ALU.is_ge, ALU.mult)
                    step(V.tensor_tensor(used[:, 1], pos[:, 1], first_used[:].unsqueeze(1).broadcast_to([P, NT, E]), ALU.add))
                    V.tensor_tensor(used[:, 0], used[:, 0], pos[:, 0], ALU.add)
                    step(V.tensor_scalar(used[:, 1], used[:, 1], float(CAP), DROPPED, ALU.is_ge, ALU.mult), last=True)
                if (part, n) == ("place", 1):
                    step(V.tensor_tensor(used[:, 1], used[:, 1], pos[:, 1], ALU.subtract))
                    step(V.tensor_tensor(used[:], used[:], e_const[:, 1:3], ALU.add))
                    step(V.tensor_tensor(used[:], used[:], hot[:], ALU.mult))
                    step(V.tensor_reduce(slotf[:], used[:], X_AXIS, ALU.add))
                    step(V.tensor_copy(slot[:], slotf[:]), last=True)
                    V.tensor_copy(tile_base[:, :, 0, :], tile_base[:, :, NT, :])
                    V.tensor_scalar(row_id[:], row_id[:], float(S), None, ALU.add)
                    assert k[0] == ROUTE_STEPS, k[0]

            dve.wait_ge(small_ready, 1)

            def body(phase, it):
                for what in EVENTS[phase]:
                    name = what[0]
                    if name == "unit":
                        (kind, g, _), u = what[1:]
                        nm = negmax[:, g]
                        dve.wait_ge(unit_filled, plan.before(phase, it, what, 1))
                        bank = p_unit[plan.half(phase, what)]
                        if kind == "x":
                            last = nc.vector.tensor_reduce(nm[:, :, u], bank[:, 0:G * C].rearrange("p (i c) -> p i c", c=C), X_AXIS, ALU.max, negate=True)
                        elif u < 4:
                            last = nc.vector.tensor_reduce(nm[:, u, 3:4], bank[:], X_AXIS, ALU.max, negate=True)
                        elif u < 8:
                            nc.vector.tensor_reduce(nm[:, u - 4, 2:3], bank[:, 0:3 * P], X_AXIS, ALU.max, negate=True)
                            last = nc.vector.tensor_reduce(nm[:, u - 4, 0:1], bank[:, 3 * P:], X_AXIS, ALU.max, negate=True)
                        else:
                            last = nc.vector.tensor_reduce(nm[:, 2 * (u - 8):2 * (u - 8) + 2, 1], bank[:].rearrange("p (i c) -> p i c", i=2), X_AXIS, ALU.max, negate=True)
                        last.then_inc(unit_read, 1)
                        continue
                    if name in ("pair", "values"):
                        continue
                    b = plan.batch(phase, it, what[-1])
                    if name in MISC:
                        bank, done = p_misc[plan.bank(phase, what)], misc_read[plan.bank(phase, what)]
                    if name == "out":
                        kind, g = what[1:3]
                        dve.wait_ge(misc_filled, plan.before(phase, it, what, 1))
                        u = bank[:].rearrange("p (t i n) -> p t i n", t=NT, i=G)
                        nc.vector.reciprocal(rsum[:, g % 2], u[:, :, :, HD]).then_inc(norm_step[kind], 1)
                        dve.wait_ge(norm_step[kind], NG * b + g + 1)
                        nc.vector.tensor_tensor(o_tok[kind][:, :, G * HD * g:G * HD * (g + 1)].rearrange("p t (i d) -> p t i d", i=G),
                                                u[:, :, :, 0:HD], rsum[:, g % 2].unsqueeze(3).broadcast_to([P, NT, G, HD]),
                                                ALU.mult).then_inc(done, 1)
                    if name in ("s_oproj", "x_oproj"):
                        kind = name[0]
                        if phase == 0:
                            dve.wait_ge(later_in, 16 * len(LATER_CONSTS))
                        dve.wait_ge(misc_filled, plan.before(phase, it, what, 1))
                        if kind == "s":
                            dve.wait_ge(tok_in, 16 * (b + 1))
                        else:
                            dve.wait_ge(bias_added, b + 1)
                        nc.vector.tensor_tensor(r[kind][:].rearrange("p t d -> p (t d)"), bank[:],
                                                (x_tok if kind == "s" else x1_bias)[:].rearrange("p t d -> p (t d)"),
                                                ALU.add).then_inc(done, 1)
                        dve.wait_ge(done, plan.reads(phase, it, what, 1))
                        spread(kind, b)
                    if name == "qk_split":
                        source = (("q_proj", "k_proj")[what[1]], what[2])
                        dve.wait_ge(misc_read[plan.bank(phase, source)], plan.reads(phase, it, source, 1))
                        split_rest(b, what[1])
                    if name == "xq_split":
                        source = ("s_xq", what[1])
                        dve.wait_ge(misc_read[plan.bank(phase, source)], plan.reads(phase, it, source, 1))
                        base = 3 * b
                        nc.vector.tensor_tensor(xq[:], xq[:], xq_parts[:, 0], ALU.subtract).then_inc(xq_split, 1)
                        dve.wait_ge(xq_split, base + 1)
                        nc.vector.tensor_copy(xq_parts[:, 1], xq[:]).then_inc(xq_split, 1)
                        dve.wait_ge(xq_split, base + 2)
                        nc.vector.tensor_tensor(xq_parts[:, 2], xq[:], xq_parts[:, 1], ALU.subtract).then_inc(xq_split, 1)
                    if name == "norm":
                        if what[1] == "s":
                            if phase:
                                hold(dve, bias_added, b)
                            norm("s", b, lambda t: x1[:, t, :])
                        else:
                            dve.wait_ge(sent, 16 * CLEARS + 16 * 2 * NT * b)
                            norm("x", b, lambda t: pay[:, 0, t, 0:D])
                    if name in ("x_logit", "pick", "x_count", "place"):
                        route(phase, it, name, what[1] if len(what) == 3 else 0, what[-1])

            phases(dve, body)

            for e in range(E):
                dve.wait_ge(xs_filled, e + 1)
                nc.vector.tensor_copy(xs_t[:, e, :], p_unit[e % 2][:, 0:CAP]).then_inc(xs_read, 1)
                if e % 2 == 0:
                    nc.vector.tensor_copy(yrow[:, e:e + 2, :], xs[:, e:e + 2, :, D + 1])
                if e >= 2:
                    weigh(e - 2)
            weigh(E - 2)
            weigh(E - 1)

            dve.wait_ge(x2_in, 16 * B)
            for b in range(B):
                dve.wait_ge(fin_added, b + 1)
                nc.vector.tensor_tensor(fin[0][:, b], fin[0][:, b], fin[1][:, b], ALU.add).then_inc(fin_step, 1)
                dve.wait_ge(fin_step, FIN_STEPS * b + 1)
                for t in range(NT):
                    last = nc.vector.bn_stats(fin_stats[:, b, t, :], fin[0][:, b, t, :])
                last.then_inc(fin_step, 1)
                dve.wait_ge(fin_step, FIN_STEPS * b + 2)
                for t in range(NT):
                    last = nc.vector.bn_aggr(fin_mv[:, b, t, :], fin_stats[:, b, t, :])
                last.then_inc(fin_step, 1)
                dve.wait_ge(fin_step, FIN_STEPS * b + 3)
                nc.vector.tensor_scalar(fin_shift[:, b], fin_mv[:, b, :, 0], -1.0, None, ALU.mult)
                nc.vector.tensor_scalar(fin_rstd[:, b], fin_mv[:, b, :, 1], EPS, None, ALU.add).then_inc(fin_step, 1)

        @block.gpsimd
        def _(pool):
            g_ = nc.gpsimd
            g_.memset(stack_q["s"][:].bitcast(F32), 0.0).then_inc(filled, 1)
            g_.memset(minus_half[:], -0.5)
            g_.memset(tile_base[:], 0.0).then_inc(small_ready, 1)
            g_.memset(vx_all, 0.0).then_inc(pool_fill, 1)
            g_.memset(v_s[:], 0.0).then_inc(pool_fill, 1)
            hold(pool, pool_fill, 1)
            g_.memset(vx_all[:, :, :, HD], 1.0).then_inc(vx_ready, 1)
            hold(pool, pool_fill, 2)
            g_.memset(v_s[:, :, :, HD], 1.0)

            g_.memset(stack_q["x"][:].bitcast(F32), 0.0).then_inc(x_ready, 1)
            g_.memset(v_x[:], 0.0).then_inc(x_ready, 1)

            def body(phase, it):
                for what in EVENTS[phase]:
                    name = what[0]
                    if name == "pair" and what[1][0] == "s":
                        _, (kind, g, rel), u = what
                        b = plan.batch(phase, it, rel)
                        if u == 0:
                            if phase == 0 and rel == 0:
                                hold(pool, v_read, 1)
                            else:
                                hold(pool, vtok_in, 16 * b)
                                hold(pool, pv_done["s"], NG * (b - 1) + g + 1)
                            g_.tensor_copy(v_s[:, :, G * g:G * g + G, 0:HD],
                                           v_tok[:, :, G * HD * g:G * HD * (g + 1)].rearrange("p t (i d) -> p t i d", i=G)).then_inc(v_put, 1)
                        hold(pool, exp_read, 2 * plan.before(phase, it, what, 1))
                        pr = probs["s"][:, g % 2, u, :]
                        if u < 2:
                            view, pattern = pr.rearrange("p (i n) -> p i n", i=2)[:, :, 0:P], [[0, 2], [1, P]]
                        elif u < 4:
                            view, pattern = pr.rearrange("p (i n) -> p i n", i=2)[:, :, 0:2 * P], [[0, 2], [0, 2], [1, P]]
                        else:
                            view, pattern = pr.rearrange("p (i n) -> p i n", i=4)[:, :, 0:P], [[0, 4], [1, P]]
                        g_.affine_select(out=view, in_=view, compare_op=ALU.is_ge, fill=0.0, base=0,
                                         pattern=pattern, channel_multiplier=-1).then_inc(masked, 1)
                    if name in ("pair", "unit", "values"):
                        continue
                    b = plan.batch(phase, it, what[-1])
                    if name == "split":
                        kind, g = what[1:3]
                        hold(pool, unit_read, plan.before(phase, it, ("unit", what[1:], UNITS[kind] - 1), 1))
                        split(pool, g_, negmax[:, g].rearrange("p i t -> p (i t)"), [nm_parts[:, g, c, :] for c in range(3)],
                              nm_step[kind], SPLITS * (NG * b + g))
                    if name == "clear":
                        k = what[1]
                        if k == 0:
                            hold(pool, later_in, 16 * len(LATER_CONSTS))
                            hold(pool, zeros_set, 1)
                        dst, src = (slots_d, empty) if k < 2 else (y_d, zeros)
                        n, part = (2, k) if k < 2 else (CLEARS - 2, k - 2)
                        dst = dst.rearrange("(n t p) c -> n p t c", n=n, p=P)[part]
                        pool.dma_start(dst, src[:].unsqueeze(1).broadcast_to(list(dst.shape))).then_inc(sent, 16)
                    if name == "root":
                        kind = what[1]
                        hold(pool, ln_step[kind], LN_STEPS * (b + 1))
                        g_.tensor_tensor(rstd[kind][:], var_eps[kind][:], minus_half[:], ALU.pow).then_inc(ln_pow[kind], 1)
                    if name == "bias":
                        if phase:
                            misc_done(pool, phase, it, ("x_oproj", what[1] - 1))
                        hold(pool, ln_done["s"], b + 1)
                        g_.tensor_tensor(x1_bias[:], x1[:], bo_row[:].unsqueeze(1).broadcast_to([P, NT, D]), ALU.add).then_inc(bias_added, 1)
                    if name == "pay":
                        hold(pool, ln_done["x"], b + 1)
                        g_.tensor_copy(pay[:, 1, :, 0:D], pay[:, 0, :, 0:D]).then_inc(pay_copied, 1)
                    if name == "send":
                        n = what[1]
                        if n == 0:
                            hold(pool, pay_copied, b + 1)
                            hold(pool, route_step, ROUTE_STEPS * (b + 1))
                            hold(pool, x2_out, 16 * (b + 1))
                            hold(pool, sent, 16 * CLEARS + 16 * 2 * NT * b)
                        for t in (n % 2 * 2, n % 2 * 2 + 1):
                            g_.indirect_dma_start(slots_d, bass.IndirectOffsetOnAxis(ap=slot[:, n // 2, t:t + 1], axis=0),
                                                  pay[:, n // 2, t, :], None, bounds_check=E * CAP - 1,
                                                  oob_is_err=False).then_inc(sent, 16)

            phases(pool, body)

            for e in range(E):
                hold(pool, y_step, 2 * (e + 1))
                for t in range(2):
                    g_.indirect_dma_start(y_d, bass.IndirectOffsetOnAxis(ap=yrow[:, e, t:t + 1], axis=0),
                                          ys[:, e, t, :], None, bounds_check=2 * B * S - 1,
                                          oob_is_err=False).then_inc(y_sent, 16)

            def last_root(b):
                hold(pool, fin_step, FIN_STEPS * (b + 1))
                g_.tensor_tensor(fin_rstd[:, b], fin_rstd[:, b], minus_half[:], ALU.pow).then_inc(fin_pow, 1)
                hold(pool, fin_pow, 2 * b + 1)
                g_.tensor_tensor(fin_shift[:, b], fin_shift[:, b], fin_rstd[:, b], ALU.mult).then_inc(fin_pow, 1)

            for b in range(B):
                hold(pool, fin_in[b], 32)
                g_.tensor_tensor(fin[1][:, b], fin[1][:, b], fin[2][:, b], ALU.add).then_inc(fin_added, 1)
                if b:
                    last_root(b - 1)
            last_root(B - 1)


def _constants():
    def bf16_bits(v):
        return (np.ascontiguousarray(v, np.float32).view(np.uint32) >> 16).astype(np.uint16)

    ident = np.eye(P, dtype=np.float32)
    row = np.arange(P)
    start = 2.0 ** (-2.0 ** (-(math.log2(H) - 3)))
    slopes = np.asarray([start * start ** i for i in range(H)], np.float32)
    alibi = -(slopes[:, None] * np.arange(S, dtype=np.float32)[None, :])
    parts = []
    rest = alibi
    for _ in range(3):
        parts.append(bf16_bits(rest))
        rest = rest - (parts[-1].astype(np.uint32) << 16).view(np.float32)
    expert = np.arange(E, dtype=np.float32)
    consts = np.stack([E - expert, expert * CAP, expert * CAP + CAP - 1])
    ids = (np.arange(2)[None, :, None] * B * S + np.arange(NT)[None, None, :] * P + row[:, None, None])
    empty = np.zeros((1, ROW), np.float32)
    empty[0, D + 1] = DROPPED
    return {
        "c_ident": ident, "c_identb": bf16_bits(ident),
        "c_causal": bf16_bits(np.where(row[None, :] > row[:, None], MASKED, 0.0)),
        "c_before": bf16_bits(row[:, None] < row[None, :]),
        "c_expert": np.broadcast_to(consts[None, :, None, :], (P, 3, NT, E)).astype(np.float32).copy(),
        "c_row": ids.astype(np.float32), "c_empty": empty,
        "c_alibi": np.stack(parts), "c_ones": bf16_bits(np.ones((3, H, S))),
    }


def kernel(**inputs):
    import concourse.bacc as _bacc
    from concourse.bass_utils import run_bass_kernel_spmd as _run

    x = {k: np.asarray(v) for k, v in inputs.items()}
    tokens = x["x"].reshape(B * S, D)
    arrays = {
        "x": tokens, "x_t": tokens.T, "ctx_t": x["ctx_1024"].reshape(B * C, D).T,
        "w_qkv_t": x["L0_attn_W_qkv"].reshape(3, D, D).transpose(2, 0, 1),
        "w_o_t": x["L0_attn_W_o"].T,
        "wx_t": np.stack([x[f"L0_xattn_W{n}"].T for n in "qkvo"], axis=1),
        "b_col": np.stack([x["L0_xattn_bq"], x["L0_xattn_bk"]], axis=1),
        "bv": x["L0_xattn_bv"].reshape(1, D), "bo": x["L0_xattn_bo"].reshape(1, D),
        "w_gate": x["L0_ffn_Wg"],
        "w1": x["L0_ffn_W1"], "b1": x["L0_ffn_b1"].reshape(E, NC, P).transpose(2, 0, 1),
        "w2": x["L0_ffn_W2"].reshape(E, NC, P, D).transpose(0, 2, 1, 3).reshape(E, P, NC * D),
        "b2": x["L0_ffn_b2"].reshape(1, E, D),
    }
    arrays.update(_constants())
    arrays = {k: np.ascontiguousarray(v) for k, v in arrays.items()}
    nc = _bacc.Bacc("TRN2", target_bir_lowering=False, num_devices=1)
    aps = {k: nc.dram_tensor(f"in_{k}", v.shape, mybir.dt.from_np(v.dtype), kind="ExternalInput").ap() for k, v in arrays.items()}
    aps.update({k: ap.bitcast(BF16) for k, ap in aps.items() if arrays[k].dtype == np.uint16})
    out = nc.dram_tensor("out", (B * S, D), F32, kind="ExternalOutput").ap()
    decoder(nc, aps, out)
    r = _run(nc, [{f"in_{k}": v for k, v in arrays.items()}], core_ids=[0])
    return r.results[0]["out"].reshape(B, S, D)
```
